# Optimizing a Trainium2 kernel written in Bass

```python
import numpy as np
import jax
import jax.numpy as jnp

def _softmax(x, axis=-1):
    return jax.nn.softmax(x, axis=axis)

def _gelu(x):
    return jax.nn.gelu(x, approximate=True)

def _silu(x):
    return jax.nn.silu(x)

def _sigmoid(x):
    return jax.nn.sigmoid(x)

def _layernorm(x, axis=-1, eps=1e-05):
    m = jnp.mean(x, axis=axis, keepdims=True)
    v = jnp.var(x, axis=axis, keepdims=True)
    return (x - m) / jnp.sqrt(v + eps)

def _scatter_add(tgt, idx, src, axis=0):
    return tgt.at[idx].add(src)

def _segment_sum(src, seg, n):
    return jax.ops.segment_sum(src, seg, n)
kernel_name = 'mk_xattn_ffn_d1_seqx_r4_70326b'

def setup_inputs(seed: int=0):
    np.random.seed(seed)
    _w = jnp.asarray

    def _rec_inputs():
        import jax
        import jax.numpy as jnp
        _rk = jax.random.key(seed)
        x = 7.22e-05 + 1 * jax.random.normal(jax.random.fold_in(_rk, 1), (4, 1024, 256), jnp.float32)
        _lenS = 1024 - jax.random.randint(jax.random.fold_in(_rk, 7), (4,), 0, max(1, 1024 // 4) + 1, jnp.int32)
        _lenS2 = 77 - jax.random.randint(jax.random.fold_in(_rk, 8), (4,), 0, max(1, 77 // 4) + 1, jnp.int32)
        _ctx_1024P = jax.random.normal(jax.random.fold_in(_rk, 11), (4, 16, 256), jnp.float32)
        _ctx_1024c = jax.random.dirichlet(jax.random.fold_in(_rk, 511), 0.3 * jnp.ones((16,), jnp.float32), (4, 77))
        _ctx_1024t = jnp.einsum('bsk,bkd->bsd', _ctx_1024c, _ctx_1024P)
        _ctx_1024t = _ctx_1024t * jax.lax.rsqrt(jnp.mean(jnp.square(_ctx_1024t)) + 1e-12) * 0.953939
        ctx_1024 = -1.39393e-06 + 0.999914 * (_ctx_1024t + 0.3 * jax.random.normal(jax.random.fold_in(_rk, 611), (4, 77, 256), jnp.float32))
        fside_BxS_0 = jax.random.uniform(jax.random.fold_in(_rk, 13), (4, 1024), jnp.float32, 0.0, 0.999833)
        _validS = jnp.arange(1024)[None, :] < _lenS[:, None]
        _validS2 = jnp.arange(77)[None, :] < _lenS2[:, None]
        _causal = jnp.tril(jnp.ones((1024, 1024), dtype=bool))
        mask_BxS2_bk0 = jnp.logical_not(jnp.broadcast_to(_validS2[:, :], (4, 77)))
        return (x, ctx_1024, fside_BxS_0, mask_BxS2_bk0)
    x, ctx_1024, fside_BxS_0, mask_BxS2_bk0 = _rec_inputs()

    def _L0_xattn_setup():
        import jax, jax.numpy as jnp
        import numpy as np
        HEADS, DIM_HEAD = (8, 64)
        EXPERTS = 8
        CAP_FACTOR = 2.0
        THRESH = 0.2
        MIN_CAP = 4
        EPS = 1e-09

        def _ln(x, g):
            mu = jnp.mean(x, -1, keepdims=True)
            var = jnp.mean((x - mu) ** 2, -1, keepdims=True)
            return (x - mu) * jax.lax.rsqrt(var + 1e-05) * g

        def _cross_attn(text, img, mask, ln_gamma, null_kv, Wq, Wkv, Wo, out_gamma):
            b, n, d = text.shape
            h, dh = (HEADS, DIM_HEAD)
            x = _ln(text, ln_gamma)
            q = (x @ Wq).reshape(b, n, h, dh).transpose(0, 2, 1, 3)
            k, v = jnp.split(img @ Wkv, 2, axis=-1)
            k = k.reshape(b, -1, h, dh).transpose(0, 2, 1, 3)
            v = v.reshape(b, -1, h, dh).transpose(0, 2, 1, 3)
            nk = jnp.broadcast_to(null_kv[0], (b, h, 1, dh))
            nv = jnp.broadcast_to(null_kv[1], (b, h, 1, dh))
            k = jnp.concatenate([nk, k], axis=2)
            v = jnp.concatenate([nv, v], axis=2)
            sc = float(dh) ** (-0.25)
            sim = jnp.einsum('bhid,bhjd->bhij', q * sc, k * sc)
            m = jnp.pad(mask, ((0, 0), (1, 0)), constant_values=True)
            sim = jnp.where(m[:, None, None, :], sim, -jnp.finfo(sim.dtype).max)
            attn = jax.nn.softmax(sim, axis=-1)
            out = jnp.einsum('bhij,bhjd->bhid', attn, v)
            out = out.transpose(0, 2, 1, 3).reshape(b, n, h * dh)
            return _ln(out @ Wo, out_gamma)

        def _moe(x, probs, w_gate, w1, w2):
            b, n, d = x.shape
            e = EXPERTS
            cap = max(min(n, int(n * CAP_FACTOR / e)), MIN_CAP)
            f = x.dtype
            raw = jax.nn.softmax(x @ w_gate, axis=-1)
            idx1 = jnp.argmax(raw, -1)
            g1 = jnp.max(raw, -1)
            m1 = jax.nn.one_hot(idx1, e, dtype=f)
            raw2 = raw * (1.0 - m1)
            idx2 = jnp.argmax(raw2, -1)
            g2 = jnp.max(raw2, -1)
            m2 = jax.nn.one_hot(idx2, e, dtype=f)
            denom = g1 + g2 + EPS
            g1, g2 = (g1 / denom, g2 / denom)
            m2 = m2 * (probs < g2 / THRESH).astype(f)[..., None]
            pos1 = (jnp.cumsum(m1, axis=-2) - m1) * m1
            m1 = m1 * (pos1 < cap).astype(f)
            m1_count = jnp.sum(m1, -2, keepdims=True)
            m1_flat = jnp.sum(m1, -1)
            p1 = jnp.sum(pos1, -1)
            g1 = g1 * m1_flat
            pos2 = (jnp.cumsum(m2, axis=-2) - m2 + m1_count) * m2
            m2 = m2 * (pos2 < cap).astype(f)
            m2_flat = jnp.sum(m2, -1)
            p2 = jnp.sum(pos2, -1)
            g2 = g2 * m2_flat
            combine = (g1 * m1_flat)[..., None, None] * jax.nn.one_hot(idx1, e, dtype=f)[..., None] * jax.nn.one_hot(p1.astype(jnp.int32), cap, dtype=f)[..., None, :] + (g2 * m2_flat)[..., None, None] * jax.nn.one_hot(idx2, e, dtype=f)[..., None] * jax.nn.one_hot(p2.astype(jnp.int32), cap, dtype=f)[..., None, :]
            dispatch = (combine != 0).astype(f)
            ein = jnp.einsum('bnd,bnec->ebcd', x, dispatch)
            hidden = jax.nn.relu(jnp.einsum('ebcd,edh->ebch', ein, w1))
            eout = jnp.einsum('ebch,ehd->ebcd', hidden, w2)
            return jnp.einsum('bnec,ebcd->bnd', combine, eout)
        key = jax.random.key(seed)
        ks = jax.random.split(key, 11)
        b, nt, ni, d = (4, 512, 256, 256)
        h, dh, e = (HEADS, DIM_HEAD, EXPERTS)
        inner, hd = (h * dh, 4 * d)
        s = 0.02
        return {'text': jax.random.normal(ks[0], (b, nt, d), jnp.float32), 'img': jax.random.normal(ks[1], (b, ni, d), jnp.float32), 'mask': jax.random.randint(ks[2], (b, ni), 0, 2).astype(bool), 'probs': jax.random.uniform(ks[3], (b, nt), jnp.float32), 'ln_gamma': jnp.ones((d,), jnp.float32), 'null_kv': jax.random.normal(ks[4], (2, dh), jnp.float32), 'Wq': jax.random.normal(ks[5], (d, inner), jnp.float32) * s, 'Wkv': jax.random.normal(ks[6], (d, 2 * inner), jnp.float32) * s, 'Wo': jax.random.normal(ks[7], (inner, d), jnp.float32) * s, 'out_gamma': jnp.ones((d,), jnp.float32), 'w_gate': jax.random.normal(ks[8], (d, e), jnp.float32) * s, 'w1': jax.random.normal(ks[9], (e, d, hd), jnp.float32) * s, 'w2': jax.random.normal(ks[10], (e, hd, d), jnp.float32) * s}
    _L0_xattn_all = _L0_xattn_setup()
    _L0_xattn_in = {k: v for k, v in _L0_xattn_all.items() if k in ('ln_gamma', 'null_kv', 'Wq', 'Wkv', 'Wo', 'out_gamma', 'w_gate', 'w1', 'w2')}
    del _L0_xattn_all

    def _L0_ffn_setup():
        import jax, jax.numpy as jnp
        import numpy as np
        TOP_K = 2
        key = jax.random.key(seed)
        ks = jax.random.split(key, 6)
        B, S, H, F, E = (4, 512, 256, 1024, 8)
        x = jax.random.normal(ks[0], (B, S, H), dtype=jnp.float32)
        gate_w = jax.random.normal(ks[1], (E, H), dtype=jnp.float32) * 0.02
        W1 = jax.random.normal(ks[2], (E, H, F), dtype=jnp.float32) * (1.0 / np.sqrt(H))
        b1 = jnp.zeros((E, F), dtype=jnp.float32)
        W2 = jax.random.normal(ks[3], (E, F, H), dtype=jnp.float32) * (1.0 / np.sqrt(F))
        b2 = jnp.zeros((E, H), dtype=jnp.float32)
        sW1 = jax.random.normal(ks[4], (H, F), dtype=jnp.float32) * (1.0 / np.sqrt(H))
        sb1 = jnp.zeros((F,), dtype=jnp.float32)
        sW2 = jax.random.normal(ks[5], (F, H), dtype=jnp.float32) * (1.0 / np.sqrt(F))
        sb2 = jnp.zeros((H,), dtype=jnp.float32)
        return {'x': x, 'gate_w': gate_w, 'W1': W1, 'b1': b1, 'W2': W2, 'b2': b2, 'sW1': sW1, 'sb1': sb1, 'sW2': sW2, 'sb2': sb2}
    _L0_ffn_all = _L0_ffn_setup()
    _L0_ffn_in = {k: v for k, v in _L0_ffn_all.items() if k in ('gate_w', 'W1', 'b1', 'W2', 'b2', 'sW1', 'sb1', 'sW2', 'sb2')}
    del _L0_ffn_all
    return {'x': x, 'ctx_1024': ctx_1024, 'fside_BxS_0': fside_BxS_0, 'mask_BxS2_bk0': mask_BxS2_bk0, 'L0_xattn_ln_gamma': _L0_xattn_in['ln_gamma'], 'L0_xattn_null_kv': _L0_xattn_in['null_kv'], 'L0_xattn_Wq': _L0_xattn_in['Wq'], 'L0_xattn_Wkv': _L0_xattn_in['Wkv'], 'L0_xattn_Wo': _L0_xattn_in['Wo'], 'L0_xattn_out_gamma': _L0_xattn_in['out_gamma'], 'L0_xattn_w_gate': _L0_xattn_in['w_gate'], 'L0_xattn_w1': _L0_xattn_in['w1'], 'L0_xattn_w2': _L0_xattn_in['w2'], 'L0_ffn_gate_w': _L0_ffn_in['gate_w'], 'L0_ffn_W1': _L0_ffn_in['W1'], 'L0_ffn_b1': _L0_ffn_in['b1'], 'L0_ffn_W2': _L0_ffn_in['W2'], 'L0_ffn_b2': _L0_ffn_in['b2'], 'L0_ffn_sW1': _L0_ffn_in['sW1'], 'L0_ffn_sb1': _L0_ffn_in['sb1'], 'L0_ffn_sW2': _L0_ffn_in['sW2'], 'L0_ffn_sb2': _L0_ffn_in['sb2']}

def reference(x, ctx_1024, fside_BxS_0, mask_BxS2_bk0, L0_xattn_ln_gamma, L0_xattn_null_kv, L0_xattn_Wq, L0_xattn_Wkv, L0_xattn_Wo, L0_xattn_out_gamma, L0_xattn_w_gate, L0_xattn_w1, L0_xattn_w2, L0_ffn_gate_w, L0_ffn_W1, L0_ffn_b1, L0_ffn_W2, L0_ffn_b2, L0_ffn_sW1, L0_ffn_sb1, L0_ffn_sW2, L0_ffn_sb2):
    import jax
    import jax.numpy as jnp

    def _L0_xattn_ref(text, img, mask, probs, ln_gamma, null_kv, Wq, Wkv, Wo, out_gamma, w_gate, w1, w2):
        import jax, jax.numpy as jnp
        import numpy as np
        HEADS, DIM_HEAD = (8, 64)
        EXPERTS = 8
        CAP_FACTOR = 2.0
        THRESH = 0.2
        MIN_CAP = 4
        EPS = 1e-09

        def _ln(x, g):
            mu = jnp.mean(x, -1, keepdims=True)
            var = jnp.mean((x - mu) ** 2, -1, keepdims=True)
            return (x - mu) * jax.lax.rsqrt(var + 1e-05) * g

        def _cross_attn(text, img, mask, ln_gamma, null_kv, Wq, Wkv, Wo, out_gamma):
            b, n, d = text.shape
            h, dh = (HEADS, DIM_HEAD)
            x = _ln(text, ln_gamma)
            q = (x @ Wq).reshape(b, n, h, dh).transpose(0, 2, 1, 3)
            k, v = jnp.split(img @ Wkv, 2, axis=-1)
            k = k.reshape(b, -1, h, dh).transpose(0, 2, 1, 3)
            v = v.reshape(b, -1, h, dh).transpose(0, 2, 1, 3)
            nk = jnp.broadcast_to(null_kv[0], (b, h, 1, dh))
            nv = jnp.broadcast_to(null_kv[1], (b, h, 1, dh))
            k = jnp.concatenate([nk, k], axis=2)
            v = jnp.concatenate([nv, v], axis=2)
            sc = float(dh) ** (-0.25)
            sim = jnp.einsum('bhid,bhjd->bhij', q * sc, k * sc)
            m = jnp.pad(mask, ((0, 0), (1, 0)), constant_values=True)
            sim = jnp.where(m[:, None, None, :], sim, -jnp.finfo(sim.dtype).max)
            attn = jax.nn.softmax(sim, axis=-1)
            out = jnp.einsum('bhij,bhjd->bhid', attn, v)
            out = out.transpose(0, 2, 1, 3).reshape(b, n, h * dh)
            return _ln(out @ Wo, out_gamma)

        def _moe(x, probs, w_gate, w1, w2):
            b, n, d = x.shape
            e = EXPERTS
            cap = max(min(n, int(n * CAP_FACTOR / e)), MIN_CAP)
            f = x.dtype
            raw = jax.nn.softmax(x @ w_gate, axis=-1)
            idx1 = jnp.argmax(raw, -1)
            g1 = jnp.max(raw, -1)
            m1 = jax.nn.one_hot(idx1, e, dtype=f)
            raw2 = raw * (1.0 - m1)
            idx2 = jnp.argmax(raw2, -1)
            g2 = jnp.max(raw2, -1)
            m2 = jax.nn.one_hot(idx2, e, dtype=f)
            denom = g1 + g2 + EPS
            g1, g2 = (g1 / denom, g2 / denom)
            m2 = m2 * (probs < g2 / THRESH).astype(f)[..., None]
            pos1 = (jnp.cumsum(m1, axis=-2) - m1) * m1
            m1 = m1 * (pos1 < cap).astype(f)
            m1_count = jnp.sum(m1, -2, keepdims=True)
            m1_flat = jnp.sum(m1, -1)
            p1 = jnp.sum(pos1, -1)
            g1 = g1 * m1_flat
            pos2 = (jnp.cumsum(m2, axis=-2) - m2 + m1_count) * m2
            m2 = m2 * (pos2 < cap).astype(f)
            m2_flat = jnp.sum(m2, -1)
            p2 = jnp.sum(pos2, -1)
            g2 = g2 * m2_flat
            combine = (g1 * m1_flat)[..., None, None] * jax.nn.one_hot(idx1, e, dtype=f)[..., None] * jax.nn.one_hot(p1.astype(jnp.int32), cap, dtype=f)[..., None, :] + (g2 * m2_flat)[..., None, None] * jax.nn.one_hot(idx2, e, dtype=f)[..., None] * jax.nn.one_hot(p2.astype(jnp.int32), cap, dtype=f)[..., None, :]
            dispatch = (combine != 0).astype(f)
            ein = jnp.einsum('bnd,bnec->ebcd', x, dispatch)
            hidden = jax.nn.relu(jnp.einsum('ebcd,edh->ebch', ein, w1))
            eout = jnp.einsum('ebch,ehd->ebcd', hidden, w2)
            return jnp.einsum('bnec,ebcd->bnd', combine, eout)
        attended = _cross_attn(text, img, mask, ln_gamma, null_kv, Wq, Wkv, Wo, out_gamma)
        activated = jnp.tanh(attended) + text
        moe_out = _moe(activated, probs, w_gate, w1, w2)
        return jnp.tanh(moe_out + activated)

    def _L0_ffn_ref(x, gate_w, W1, b1, W2, b2, sW1, sb1, sW2, sb2):
        import jax, jax.numpy as jnp
        import numpy as np
        TOP_K = 2
        B, S, H = x.shape
        E = gate_w.shape[0]
        x_flat = x.reshape(-1, H)
        logits = x_flat @ gate_w.T
        probs = jax.nn.softmax(logits.astype(jnp.float32), axis=-1)
        top_w, sel = jax.lax.top_k(probs, TOP_K)
        top_w = top_w / jnp.sum(top_w, axis=-1, keepdims=True)
        combine = jnp.sum(jax.nn.one_hot(sel, E, dtype=top_w.dtype) * top_w[..., None], axis=1)
        combine = combine.astype(x.dtype)
        h = jax.nn.gelu(jnp.einsum('th,ehf->tef', x_flat, W1) + b1[None], approximate=False)
        y = jnp.einsum('tef,efh->teh', h, W2) + b2[None]
        out = jnp.einsum('teh,te->th', y, combine)
        sh = jax.nn.gelu(x_flat @ sW1 + sb1, approximate=False)
        out = out + sh @ sW2 + sb2
        return out.reshape(B, S, H)
    x = x + _L0_xattn_ref(_layernorm(x, axis=-1), ctx_1024, mask_BxS2_bk0, fside_BxS_0, L0_xattn_ln_gamma, L0_xattn_null_kv, L0_xattn_Wq, L0_xattn_Wkv, L0_xattn_Wo, L0_xattn_out_gamma, L0_xattn_w_gate, L0_xattn_w1, L0_xattn_w2)
    x = x + _L0_ffn_ref(_layernorm(x, axis=-1), L0_ffn_gate_w, L0_ffn_W1, L0_ffn_b1, L0_ffn_W2, L0_ffn_b2, L0_ffn_sW1, L0_ffn_sb1, L0_ffn_sW2, L0_ffn_sb2)
    return x

_drawn_inputs = setup_inputs


def setup_inputs(seed=0):
    import zlib

    import numpy as np

    out = dict(_drawn_inputs(seed))
    spreads = {'L0_xattn_ln_gamma': (1.0, 0.565),
     'L0_xattn_out_gamma': (1.0, 0.2),
     'L0_ffn_b1': (0.0, 0.289),
     'L0_ffn_b2': (0.0, 0.1),
     'L0_ffn_sb1': (0.0, 0.1),
     'L0_ffn_sb2': (0.0, 0.1)}
    factors = {}
    for name, (base, spread) in spreads.items():
        noise = np.random.default_rng([zlib.crc32(name.encode()), seed]).standard_normal(out[name].shape)
        drawn = base * np.exp(spread * noise) if base else spread * noise
        out[name] = jnp.asarray(drawn.astype(out[name].dtype))
    for name, factor in factors.items():
        out[name] = (out[name] * factor).astype(out[name].dtype)
    return out
```

```python
from contextlib import ExitStack

import concourse.bass as bass
from concourse import mybir

F32 = mybir.dt.float32
I32 = mybir.dt.int32
U8 = mybir.dt.uint8
ALU = mybir.AluOpType
ACT = mybir.ActivationFunctionType
AX = mybir.AxisListType
ds = bass.ds

P = 128
B, N, D = 4, 1024, 256
KC = D // P
NCTX = 77
NK = NCTX + 1
H, DH = 8, 64
NQ = H * DH // P
SK = H * NK
PK = 640
PC = PK // P
E = 8
F = 1024
FC = F // P
CAP = 2 * N // E
THRESH = 0.2
T = B * N
NT = T // P
NP_ = NT // 2
TPB = N // P
R = 2 * P
RW = 272
CID = D + E
S1 = E * B * CAP
G1 = S1 // R
GS = T // R
G2 = (2 * T + E * (R - 1)) // R
S2 = G2 * R
SPARE = 2 * P
S1ROWS = S1 + 2 * T
EPS = 1e-5
FMAX = 3.4028234663852886e38
RSQRT_SEED = 1597463007.0


def build(nc, io):
    with ExitStack() as ctx:
        def sb(name, shape, dt=F32):
            return ctx.enter_context(nc.sbuf_tensor(name, shape, dt))

        def sem(name):
            return ctx.enter_context(nc.semaphore(name))

        bank = [ctx.enter_context(nc.psum_tensor(f"bank{i}", [P, 512], F32)) for i in range(8)]

        xs1 = nc.dram_tensor("xs1", [S1ROWS, RW], F32).ap()
        xs2 = nc.dram_tensor("xs2", [S2, RW], F32).ap()
        xn2 = nc.dram_tensor("xn2", [T, D], F32).ap()
        acc1 = nc.dram_tensor("acc1", [T + SPARE, D], F32).ap()
        out = io["out"]

        X = sb("X", [P, NT, D])
        AR = sb("AR", [P, NT, RW])
        ident = sb("ident", [P, P])
        upper = sb("upper", [P, P])
        ones = sb("ones", [P, P])
        iota_e8 = sb("iota_e8", [P, E])
        first_slot = sb("first_slot", [P, B, E])
        spare_row = sb("spare_row", [P, 2, NT])
        iota_256k = sb("iota_256k", [P, NT // 2])
        iota_t = sb("iota_t", [P, G2])
        iota_e = sb("iota_e", [P, E])
        seg1 = sb("seg1", [P, 2 * E * NT])
        fill = sb("fill", [P, 2, RW])
        nullc = sb("nullc", [P, 2])
        gcol = sb("gcol", [P, KC])
        ogam = sb("ogam", [P, D])
        sb2 = sb("sb2", [P, D])
        mask8 = sb("mask8", [P, B * NCTX], U8)
        maskb = sb("maskb", [P, B, NK])
        sb1 = sb("sb1", [P, FC])
        prob = sb("prob", [P, NT])
        wg1 = sb("wg1", [P, KC, E])
        wg2 = sb("wg2", [P, KC, E])

        area = sb("area", [P, 12288])
        KB = area[:, 0:2496].rearrange("p (b q c) -> p b q c", b=B, q=NQ)
        VB = area[:, 2496:6592].rearrange("p (b q c) -> p b q c", b=B, q=NQ)
        MQ = area[:, 6592:11584].rearrange("p (b k c) -> p b k c", b=B, k=KC)
        w1b = [area[:, 4096 * i:4096 * i + 2048].rearrange("p (k f) -> p k f", k=KC) for i in range(2)]
        w2b = [area[:, 4096 * i + 2048:4096 * i + 4096].rearrange("p (c d) -> p c d", c=FC) for i in range(2)]
        area2 = sb("area2", [P, 5120])
        VW = area2[:, :].rearrange("p (b c d) -> p b c d", b=B, c=PC)
        hT = [area2[:, 2048 * i:2048 * i + 2048].rearrange("p (c r) -> p c r", c=FC) for i in range(2)]
        xT = [area2[:, 4096 + 512 * i:4608 + 512 * i].rearrange("p (k r) -> p k r", k=KC) for i in range(2)]
        area3 = sb("area3", [P, 4712])
        wkv = area3[:, 0:2048].rearrange("p (k n) -> p k n", k=KC)
        wqT = area3[:, 2048:3072].rearrange("p (q n) -> p q n", q=NQ)
        wo = area3[:, 3072:4096].rearrange("p (q n) -> p q n", q=NQ)
        ctxT = area3[:, 4096:4712].rearrange("p (k n) -> p k n", k=KC)
        score = [[area3[:, PK * (2 * i + u):PK * (2 * i + u + 1)] for u in range(2)] for i in range(2)]
        pT = [area3[:, PK * (4 + u):PK * (5 + u)].rearrange("p (c n) -> p c n", c=PC) for u in range(2)]
        b1b = [sb(f"b1b{i}", [P, FC]) for i in range(2)]
        b2b = [sb(f"b2b{i}", [P, D]) for i in range(2)]

        text = [sb(f"text{i}", [P, 2, D]) for i in range(2)]
        tT = sb("tT", [P, 2, KC, P])
        z = sb("z", [P, 2, D])
        act_a = [sb(f"act_a{i}", [P, 2, D]) for i in range(2)]
        aT = sb("aT", [P, 2, KC, P])
        smax = [sb(f"smax{u}", [P, H]) for u in range(2)]
        ssum = [sb(f"ssum{u}", [P, H]) for u in range(2)]
        srec = [sb(f"srec{u}", [P, H]) for u in range(2)]
        st6 = sb("st6", [P, 4, 6])
        mv_in = sb("mv_in", [P, 2, 2])
        mv_out = sb("mv_out", [P, 2, 2])
        var = sb("var", [P, 6])
        rstd = sb("rstd", [P, 6])
        nwt = sb("nwt", [P, 6])
        rsc = sb("rsc", [P, 2])
        LG = sb("LG", [P, NT, E])

        RA = sb("RA", [P, NT, E])
        RB = sb("RB", [P, NT, E])
        RT = sb("RT", [P, NT, E])
        OH = sb("OH", [P, 2, NT, E])
        TO = sb("TO", [P, 2, E, NT])
        SCN = sb("SCN", [P, 2, E, NT])
        POS = sb("POS", [P, 2, NT, E])
        v32 = sb("v32", [P, 16, NT])
        m1c = sb("m1c", [P, B, E])
        slot = [sb(f"slot{k}", [P, NT], I32) for k in range(2)]
        cmp = sb("cmp", [P, E, NT // 2])
        e8 = sb("e8", [P, 5, E])
        OHT = sb("OHT", [P, G2, E])
        oht2 = sb("oht2", [P, G2, E])
        eidf = sb("eidf", [P, G2])
        eid = sb("eid", [P, G2], I32)

        cell_v = sb("cell_v", [P, 2])

        xr = [sb(f"xr{i}", [P, 2, D]) for i in range(2)]
        meta = [sb(f"meta{i}", [P, 2, E + 1]) for i in range(2)]
        y = [sb(f"y{i}", [P, 2, D]) for i in range(2)]
        yb = sb("yb", [P, 2, D])
        wsel = sb("wsel", [P, 2, E])
        wv = sb("wv", [P, 2])

        x_in, par_in, filled, consts, kb_zero = sem("x_in"), sem("par_in"), sem("filled"), sem("consts"), sem("kb_zero")
        kv_ps, k_ev, v_ev, m_ps, m_ev, vw_ps, vw_ev, maskb_ready = (sem(n) for n in (
            "kv_ps", "k_ev", "v_ev", "m_ps", "m_ev", "vw_ps", "vw_ev", "maskb_ready"))
        (text_ready, textT_ps, textT_ready, att_ps, z_ready, rstd_ready, tanh_ready, a_ready, text_kept, a_kept,
         aT_ps, aT_ready, gate_ps, gate_ready, acc_init) = (sem(n) for n in (
             "text_ready", "textT_ps", "textT_ready", "att_ps", "z_ready", "rstd_ready", "tanh_ready", "a_ready",
             "text_kept", "a_kept", "aT_ps", "aT_ready", "gate_ps", "gate_ready", "acc_init"))
        (score_ps, score_ready, max_ready, sub_ready, exp_ready, rec_ready, prob_ready, probT_ps,
         probT_ready) = (sem(n) for n in (
             "score_ps", "score_ready", "max_ready", "sub_ready", "exp_ready", "rec_ready", "prob_ready",
             "probT_ps", "probT_ready"))
        dve_self = sem("dve_self")
        rt_sub, rt_exp, rt_hot, rt_pos, rt_done = (sem(n) for n in ("rt_sub", "rt_exp", "rt_hot", "rt_pos", "rt_done"))
        rows_out, rows_out2 = sem("rows_out"), sem("rows_out2")
        x_rows = [sem(f"x_rows{i}") for i in range(2)]
        meta_in = [sem(f"meta_in{i}") for i in range(2)]
        w1_in = [sem(f"w1_in{i}") for i in range(2)]
        w2_in = [sem(f"w2_in{i}") for i in range(2)]
        shared_out = [sem(f"shared_out{i}") for i in range(2)]
        xT_ps, xT_ready, h_ps, h_ready, y_ps, y_ready, added1, added2 = (sem(n) for n in (
            "xT_ps", "xT_ready", "h_ps", "h_ready", "y_ps", "y_ready", "added1", "added2"))
        acc_in = [sem(f"acc_in{i}") for i in range(2)]
        xn_out = [sem(f"xn_out{i}") for i in range(2)]
        c_tanh, c_norm, c_kept, c_bias, c_x, cT_ps, cT_ready, cg_ps, cg_ready = (sem(n) for n in (
            "c_tanh", "c_norm", "c_kept", "c_bias", "c_x", "cT_ps", "cT_ready", "cg_ps", "cg_ready"))

        NPAR = 14
        NCONST = 12
        M2 = G1 + GS
        block = ctx.enter_context(nc.Block())

        def rows(dram, g, width=D):
            return dram[ds(g * R, R), 0:width].rearrange("(h p) d -> p h d", p=P)

        def run_steps(eng, step, lo, first, last, hi, chain=None, per=0):
            for s in range(lo, first):
                step(s, s % 2)
            with eng.Fori(first // 2, last // 2) as i:
                if chain:
                    chain.enter((i - first // 2) * per)
                step(2 * i, 0)
                step(2 * i + 1, 1)
                if chain:
                    chain.leave((last - first) // 2, per)
            for s in range(last, hi):
                step(s, s % 2)

        def wait_apart(eng, cell, own, n):
            eng.wait_ge(own, n)
            eng.tensor_tensor(cell[:, 1:2], cell[:, 0:1], cell[:, 0:1], ALU.add)

        class Chain:

            def __init__(self, eng, own):
                self.eng, self.own, self.n, self.base = eng, own, 0, 0

            def link(self, ins, scratch=None):
                ins.then_inc(self.own, 1)
                self.n += 1
                if scratch:
                    wait_apart(self.eng, scratch, self.own, self.base + self.n)
                else:
                    self.eng.wait_ge(self.own, self.base + self.n)

            def enter(self, base):
                self.base, self.at = base, self.n

            def leave(self, turns, per):
                assert self.n - self.at == per, (self.n - self.at, per)
                self.n, self.base = self.at + turns * per, 0

        def known(s, least):
            return not isinstance(s, int) or s >= least

        def below(s, end):
            return not isinstance(s, int) or s < end

        @block.sync
        def _(sp):
            def par(dst, src):
                sp.dma_start(dst, src).then_inc(par_in, 16)

            par(ctxT, io["ctxT"].rearrange("(k p) n -> p k n", p=P))
            par(wkv, io["Wkv"].rearrange("(k p) n -> p k n", p=P))
            par(nullc[0:DH, :], io["null"])
            par(nullc[DH:P, :], io["null"])
            par(wqT, io["WqT"].rearrange("(q p) n -> p q n", p=P))
            par(wo, io["Wo"].rearrange("(q p) n -> p q n", p=P))
            par(gcol[:], io["ln_g"])
            par(mask8[:], io["mask"].partition_broadcast(P))
            for b in range(B):
                sp.dma_start(X[:, b * TPB:(b + 1) * TPB, :],
                             io["x"][b * N:(b + 1) * N, :].rearrange("(t p) d -> p t d", p=P)).then_inc(x_in, 16)
            par(ogam[:], io["out_g"].partition_broadcast(P))
            par(sb2[:], io["sb2"].partition_broadcast(P))
            par(prob[:], io["probs"])
            par(wg1[:], io["wg1"].rearrange("(k p) n -> p k n", p=P))
            par(wg2[:], io["wg2"].rearrange("(k p) n -> p k n", p=P))
            par(sb1[:], io["sb1"])

            def init_step(s, _):
                sp.wait_ge(a_kept, s + 1)
                sp.dma_start(rows(acc1, s), AR[:, ds(2 * s, 2), 0:D]).then_inc(acc_init, 16)
            run_steps(sp, init_step, 0, 0, NP_, NP_)

            def w1_load(e, name, wb):
                sp.dma_start(w1b[wb], io[name][ds(e, 1), :, :].rearrange("o p (k f) -> p (o k) f", k=KC)).then_inc(w1_in[wb], 16)

            def w2_load(e, name, wb):
                sp.dma_start(w2b[wb], io[name][ds(e, 1), :, :].rearrange("o p (c d) -> p (o c) d", c=FC)).then_inc(w2_in[wb], 16)

            sp.wait_ge(att_ps, NP_)
            for e in range(2):
                w1_load(e, "W1a", e)
                w2_load(e, "W2a", e)
            sp.wait_ge(rows_out, 16 * 2 * NT)

            def x_load(g, par, src):
                if known(g, 2):
                    sp.wait_ge(xT_ps, g - 1)
                sp.dma_start(xr[par][:], src).then_inc(x_rows[par], 16)

            for g in range(8):
                x_load(g, g % 2, rows(xs1, g))
            with sp.Fori(1, E // 2) as i:
                for h in range(2):
                    sp.wait_ge(h_ps, 4 * (8 * i - 4 + 4 * h))
                    w1_load(2 * i + h, "W1a", h)
                    sp.wait_ge(y_ps, 8 * i - 4 + 4 * h)
                    w2_load(2 * i + h, "W2a", h)
                    for k in range(4):
                        x_load(8 * i + 4 * h + k, k % 2, rows(xs1, 8 * i + 4 * h + k))
            sp.wait_ge(h_ps, 4 * (G1 - 4))
            w1_load(0, "sW1", 0)
            sp.wait_ge(y_ps, G1 - 4)
            w2_load(0, "sW2", 0)

            sp.wait_ge(added1, 32 * G1)

            def acc_step(s, par):
                if below(s, NP_):
                    if known(s, 2):
                        sp.wait_ge(c_x, s - 1)
                    sp.dma_start(y[par][:], rows(acc1, s)).then_inc(acc_in[par], 16)
                if known(s, 1):
                    sp.wait_ge(c_norm, s)
                    sp.dma_start(rows(xn2, s - 1), text[1 - par][:]).then_inc(xn_out[1 - par], 16)
            run_steps(sp, acc_step, 0, 2, NP_, NP_ + 1)
            for i in range(2):
                sp.wait_ge(xn_out[i], 16 * NP_ // 2)

            for t in range(2):
                x_load(G1 + t, t, rows(xn2, t))

            def shared_store(t, par):
                sp.wait_ge(y_ready, G1 + t + 1)
                sp.dma_start(rows(out, t), y[par][:]).then_inc(shared_out[par], 16)

            def shared_step(t, par):
                x_load(G1 + t + 2, par, rows(xn2, t + 2))
                shared_store(t, par)
            run_steps(sp, shared_step, 0, 0, GS - 2, GS - 2)

            sp.wait_ge(rt_done, 2)
            sp.wait_ge(rows_out2, 16 * 2 * NT)

            def routed_w(t, wb):
                e = sp.value_load(eid[0:1, ds(t, 1)], min_val=0, max_val=E - 1)
                last = G1 if not known(t, 1) else M2 + t - 1
                sp.wait_ge(h_ps, 4 * last)
                w1_load(e, "W1b", wb)
                sp.wait_ge(h_ready, 4 * last)
                sp.dma_start(b1b[wb][:], io["b1"][ds(e, 1), :, :].rearrange("o p c -> p (o c)")).then_inc(w1_in[wb], 16)
                sp.wait_ge(y_ps, last)
                w2_load(e, "W2b", wb)
                sp.wait_ge(y_ready, last)
                sp.dma_start(b2b[wb][:], io["b2"][ds(e, 1), :].broadcast_to([P, D])).then_inc(w2_in[wb], 16)

            routed_w(0, 1)
            for t in (GS - 2, GS - 1):
                x_load(G1 + t + 2, t % 2, rows(xs2, t + 2 - GS))
                shared_store(t, t % 2)

            def routed_step(t, par):
                x_load(M2 + t + 2, par, rows(xs2, t + 2))
                routed_w(t + 1, par)
            last = G2 - 2 - G2 % 2
            run_steps(sp, routed_step, 0, 2, last, G2 - 2)
            routed_w(G2 - 1, (G2 - 2) % 2)
            sp.wait_ge(added2, 32 * G2)
            for i in range(2):
                sp.wait_ge(shared_out[i], 16 * GS // 2)
            sp.wait_ge(filled, 16 * 6)
            sp.wait_ge(acc_init, 16 * NP_)

        @block.tensor
        def _(pe):
            mm = nc.tensor.matmul
            pe.wait_ge(par_in, 16 * NPAR)
            for kv in range(2):
                for q in range(NQ):
                    for k in range(KC):
                        last = mm(bank[4 * kv + q][:, 0:B * NCTX],
                                  wkv[:, k, kv * H * DH + q * P:kv * H * DH + (q + 1) * P], ctxT[:, k, :],
                                  start=(k == 0), stop=(k == KC - 1))
            last.then_inc(kv_ps, 1)
            pe.wait_ge(k_ev, 1)
            for b in range(B):
                for k in range(KC):
                    n = b * KC + k
                    if n >= 2:
                        pe.wait_ge(m_ev, n - 1)
                    for q in range(NQ):
                        last = mm(bank[2 * (n % 2) + q // 2][:, (q % 2) * 2 * NK:(q % 2 + 1) * 2 * NK],
                                  wqT[:, q, k * P:(k + 1) * P], KB[:, b, q, :], start=True, stop=True)
                    last.then_inc(m_ps, 1)
            pe.wait_ge(v_ev, 1)
            for b in range(B):
                for c2 in range(3):
                    n = b * 3 + c2
                    if n >= 4:
                        pe.wait_ge(vw_ev, n - 3)
                    for c in range(2 * c2, min(2 * c2 + 2, PC)):
                        parts = [(q, v) for q, v in ((c - 1, 1), (c, 0)) if 0 <= q < NQ]
                        for m, (q, v) in enumerate(parts):
                            last = mm(bank[4 + n % 4][:, (c % 2) * D:(c % 2 + 1) * D], VB[:, b, q, v * P:(v + 1) * P],
                                      wo[:, q, :], start=(m == 0), stop=(m == len(parts) - 1))
                    last.then_inc(vw_ps, 1)
            pe.wait_ge(m_ev, B * KC)
            pe.wait_ge(vw_ev, B * 3)
            pe.wait_ge(consts, NCONST)

            def transposes(dst, src, done):
                for u in range(2):
                    for k in range(KC):
                        last = nc.tensor.transpose(dst[:, (u * KC + k) * P:(u * KC + k + 1) * P],
                                                   src[:, u, k * P:(k + 1) * P], ident[:])
                last.then_inc(done, 1)

            def att_step(s, par):
                A, Bs, C = below(s, NP_), known(s, 1) and below(s, NP_ + 1), known(s, 2)

                def scores(u):
                    if u == 0:
                        pe.wait_ge(textT_ready, s + 1)
                    if known(s, 1) or u:
                        pe.wait_ge(score_ready, 2 * s + u)
                    for half in range(2):
                        for k in range(KC):
                            last = mm(bank[1 + half][:, 0:SK // 2], tT[:, u, k, :],
                                      MQ[:, ds(s // 4, 1), k, half * SK // 2:(half + 1) * SK // 2].rearrange("p b c -> p (b c)"),
                                      start=(k == 0), stop=(k == KC - 1))
                    last.then_inc(score_ps, 1)

                def prob_t(u):
                    pe.wait_ge(prob_ready, 2 * (s - 1) + u + 1)
                    for c in range(PC):
                        last = nc.tensor.transpose(bank[3 + c // 4][:, (c % 4) * P:(c % 4 + 1) * P],
                                                   score[1 - par][u][:, c * P:(c + 1) * P], ident[:])
                    last.then_inc(probT_ps, 1)

                def attend(u):
                    pe.wait_ge(probT_ready, 2 * (s - 1) + u + 1)
                    if u == 0 and known(s, 2):
                        pe.wait_ge(z_ready, s - 1)
                    for c in range(PC):
                        last = mm(bank[5][:, u * D:(u + 1) * D], pT[u][:, c, :],
                                  VW[:, ds((s - 1) // 4, 1), c, :].rearrange("p b d -> p (b d)"),
                                  start=(c == 0), stop=(c == PC - 1))
                    if u:
                        last.then_inc(att_ps, 1)

                if A:
                    pe.wait_ge(text_ready, s + 1)
                    transposes(bank[0], text[par], textT_ps)
                    scores(0)
                if Bs:
                    prob_t(0)
                if C:
                    pe.wait_ge(a_ready, s - 1)
                    transposes(bank[6], act_a[par], aT_ps)
                    pe.wait_ge(aT_ready, s - 1)
                    if known(s, 3):
                        pe.wait_ge(gate_ready, s - 2)
                    for u in range(2):
                        for k in range(KC):
                            last = mm(bank[7][:, u * E:(u + 1) * E], aT[:, u, k, :], wg1[:, k, :],
                                      start=(k == 0), stop=(k == KC - 1))
                    last.then_inc(gate_ps, 1)
                if Bs:
                    attend(0)
                    prob_t(1)
                if A:
                    scores(1)
                if Bs:
                    attend(1)
            run_steps(pe, att_step, 0, 4, 14, NP_ + 2)

            def count_slots(n, w, banks):
                pe.wait_ge(rt_hot, n)
                mm(banks[0], upper[:], OH[:, 0:w, :, :].rearrange("p k j e -> p (k j e)"), start=True, stop=True)
                mm(banks[1], ones[:], OH[:, 0:w, :, :].rearrange("p k j e -> p (k j e)"), start=True,
                   stop=True).then_inc(rt_pos, 1)

            count_slots(1, 2, (bank[5][:], bank[6][:]))

            def x_turn(g, par):
                pe.wait_ge(x_rows[par], 16 * (g // 2 + 1))
                if known(g, 1):
                    pe.wait_ge(xT_ready, g)
                for k in range(KC):
                    for u in range(2):
                        last = nc.tensor.transpose(bank[0][:, k * R + u * P:k * R + (u + 1) * P],
                                                   xr[par][:, u, k * P:(k + 1) * P], ident[:])
                last.then_inc(xT_ps, 1)

            def first_product(g, par, wb, arrived):
                pe.wait_ge(xT_ready, g + 1)
                if arrived is not None:
                    pe.wait_ge(w1_in[wb], arrived)
                for j in range(FC // 2):
                    if known(g, 1):
                        pe.wait_ge(h_ready, 4 * (g - 1) + j + 1)
                    for c in (2 * j, 2 * j + 1):
                        for k in range(KC):
                            last = mm(bank[1 + j][:, (c % 2) * R:(c % 2 + 1) * R], w1b[wb][:, k, c * P:(c + 1) * P],
                                      xT[par][:, k, :], start=(k == 0), stop=(k == KC - 1))
                    last.then_inc(h_ps, 1)

            def second_product(g, par, wb, arrived):
                pe.wait_ge(h_ready, 4 * g + 4)
                if arrived is not None:
                    pe.wait_ge(w2_in[wb], arrived)
                if known(g, 2):
                    pe.wait_ge(y_ready, g - 1)
                for u in range(2):
                    for c in range(FC):
                        last = mm(bank[5 + par][:, u * D:(u + 1) * D], hT[par][:, c, u * P:(u + 1) * P], w2b[wb][:, c, :],
                                  start=(c == 0), stop=(c == FC - 1))
                last.then_inc(y_ps, 1)

            x_turn(0, 0)

            def moe1_pair(i):
                for k in range(8):
                    g = 8 * i + k
                    if not (isinstance(g, int) and g == G1 - 1):
                        x_turn(g + 1, (k + 1) % 2)
                    first_product(g, k % 2, k // 4, 16 * (i + 1) if k % 4 == 0 else None)
                    if known(g, 1):
                        kb = (k - 1) % 8
                        n = i + 1 if k else i
                        second_product(g - 1, (k - 1) % 2, kb // 4, 16 * n if kb % 4 == 0 else None)
            moe1_pair(0)
            with pe.Fori(1, E // 2 - 1) as i:
                moe1_pair(i)
            moe1_pair(E // 2 - 1)
            second_product(G1 - 1, 1, 1, None)

            def x2_step(s, par):
                pe.wait_ge(c_norm, s + 1)
                transposes(bank[0], text[par], cT_ps)
                pe.wait_ge(cT_ready, s + 1)
                if known(s, 1):
                    pe.wait_ge(cg_ready, s)
                for u in range(2):
                    for k in range(KC):
                        last = mm(bank[7][:, u * E:(u + 1) * E], aT[:, u, k, :], wg2[:, k, :],
                                  start=(k == 0), stop=(k == KC - 1))
                last.then_inc(cg_ps, 1)
            run_steps(pe, x2_step, 0, 2, NP_, NP_)

            def shared_step(t, par):
                g = G1 + t
                x_turn(g + 1, 1 - par)
                first_product(g, par, 0, 16 * 5 if isinstance(t, int) and t == 0 else None)
                if known(t, 1):
                    second_product(g - 1, 1 - par, 0, 16 * 5 if isinstance(t, int) and t == 1 else None)
            x_turn(G1, 0)
            shared_step(0, 0)
            shared_step(1, 1)
            count_slots(2, 1, (bank[7][:, 0:NT * E], bank[7][:, NT * E:2 * NT * E]))
            run_steps(pe, shared_step, 2, 2, GS, GS)

            def landed(t, par):
                return (80 if par else 64) + 32 * (t // 2 + 1)

            def routed_step(t, par):
                g = M2 + t
                if below(t, G2 - 1):
                    x_turn(g + 1, 1 - par)
                first_product(g, par, 1 - par, landed(t, par))
                if known(t, 1):
                    second_product(g - 1, 1 - par, par, landed(t - 1, 1 - par))
                else:
                    second_product(g - 1, 1 - par, 0, None)
            run_steps(pe, routed_step, 0, 2, G2 - 1 - (G2 - 1) % 2, G2)
            second_product(M2 + G2 - 1, (G2 - 1) % 2, G2 % 2, landed(G2 - 1, (G2 - 1) % 2))

        @block.scalar
        def _(act):
            A_ = nc.scalar.activation
            act.wait_ge(consts, NCONST)
            for dram, n in ((xs1, G1), (xs2, G2)):
                for h in range(2):
                    act.dma_start(dram[0:n * R, :].rearrange("(n h p) c -> h p n c", h=2, p=P)[h],
                                  fill[:, h, :].unsqueeze(1).broadcast_to([P, n, RW])).then_inc(filled, 16)
            act.dma_start(acc1[T:T + SPARE, :].rearrange("(h p) d -> p h d", p=P), fill[:, :, 0:D]).then_inc(filled, 16)
            act.dma_start(out[T:T + SPARE, :].rearrange("(h p) d -> p h d", p=P), fill[:, :, 0:D]).then_inc(filled, 16)

            act.wait_ge(kv_ps, 1)
            act.wait_ge(kb_zero, 2)
            for q in range(NQ):
                v = bank[4 + q][:, 0:B * NCTX].rearrange("p (b n) -> p b n", b=B)
                o = 28 * q
                A_(VB[0:DH, :, q, o + 1:o + NK], v[0:DH], ACT.Copy)
                A_(VB[DH:P, :, q, o + NK + 1:o + 2 * NK], v[DH:P], ACT.Copy)
                A_(VB[0:DH, :, q, o], nullc[0:DH, 1:2].broadcast_to([DH, B]), ACT.Copy)
                last = A_(VB[DH:P, :, q, o + NK], nullc[DH:P, 1:2].broadcast_to([DH, B]), ACT.Copy)
            last.then_inc(v_ev, 1)
            for n in range(B * 3):
                b, c = n // 3, 2 * (n % 3)
                w = min(2, PC - c)
                act.wait_ge(vw_ps, n + 1)
                A_(VW[:, b, c:c + w, :].rearrange("p c d -> p (c d)"), bank[4 + n % 4][:, 0:w * D], ACT.Copy).then_inc(vw_ev, 1)

            def att_step(s, par):
                A, Bs, C = below(s, NP_), known(s, 1) and below(s, NP_ + 1), known(s, 2)

                def prob_t(u):
                    act.wait_ge(probT_ps, 2 * (s - 1) + u + 1)
                    A_(pT[u][:, 0:4, :].rearrange("p c n -> p (c n)"), bank[3][:], ACT.Copy)
                    A_(pT[u][:, 4, :], bank[4][:, 0:P], ACT.Copy).then_inc(probT_ready, 1)

                if A:
                    act.wait_ge(textT_ps, s + 1)
                    A_(tT[:].rearrange("p u k n -> p (u k n)"), bank[0][:], ACT.Copy).then_inc(textT_ready, 1)
                if Bs:
                    prob_t(0)
                if C:
                    act.wait_ge(aT_ps, s - 1)
                    A_(aT[:].rearrange("p u k n -> p (u k n)"), bank[6][:], ACT.Copy).then_inc(aT_ready, 1)
                if Bs:
                    prob_t(1)
                if A:
                    for u in range(2):
                        act.wait_ge(sub_ready, 2 * s + u + 1)
                        A_(score[par][u][:, 0:SK], score[par][u][:, 0:SK], ACT.Exp).then_inc(exp_ready, 1)
                if Bs:
                    act.wait_ge(rstd_ready, s)
                    for u in range(2):
                        last = A_(z[:, u, :], z[:, u, :], ACT.Tanh, scale=rstd[:, 4 + u:5 + u])
                    last.then_inc(tanh_ready, 1)
            run_steps(act, att_step, 0, 4, 14, NP_ + 2)

            def route_exp(n):
                act.wait_ge(rt_sub, n)
                A_(RA[:], RA[:], ACT.Exp).then_inc(rt_exp, 1)

            route_exp(1)

            def x_turn(g, par):
                act.wait_ge(xT_ps, g + 1)
                if known(g, 2):
                    act.wait_ge(h_ps, 4 * (g - 1))
                A_(xT[par].rearrange("p k r -> p (k r)"), bank[0][:], ACT.Copy).then_inc(xT_ready, 1)

            def hidden(g, par, gelu_bias):
                if known(g, 2):
                    act.wait_ge(y_ps, g - 1)
                for j in range(FC // 2):
                    act.wait_ge(h_ps, 4 * g + j + 1)
                    if gelu_bias is None:
                        last = A_(hT[par][:, 2 * j:2 * j + 2, :].rearrange("p c r -> p (c r)"), bank[1 + j][:], ACT.Relu)
                    else:
                        for c in (2 * j, 2 * j + 1):
                            last = A_(hT[par][:, c, :], bank[1 + j][:, (c % 2) * R:(c % 2 + 1) * R], ACT.Gelu,
                                      bias=gelu_bias[:, c:c + 1])
                    last.then_inc(h_ready, 1)

            def moe1_step(g, par):
                if below(g, G1 - 1):
                    x_turn(g + 1, 1 - par)
                hidden(g, par, None)
            x_turn(0, 0)
            run_steps(act, moe1_step, 0, 2, G1 - 2, G1)

            def x2_tanh(s, par):
                act.wait_ge(acc_in[par], 16 * (s // 2 + 1))
                A_(y[par][:], y[par][:], ACT.Tanh).then_inc(c_tanh, 1)

            def x2_step(s, par):
                if below(s, NP_ - 1):
                    x2_tanh(s + 1, 1 - par)
                act.wait_ge(cT_ps, s + 1)
                A_(aT[:].rearrange("p u k n -> p (u k n)"), bank[0][:], ACT.Copy).then_inc(cT_ready, 1)
            x2_tanh(0, 0)
            run_steps(act, x2_step, 0, 2, NP_ - 2, NP_)
            route_exp(2)

            def shared_step(t, par):
                x_turn(G1 + t + 1, 1 - par)
                hidden(G1 + t, par, sb1)
            x_turn(G1, 0)
            run_steps(act, shared_step, 0, 2, GS, GS)

            def routed_step(t, par):
                if below(t, G2 - 1):
                    x_turn(M2 + t + 1, 1 - par)
                act.wait_ge(w1_in[1 - par], (80 if par else 64) + 32 * (t // 2 + 1))
                hidden(M2 + t, par, b1b[1 - par])
            run_steps(act, routed_step, 0, 2, G2 - 1 - (G2 - 1) % 2, G2)

        @block.vector
        def _(v):
            ve = nc.vector
            chain = Chain(v, dve_self)
            link = chain.link
            scratch = cell_v
            link(ve.memset(cell_v[:], 0.0))

            def rsqrt(c0, c1):
                x, r, t = var[:, c0:c1], rstd[:, c0:c1], nwt[:, c0:c1]
                link(ve.tensor_scalar(t.bitcast(I32), x.bitcast(I32), 1, None, ALU.logical_shift_right))
                link(ve.tensor_scalar(r.bitcast(I32), t.bitcast(I32), -1.0, RSQRT_SEED, ALU.mult, ALU.add))
                for k in range(3):
                    link(ve.scalar_tensor_tensor(t, r, -0.5, r, ALU.mult, ALU.mult))
                    link(ve.tensor_tensor(t, t, x, ALU.mult))
                    link(ve.scalar_tensor_tensor(r, t, 1.5, r, ALU.add, ALU.mult))

            v.wait_ge(par_in, 16 * NPAR)
            v.wait_ge(kb_zero, 2)
            link(ve.memset(var[:], 1.0))
            link(ve.memset(maskb[:], 0.0))
            ve.tensor_scalar(maskb[:, :, 1:NK], mask8[:].rearrange("p (b n) -> p b n", b=B), FMAX, -FMAX, ALU.mult,
                             ALU.add).then_inc(maskb_ready, 1)
            v.wait_ge(kv_ps, 1)
            for q in range(NQ):
                k = bank[q][:, 0:B * NCTX].rearrange("p (b n) -> p b n", b=B)
                ve.tensor_copy(KB[0:DH, :, q, 1:NK], k[0:DH])
                ve.tensor_copy(KB[DH:P, :, q, NK + 1:2 * NK], k[DH:P])
                ve.tensor_copy(KB[0:DH, :, q, 0], nullc[0:DH, 0:1].broadcast_to([DH, B]))
                last = ve.tensor_copy(KB[DH:P, :, q, NK], nullc[DH:P, 0:1].broadcast_to([DH, B]))
            last.then_inc(k_ev, 1)
            for n in range(B * KC):
                b, k = n // KC, n % KC
                v.wait_ge(m_ps, n + 1)
                for half in range(2):
                    last = ve.tensor_scalar(MQ[:, b, k, half * SK // 2:(half + 1) * SK // 2],
                                            bank[2 * (n % 2) + half][:, 0:SK // 2], gcol[:, k:k + 1], float(DH) ** -0.5,
                                            ALU.mult, ALU.mult)
                last.then_inc(m_ev, 1)
            v.wait_ge(x_in, 16 * B)
            v.wait_ge(vw_ps, B * 3)
            for i in range(2):
                for u in range(2):
                    link(ve.memset(score[i][u][:, SK:PK], 0.0))

            def att_step(s, par):
                A, L = known(s, 0) and below(s, NP_), below(s, NP_ - 1)
                Bs, C = known(s, 1) and below(s, NP_ + 1), known(s, 2)

                def mask_and_max(u):
                    v.wait_ge(score_ps, 2 * s + u + 1)
                    if known(s, 2):
                        v.wait_ge(probT_ps, 2 * (s - 2) + u + 1)
                    sc = score[par][u]
                    for half in range(2):
                        c = slice(half * SK // 2, (half + 1) * SK // 2)
                        last = ve.scalar_tensor_tensor(
                            sc[:, c].rearrange("p (h n) -> p h n", n=NK),
                            bank[1 + half][:, 0:SK // 2].rearrange("p (h n) -> p h n", n=NK), rsc[:, u:u + 1],
                            maskb[:, ds(s // 4, 1), :].broadcast_to([P, H // 2, NK]), ALU.mult, ALU.add)
                    last.then_inc(score_ready, 1)
                    v.wait_ge(score_ready, 2 * s + u + 1)
                    ve.tensor_reduce(smax[u][:], sc[:, 0:SK].rearrange("p (h n) -> p h n", n=NK), AX.X,
                                     ALU.max).then_inc(max_ready, 1)

                if C:
                    v.wait_ge(tanh_ready, s - 1)
                    v.wait_ge(text_kept, s - 1)
                    if known(s, 4):
                        v.wait_ge(aT_ps, s - 3)
                        v.wait_ge(a_kept, s - 3)
                    ve.tensor_tensor(act_a[par][:], z[:], AR[:, ds(2 * s - 4, 2), 0:D], ALU.add).then_inc(a_ready, 1)
                if A:
                    mask_and_max(0)
                if C:
                    v.wait_ge(gate_ps, s - 1)
                    ve.tensor_copy(LG[:, ds(2 * s - 4, 2), :], bank[7][:, 0:2 * E].rearrange("p (u e) -> p u e", u=2))\
                      .then_inc(gate_ready, 1)
                if L:
                    for u in range(2):
                        link(ve.bn_stats(st6[:, u, :], X[:, ds(2 * s + 2 + u, 1), :].rearrange("p o d -> p (o d)")), scratch)
                        link(ve.bn_aggr(mv_in[:, u, :], st6[:, u, :]), scratch)
                if A:
                    mask_and_max(1)
                if Bs:
                    wait_apart(v, scratch, att_ps, s)
                    for u in range(2):
                        link(ve.bn_stats(st6[:, 2 + u, :], bank[5][:, u * D:(u + 1) * D]), scratch)
                        link(ve.bn_aggr(mv_out[:, u, :], st6[:, 2 + u, :]), scratch)
                    for u in range(2):
                        last = ve.scalar_tensor_tensor(z[:, u, :], bank[5][:, u * D:(u + 1) * D], mv_out[:, u, 0:1], ogam[:],
                                                       ALU.subtract, ALU.mult)
                    last.then_inc(z_ready, 1)
                if L:
                    ve.tensor_scalar(var[:, 0:2], mv_in[:, :, 1], EPS, None, ALU.add)
                    link(ve.tensor_scalar(var[:, 2:4], mv_in[:, :, 1], 1.0 + EPS, EPS * EPS, ALU.mult, ALU.add))
                if Bs:
                    link(ve.tensor_scalar(var[:, 4:6], mv_out[:, :, 1], EPS, None, ALU.add))
                if L or Bs:
                    rsqrt(0, 6)
                if Bs:
                    ve.tensor_copy(nwt[:, 4:6], rstd[:, 4:6]).then_inc(rstd_ready, 1)
                if L:
                    if known(s, 1):
                        v.wait_ge(textT_ps, s)
                        v.wait_ge(text_kept, s)
                    for u in range(2):
                        last = ve.tensor_scalar(text[1 - par][:, u, :],
                                                X[:, ds(2 * s + 2 + u, 1), :].rearrange("p o d -> p (o d)"),
                                                mv_in[:, u, 0:1], rstd[:, u:u + 1], ALU.subtract, ALU.mult)
                    last.then_inc(text_ready, 1)
                    link(ve.tensor_tensor(rsc[:], rstd[:, 2:4], rstd[:, 0:2], ALU.mult))
                    link(ve.tensor_tensor(rsc[:], rsc[:], var[:, 0:2], ALU.mult))
                if A:
                    for u in range(2):
                        v.wait_ge(exp_ready, 2 * s + u + 1)
                        link(ve.tensor_reduce(ssum[u][:], score[par][u][:, 0:SK].rearrange("p (h n) -> p h n", n=NK), AX.X,
                                              ALU.add))
                        if known(s, 1):
                            v.wait_ge(prob_ready, 2 * s - 1 + u)
                        ve.reciprocal(srec[u][:], ssum[u][:]).then_inc(rec_ready, 1)
            run_steps(v, att_step, -1, 4, 14, NP_ + 2, chain, 2 * 25)

            def bc(a):
                return a.unsqueeze(2).broadcast_to([P, NT, E])

            def te(a):
                return a.unsqueeze(1).broadcast_to([P, NT, E])

            mx, sm, g1, g2, ix, den, w1, w2, p1, p2, k1, k2, t0, t1 = (v32[:, i, :] for i in range(14))

            def top(src, g, hot):
                link(ve.tensor_reduce(g, src, AX.X, ALU.max))
                link(ve.tensor_tensor(RT[:], src, bc(g), ALU.is_equal))
                link(ve.tensor_tensor(RT[:], RT[:], te(iota_e8[:]), ALU.mult))
                link(ve.tensor_reduce(ix, RT[:], AX.X, ALU.min))
                link(ve.tensor_tensor(hot, te(iota_e8[:]), bc(ix), ALU.is_equal))

            def softmax(n):
                link(ve.tensor_reduce(mx, LG[:], AX.X, ALU.max))
                ve.tensor_tensor(RA[:], LG[:], bc(mx), ALU.subtract).then_inc(rt_sub, 1)
                v.wait_ge(rt_exp, n)
                link(ve.tensor_reduce(sm, RA[:], AX.X, ALU.add))
                link(ve.reciprocal(t0, sm))
                link(ve.tensor_tensor(RA[:], RA[:], bc(t0), ALU.mult))

            def gate_weights(eps):
                link(ve.scalar_tensor_tensor(den, g1, eps, g2, ALU.add, ALU.add))
                link(ve.reciprocal(t0, den))
                link(ve.tensor_tensor(w1, g1, t0, ALU.mult))
                link(ve.tensor_tensor(w2, g2, t0, ALU.mult))

            def combine_weights():
                link(ve.tensor_tensor(RT[:], hot1, bc(w1), ALU.mult))
                link(ve.tensor_tensor(RB[:], hot2, bc(w2), ALU.mult))
                link(ve.tensor_tensor(AR[:, :, D:D + E], RT[:], RB[:], ALU.add))

            def pick(dst, hot, src):
                link(ve.tensor_tensor(RT[:], hot, src, ALU.mult))
                link(ve.tensor_reduce(dst, RT[:], AX.X, ALU.add))

            hot1, hot2 = OH[:, 0], OH[:, 1]
            v.wait_ge(gate_ready, NP_)
            softmax(1)
            top(RA[:], g1, hot1)
            link(ve.tensor_scalar(RT[:], hot1, -1.0, 1.0, ALU.mult, ALU.add))
            link(ve.tensor_tensor(RA[:], RA[:], RT[:], ALU.mult))
            top(RA[:], g2, hot2)
            gate_weights(1e-9)
            link(ve.tensor_scalar(t0, w2, 1.0 / THRESH, None, ALU.mult))
            link(ve.tensor_tensor(t0, prob[:], t0, ALU.is_lt))
            ve.tensor_tensor(hot2, hot2, bc(t0), ALU.mult).then_inc(rt_hot, 1)
            v.wait_ge(rt_pos, 1)
            link(ve.tensor_copy(TO[:], bank[6][:].rearrange("p (k j e) -> p k e j", k=2, e=E)))
            link(ve.tensor_tensor_scan(SCN[:].rearrange("p k e j -> p (k e j)"), seg1[:],
                                       TO[:].rearrange("p k e j -> p (k e j)"), 0.0, ALU.mult, ALU.add))
            link(ve.tensor_scalar(m1c[:], SCN[:, 0].rearrange("p e (b j) -> p b e j", b=B)[:, :, :, TPB - 1], float(CAP), None,
                                  ALU.min))
            link(ve.tensor_tensor(SCN[:], SCN[:], TO[:], ALU.subtract))
            link(ve.tensor_tensor(POS[:], bank[5][:].rearrange("p (k j e) -> p k j e", k=2, e=E),
                                  SCN[:].rearrange("p k e j -> p k j e"), ALU.add))
            link(ve.tensor_tensor(POS[:, 1].rearrange("p (b j) e -> p b j e", b=B),
                                  POS[:, 1].rearrange("p (b j) e -> p b j e", b=B),
                                  m1c[:].unsqueeze(2).broadcast_to([P, B, TPB, E]), ALU.add))
            pick(p1, hot1, POS[:, 0])
            pick(p2, hot2, POS[:, 1])
            link(ve.tensor_scalar(k1, p1, float(CAP), None, ALU.is_lt))
            link(ve.tensor_reduce(t1, hot2, AX.X, ALU.add))
            link(ve.scalar_tensor_tensor(k2, p2, float(CAP), t1, ALU.is_lt, ALU.mult))
            link(ve.scalar_tensor_tensor(k2, w2, 0.0, k2, ALU.is_gt, ALU.mult))
            link(ve.tensor_tensor(w1, w1, k1, ALU.mult))
            link(ve.tensor_tensor(w2, w2, k2, ALU.mult))
            combine_weights()
            for hot, p, k, dst, spare in ((hot1, p1, k1, slot[0], spare_row[:, 0, :]), (hot2, p2, k2, slot[1], spare_row[:, 1, :])):
                link(ve.tensor_tensor(RT[:].rearrange("p (b j) e -> p b j e", b=B), hot.rearrange("p (b j) e -> p b j e", b=B),
                                      first_slot[:].unsqueeze(2).broadcast_to([P, B, TPB, E]), ALU.mult))
                link(ve.tensor_reduce(t0, RT[:], AX.X, ALU.add))
                link(ve.tensor_tensor(t0, t0, p, ALU.add))
                link(ve.tensor_tensor(t0, t0, spare, ALU.subtract))
                link(ve.tensor_tensor(t0, t0, k, ALU.mult))
                link(ve.tensor_tensor(dst[:], t0, spare, ALU.add))
            ve.tensor_copy(t1, t0).then_inc(rt_done, 1)

            def scale_out(g, par, free, metas, w):
                v.wait_ge(y_ps, g + 1)
                free()
                v.wait_ge(meta_in[par], metas)
                for u in range(2):
                    last = ve.tensor_scalar(y[par][:, u, :], bank[5 + par][:, u * D:(u + 1) * D], w(u), None, ALU.mult)
                last.then_inc(y_ready, 1)

            def moe1_out(g, k, e):
                par = k % 2

                def free():
                    if known(g, 2):
                        v.wait_ge(added1, 32 * (g - 1))
                scale_out(g, par, free, 16 * (g // 2 + 1), lambda u: meta[par][:, u, ds(e, 1)])

            for g in range(8):
                moe1_out(g, g, g // 4)
            with v.Fori(1, E // 2) as i:
                for k in range(8):
                    moe1_out(8 * i + k, k, 2 * i + k // 4)

            def x2_step(s, par):
                v.wait_ge(c_tanh, s + 1)
                xp = X[:, ds(2 * s, 2), :]
                ve.tensor_tensor(xp, xp, y[par][:], ALU.add).then_inc(c_x, 1)
                wait_apart(v, scratch, c_x, s + 1)
                for u in range(2):
                    xu = X[:, ds(2 * s + u, 1), :].rearrange("p o d -> p (o d)")
                    link(ve.bn_stats(st6[:, u, :], xu), scratch)
                    link(ve.bn_aggr(mv_in[:, u, :], st6[:, u, :]), scratch)
                link(ve.tensor_scalar(var[:, 0:2], mv_in[:, :, 1], EPS, None, ALU.add))
                rsqrt(0, 2)
                if known(s, 2):
                    v.wait_ge(cT_ps, s - 1)
                    v.wait_ge(c_kept, s - 1)
                    v.wait_ge(xn_out[par], 16 * (s // 2))
                for u in range(2):
                    xu = X[:, ds(2 * s + u, 1), :].rearrange("p o d -> p (o d)")
                    last = ve.tensor_scalar(text[par][:, u, :], xu, mv_in[:, u, 0:1], rstd[:, u:u + 1], ALU.subtract, ALU.mult)
                last.then_inc(c_norm, 1)
                if known(s, 1):
                    x2_logits(s - 1)

            def x2_logits(s):
                v.wait_ge(cg_ps, s + 1)
                ve.tensor_copy(LG[:, ds(2 * s, 2), :], bank[7][:, 0:2 * E].rearrange("p (u e) -> p u e", u=2))\
                  .then_inc(cg_ready, 1)
            run_steps(v, x2_step, 0, 2, NP_, NP_, chain, 2 * 16)
            x2_logits(NP_ - 1)
            v.wait_ge(cg_ready, NP_)

            softmax(2)
            top(RA[:], g1, hot1)
            link(ve.scalar_tensor_tensor(RA[:], hot1, -2.0, RA[:], ALU.mult, ALU.add))
            top(RA[:], g2, hot2)
            gate_weights(0.0)
            combine_weights()
            link(ve.tensor_copy(POS[:, 1], hot1))
            ve.tensor_tensor(OH[:, 0], OH[:, 0], OH[:, 1], ALU.add).then_inc(rt_hot, 1)
            both, hot1 = OH[:, 0], POS[:, 1]

            def shared_out_step(t, par):
                v.wait_ge(y_ps, G1 + t + 1)
                v.wait_ge(c_bias, t + 1)
                if known(t, 2):
                    v.wait_ge(shared_out[par], 16 * (t // 2))
                ve.tensor_tensor(y[par][:], bank[5 + par][:].rearrange("p (u d) -> p u d", u=2), X[:, ds(2 * t, 2), :],
                                 ALU.add).then_inc(y_ready, 1)

            shared_out_step(0, 0)
            v.wait_ge(rt_pos, 2)
            tot, pos = TO[:, 0], bank[7][:, 0:NT * E].rearrange("p (j e) -> p j e", e=E)
            link(ve.tensor_copy(tot, bank[7][:, NT * E:2 * NT * E].rearrange("p (j e) -> p e j", e=E)))
            link(ve.memset(TO[:, 1], 1.0))
            link(ve.memset(TO[:, 1, :, 0:1], 0.0))
            link(ve.tensor_tensor_scan(SCN[:, 0].rearrange("p e j -> p (e j)"), TO[:, 1].rearrange("p e j -> p (e j)"),
                                       tot.rearrange("p e j -> p (e j)"), 0.0, ALU.mult, ALU.add))
            count, tiles, end, start, off = (e8[:, i, :] for i in range(5))
            link(ve.tensor_copy(count, SCN[:, 0, :, NT - 1]))
            link(ve.tensor_tensor(SCN[:, 0], SCN[:, 0], tot, ALU.subtract))
            link(ve.tensor_tensor(POS[:, 0], pos, SCN[:, 0].rearrange("p e j -> p j e"), ALU.add))
            link(ve.tensor_tensor(cmp[:], iota_256k[:].unsqueeze(1).broadcast_to([P, E, NT // 2]),
                                  count.unsqueeze(2).broadcast_to([P, E, NT // 2]), ALU.is_lt))
            link(ve.tensor_reduce(tiles, cmp[:], AX.X, ALU.add))
            link(ve.tensor_tensor_scan(end, ones[:, 0:E], tiles, 0.0, ALU.mult, ALU.add))
            link(ve.tensor_tensor(start, end, tiles, ALU.subtract))
            link(ve.tensor_scalar(off, start, float(R), None, ALU.mult))
            link(ve.tensor_tensor(POS[:, 0], POS[:, 0], te(off), ALU.add))
            pick(p1, hot1, POS[:, 0])
            pick(p2, hot2, POS[:, 0])
            link(ve.tensor_copy(slot[0][:], p1))
            link(ve.tensor_copy(slot[1][:], p2))
            it = iota_t[:].unsqueeze(2).broadcast_to([P, G2, E])
            link(ve.tensor_tensor(OHT[:], it, start.unsqueeze(1).broadcast_to([P, G2, E]), ALU.is_ge))
            link(ve.tensor_tensor(oht2[:], it, end.unsqueeze(1).broadcast_to([P, G2, E]), ALU.is_lt))
            link(ve.tensor_tensor(OHT[:], OHT[:], oht2[:], ALU.mult))
            link(ve.tensor_tensor(oht2[:], OHT[:], iota_e[:].unsqueeze(1).broadcast_to([P, G2, E]), ALU.mult))
            link(ve.tensor_reduce(eidf[:], oht2[:], AX.X, ALU.add))
            ve.tensor_copy(eid[:], eidf[:]).then_inc(rt_done, 1)
            run_steps(v, shared_out_step, 1, 2, GS, GS)

            def routed_out(t, par):
                g = M2 + t
                v.wait_ge(meta_in[par], 16 * (G1 // 2 + t // 2 + 1))
                link(ve.tensor_tensor(wsel[:], meta[par][:, :, 0:E], OHT[:, ds(t, 1), :].broadcast_to([P, 2, E]), ALU.mult))
                link(ve.tensor_reduce(wv[:], wsel[:], AX.X, ALU.add))
                v.wait_ge(y_ps, g + 1)
                v.wait_ge(w2_in[1 - par], (80 if par else 64) + 32 * (t // 2 + 1))
                link(ve.tensor_tensor(yb[:], bank[5 + par][:].rearrange("p (u d) -> p u d", u=2),
                                      b2b[1 - par][:].unsqueeze(1).broadcast_to([P, 2, D]), ALU.add))
                if known(t, 2):
                    v.wait_ge(added2, 32 * (t - 1))
                else:
                    v.wait_ge(shared_out[par], 16 * GS // 2)
                for u in range(2):
                    last = ve.tensor_scalar(y[par][:, u, :], yb[:, u, :], wv[:, u:u + 1], None, ALU.mult)
                last.then_inc(y_ready, 1)
            run_steps(v, routed_out, 0, 2, G2 - 1 - (G2 - 1) % 2, G2, chain, 2 * 3)

        @block.gpsimd
        def _(pool):
            po = nc.gpsimd
            tiles_done = pool.alloc_register("tiles_done")
            po.memset(area[:, 0:2496], 0.0).then_inc(kb_zero, 1)
            po.memset(area[:, 2496:6592], 0.0).then_inc(kb_zero, 1)
            n = [0]

            def const(ins, wait=False):
                ins.then_inc(consts, 1)
                n[0] += 1
                if wait:
                    pool.wait_ge(consts, n[0])

            def iota(dst, pattern, base=0, mult=0, wait=False):
                const(po.iota(dst, pattern, base=base, channel_multiplier=mult, allow_small_or_imprecise_dtypes=True), wait)

            const(po.memset(ident[:], 0.0))
            const(po.memset(upper[:], 1.0))
            const(po.memset(fill[:], 0.0), True)
            const(po.affine_select(out=ident[:], in_=ident[:], compare_op=ALU.not_equal, fill=1.0, base=0,
                                   pattern=[[-1, P]], channel_multiplier=1))
            const(po.affine_select(out=upper[:], in_=upper[:], compare_op=ALU.is_gt, fill=0.0, base=0,
                                   pattern=[[1, P]], channel_multiplier=-1))
            iota(fill[:, :, CID:CID + 1].rearrange("p h o -> p (h o)").bitcast(I32), [[P, 2]], base=T, mult=1)
            const(po.memset(ones[:], 1.0))
            iota(iota_e8[:], [[1, E]], base=-E)
            iota(iota_e[:], [[1, E]])
            iota(first_slot[:], [[CAP, B], [B * CAP, E]])
            iota(iota_256k[:], [[R, NT // 2]])
            iota(iota_t[:], [[1, G2]])
            assert n[0] == NCONST
            po.iota(spare_row[:], [[T, 2], [P, NT]], base=S1, channel_multiplier=1, allow_small_or_imprecise_dtypes=True)
            po.memset(AR[:, :, CID:RW], 0.0).then_inc(kb_zero, 1)
            po.memset(seg1[:], 1.0).then_inc(kb_zero, 1)
            pool.wait_ge(kb_zero, 4)
            po.memset(seg1[:].rearrange("p (s j) -> p s j", j=TPB)[:, :, 0:1], 0.0)
            po.iota(AR[:, :, CID:CID + 1].rearrange("p j o -> p (j o)").bitcast(I32), [[P, NT]], base=0, channel_multiplier=1)

            def att_step(s, par):
                A, L, C = known(s, 0) and below(s, NP_), below(s, NP_ - 1), known(s, 2)
                if C:
                    pool.wait_ge(a_ready, s - 1)
                    po.tensor_copy(AR[:, ds(2 * s - 4, 2), 0:D], act_a[par][:]).then_inc(a_kept, 1)

                def heads(op, u, col):
                    sc = score[par][u][:, 0:SK].rearrange("p (h n) -> p h n", n=NK)
                    return po.tensor_tensor(sc, sc, col[u][:].unsqueeze(2).broadcast_to([P, H, NK]), op)
                if A:
                    for u in range(2):
                        pool.wait_ge(max_ready, 2 * s + u + 1)
                        heads(ALU.subtract, u, smax).then_inc(sub_ready, 1)
                if L:
                    pool.wait_ge(text_ready, s + 2)
                    po.tensor_copy(AR[:, ds(2 * s + 2, 2), 0:D], text[1 - par][:]).then_inc(text_kept, 1)
                if A:
                    for u in range(2):
                        pool.wait_ge(rec_ready, 2 * s + u + 1)
                        heads(ALU.mult, u, srec).then_inc(prob_ready, 1)
            run_steps(pool, att_step, -1, 4, 14, NP_ + 2)

            def scatter_rows(dram, done):
                for j in range(NT):
                    for k in range(2):
                        po.indirect_dma_start(dram, bass.IndirectOffsetOnAxis(ap=slot[k][:, j:j + 1], axis=0),
                                              AR[:, j, :], None).then_inc(done, 16)

            def scatter_add(dram, par, done):
                for u in range(2):
                    po.indirect_dma_start(dram, bass.IndirectOffsetOnAxis(ap=meta[par][:, u, E:E + 1].bitcast(I32), axis=0),
                                          y[par][:, u, :], None, compute_op=ALU.add).then_inc(done, 16)

            pool.wait_ge(a_kept, NP_)
            pool.wait_ge(rt_done, 1)
            pool.wait_ge(filled, 16 * 6)
            scatter_rows(xs1, rows_out)
            pool.wait_ge(rows_out, 16 * 2 * NT)
            pool.wait_ge(acc_init, 16 * NP_)

            def meta_load(dram, g, par, base):
                po.dma_start(meta[par][:], dram[ds(g * R, R), D:D + E + 1].rearrange("(h p) d -> p h d", p=P))\
                  .then_inc(meta_in[par], 16)

            def tile_step(n, dram, sums, first, done):
                def step(t, par):
                    if known(t, 2):
                        pool.wait_ge(done, 32 * (t - 1))
                    if below(t, n):
                        meta_load(dram, t, par, 0)
                    if known(t, 1):
                        pool.reg_mov(tiles_done, first + t)
                        pool.wait_ge(a_kept, NP_)
                        pool.wait_ge(y_ready, tiles_done)
                        scatter_add(sums, 1 - par, done)
                return step
            run_steps(pool, tile_step(G1, xs1, acc1, 0, added1), 0, 2, G1, G1 + 1)
            pool.wait_ge(added1, 32 * G1)

            def x2_step(s, par):
                pool.wait_ge(c_norm, s + 1)
                po.tensor_copy(AR[:, ds(2 * s, 2), 0:D], text[par][:]).then_inc(c_kept, 1)
                xp = X[:, ds(2 * s, 2), :]
                po.tensor_tensor(xp, xp, sb2[:].unsqueeze(1).broadcast_to([P, 2, D]), ALU.add).then_inc(c_bias, 1)
            run_steps(pool, x2_step, 0, 0, NP_, NP_)
            pool.wait_ge(c_kept, NP_)
            pool.wait_ge(rt_done, 2)
            scatter_rows(xs2, rows_out2)
            pool.wait_ge(rows_out2, 16 * 2 * NT)
            for i in range(2):
                pool.wait_ge(shared_out[i], 16 * GS // 2)
            run_steps(pool, tile_step(G2, xs2, out, M2, added2), 0, 2, G2 - G2 % 2, G2 + 1)


def kernel(x, ctx_1024, fside_BxS_0, mask_BxS2_bk0, L0_xattn_ln_gamma, L0_xattn_null_kv, L0_xattn_Wq, L0_xattn_Wkv,
           L0_xattn_Wo, L0_xattn_out_gamma, L0_xattn_w_gate, L0_xattn_w1, L0_xattn_w2, L0_ffn_gate_w, L0_ffn_W1,
           L0_ffn_b1, L0_ffn_W2, L0_ffn_b2, L0_ffn_sW1, L0_ffn_sb1, L0_ffn_sW2, L0_ffn_sb2):
    import numpy as np
    import concourse.bacc as bacc
    from concourse.bass_utils import run_bass_kernel_spmd

    def a(v):
        return np.asarray(v)

    def w1_rows(w):
        return a(w).reshape(-1, KC, P, F).transpose(0, 2, 1, 3).reshape(-1, P, KC * F)

    def w2_rows(w):
        return a(w).reshape(-1, FC, P, D).transpose(0, 2, 1, 3).reshape(-1, P, FC * D)

    data = {
        "x": a(x).reshape(T, D),
        "ctxT": a(ctx_1024).reshape(B * NCTX, D).T,
        "probs": a(fside_BxS_0).reshape(NT, P).T,
        "mask": a(mask_BxS2_bk0).reshape(B * NCTX),
        "ln_g": a(L0_xattn_ln_gamma).reshape(KC, P).T,
        "null": a(L0_xattn_null_kv).T,
        "WqT": a(L0_xattn_Wq).T,
        "Wkv": a(L0_xattn_Wkv),
        "Wo": a(L0_xattn_Wo),
        "out_g": a(L0_xattn_out_gamma),
        "wg1": a(L0_xattn_w_gate),
        "wg2": a(L0_ffn_gate_w).T,
        "W1a": w1_rows(L0_xattn_w1), "W2a": w2_rows(L0_xattn_w2),
        "W1b": w1_rows(L0_ffn_W1), "W2b": w2_rows(L0_ffn_W2),
        "sW1": w1_rows(L0_ffn_sW1), "sW2": w2_rows(L0_ffn_sW2),
        "b1": a(L0_ffn_b1).reshape(E, FC, P).transpose(0, 2, 1),
        "b2": a(L0_ffn_b2),
        "sb1": a(L0_ffn_sb1).reshape(FC, P).T,
        "sb2": a(L0_ffn_sb2),
    }
    nc = bacc.Bacc("TRN2", target_bir_lowering=False, num_devices=1)
    arrays, io = {}, {}
    for name, v in data.items():
        v = np.ascontiguousarray(v)
        arrays[f"in_{name}"] = v
        io[name] = nc.dram_tensor(f"in_{name}", v.shape, mybir.dt.from_np(v.dtype), kind="ExternalInput").ap()
    io["out"] = nc.dram_tensor("out_rows", (T + SPARE, D), F32, kind="ExternalOutput").ap()
    build(nc, io)
    r = run_bass_kernel_spmd(nc, [arrays], core_ids=[0])
    return r.results[0]["out_rows"][:T].reshape(B, N, D)
```

```python
from contextlib import ExitStack

import concourse.bass as bass
from concourse import mybir

F32 = mybir.dt.float32
F32R = mybir.dt.float32r
I32 = mybir.dt.int32
U8 = mybir.dt.uint8
ALU = mybir.AluOpType
ACT = mybir.ActivationFunctionType
AX = mybir.AxisListType
ds = bass.ds

P = 128
B, N, D = 4, 1024, 256
KC = D // P
NCTX = 77
NK = NCTX + 1
H, DH = 8, 64
NQ = H * DH // P
SK = H * NK
PK = 640
PC = PK // P
E = 8
F = 1024
FC = F // P
CAP = 2 * N // E
THRESH = 0.2
T = B * N
NT = T // P
NP_ = NT // 2
HT = NT // 2
TPB = N // P
R = 2 * P
RW = 272
CID = D + E
S1 = E * B * CAP
G1 = S1 // R
GS = T // R
G2 = (2 * T + E * (R - 1)) // R
S2 = G2 * R
SPARE = 2 * P
S1ROWS = S1 + 2 * T
EPS = 1e-5
FMAX = 3.4028234663852886e38
RSQRT_SEED = 1597463007.0


def build(nc, io):
    with ExitStack() as ctx:
        def sb(name, shape, dt=F32):
            return ctx.enter_context(nc.sbuf_tensor(name, shape, dt))

        def sem(name):
            return ctx.enter_context(nc.semaphore(name))

        bank = [ctx.enter_context(nc.psum_tensor(f"bank{i}", [P, 512], F32)) for i in range(8)]

        xs1 = nc.dram_tensor("xs1", [S1ROWS, RW], F32).ap()
        xs2 = nc.dram_tensor("xs2", [S2, RW], F32).ap()
        xn2 = nc.dram_tensor("xn2", [T, D], F32).ap()
        x2b = nc.dram_tensor("x2b", [T, D], F32).ap()
        acc1 = nc.dram_tensor("acc1", [T + SPARE, D], F32).ap()
        out = io["out"]

        AR = sb("AR", [P, NT, RW])
        ident = sb("ident", [P, P])
        upper = sb("upper", [P, P])
        ones = sb("ones", [P, P])
        iota_e8 = sb("iota_e8", [P, E])
        iota_256k = sb("iota_256k", [P, NT // 2])
        iota_t = sb("iota_t", [P, G2])
        iota_e = sb("iota_e", [P, E])
        sb2 = sb("sb2", [P, D])
        sb1 = sb("sb1", [P, FC])
        wg2 = sb("wg2", [P, KC, E])
        b1b = [sb(f"b1b{i}", [P, FC]) for i in range(2)]
        b2b = [sb(f"b2b{i}", [P, D]) for i in range(2)]
        text = [sb(f"text{i}", [P, 2, D]) for i in range(2)]
        xr = text
        y = [sb(f"y{i}", [P, 2, D]) for i in range(2)]
        xn = text + y
        meta = [sb(f"meta{i}", [P, 2, E + 1]) for i in range(2)]
        wsel = sb("wsel", [P, 2, E])
        wv = sb("wv", [P, 2])
        ln = sb("ln", [P, 7, NT])
        LG = sb("LG", [P, NT, E])
        RA = sb("RA", [P, NT, E])
        RB = sb("RB", [P, NT, E])
        rows6 = RB[:, :, 0:6]
        RT = sb("RT", [P, NT, E])
        OH = sb("OH", [P, 2, NT, E])
        OH1 = OH[:].rearrange("p k j e -> p (k j e)").rearrange("p (h k j e) -> p h k j e", h=2, k=2, e=E)
        TO = sb("TO", [P, 2, E, NT])
        SCN = sb("SCN", [P, 2, E, NT])
        POS = sb("POS", [P, 2, NT, E])
        v32 = sb("v32", [P, 16, NT])
        slot = [sb(f"slot{k}", [P, NT], I32) for k in range(2)]
        cmp = TO[:].rearrange("p k e j -> p (k e j)")[:, 0:E * NT // 2].rearrange("p (e n) -> p e n", e=E)
        e8 = sb("e8", [P, 5, E])
        OHT = sb("OHT", [P, G2, E])
        oht2 = SCN[:].rearrange("p k e j -> p (k e j)")[:, 0:G2 * E].rearrange("p (t e) -> p t e", e=E)
        eidf = sb("eidf", [P, G2])
        eid = sb("eid", [P, G2], I32)
        cell_v = sb("cell_v", [P, 2])

        with ExitStack() as first:
            def sa(name, shape, dt=F32):
                return first.enter_context(nc.sbuf_tensor(name, shape, dt))

            X = sa("X", [P, NT, D])
            area = sa("area", [P, 12288])
            KB = area[:, 0:2496].rearrange("p (b q c) -> p b q c", b=B, q=NQ)
            VB = area[:, 2496:6592].rearrange("p (b q c) -> p b q c", b=B, q=NQ)
            MQ = area[:, 6592:11584].rearrange("p (b k c) -> p b k c", b=B, k=KC)
            VW = sa("VW", [P, B, PC, D])
            area3 = sa("area3", [P, 4712])
            wkv = area3[:, 0:2048].rearrange("p (k n) -> p k n", k=KC)
            wqT = area3[:, 2048:3072].rearrange("p (q n) -> p q n", q=NQ)
            wo = area3[:, 3072:4096].rearrange("p (q n) -> p q n", q=NQ)
            ctxT = area3[:, 4096:4712].rearrange("p (k n) -> p k n", k=KC)
            score = [[area3[:, PK * (2 * i + u):PK * (2 * i + u + 1)] for u in range(2)] for i in range(2)]
            pT = [area3[:, PK * (4 + u):PK * (5 + u)].rearrange("p (c n) -> p c n", c=PC) for u in range(2)]
            z = [sa(f"z{i}", [P, 2, D]) for i in range(2)]
            act_a = [sa(f"act_a{i}", [P, 2, D]) for i in range(2)]
            tT = sa("tT", [P, 2, KC, P])
            aT = sa("aT", [P, 2, KC, P])
            smax = [[sa(f"smax{i}{u}", [P, H]) for u in range(2)] for i in range(2)]
            ssum = [sa(f"ssum{u}", [P, H]) for u in range(2)]
            srec = [sa(f"srec{u}", [P, H]) for u in range(2)]
            st6 = sa("st6", [P, 2, 6])
            mv_out = sa("mv_out", [P, 2, 2])
            var = sa("var", [P, 2])
            rstd = sa("rstd", [P, 2])
            nwt = sa("nwt", [P, 2])
            first_slot = sa("first_slot", [P, B, E])
            spare_row = sa("spare_row", [P, 2, NT])
            seg1 = sa("seg1", [P, 2 * E * HT])
            m1c = sa("m1c", [P, B // 2, E])
            fill = sa("fill", [P, 2, RW])
            nullc = sa("nullc", [P, 2])
            gcol = sa("gcol", [P, KC])
            ogam = sa("ogam", [P, D])
            mask8 = sa("mask8", [P, B * NCTX], U8)
            maskb = sa("maskb", [P, B, NK])
            prob = sa("prob", [P, NT])
            wg1 = sa("wg1", [P, KC, E])

        raw = sb("raw", [P, 4, F])
        w_h = [sb(f"w_h{i}", [P, 4, F], F32R) for i in range(2)]
        w_l = [sb(f"w_l{i}", [P, 4, F], F32R) for i in range(2)]
        h_h = [sb(f"h_h{i}", [P, FC, R], F32R) for i in range(2)]
        h_l = [sb(f"h_l{i}", [P, FC, R], F32R) for i in range(2)]
        x_h = [sb(f"x_h{i}", [P, KC, R], F32R) for i in range(2)]
        x_l = [sb(f"x_l{i}", [P, KC, R], F32R) for i in range(2)]
        gel = sb("gel", [P, FC // 2, 2 * R])
        x2 = [raw[:, 2 * i:2 * i + 2, :].rearrange("p q f -> p (q f)").rearrange("p (t d) -> p t d", t=TPB)
              for i in range(2)]
        xnT = [gel[:, i, :].rearrange("p (u k n) -> p u k n", u=2, k=KC) for i in range(2)]
        yb = sb("yb", [P, 2, D])

        x_in, par_in, consts, kb_zero = sem("x_in"), sem("par_in"), sem("consts"), sem("kb_zero")
        filled = [sem(f"filled{m}") for m in range(2)]
        kv_ps, k_ev, v_ev, m_ps, m_ev, vw_ps, vw_ev, maskb_ready = (sem(n) for n in (
            "kv_ps", "k_ev", "v_ev", "m_ps", "m_ev", "vw_ps", "vw_ev", "maskb_ready"))
        (text_ready, textT_ps, textT_ready, att_ps, z_ready, rstd_ready, tanh_ready, a_ready,
         aT_ps, aT_ready, gate_ps, gate_ready) = (sem(n) for n in (
             "text_ready", "textT_ps", "textT_ready", "att_ps", "z_ready", "rstd_ready", "tanh_ready", "a_ready",
             "aT_ps", "aT_ready", "gate_ps", "gate_ready"))
        text_kept = [sem(f"text_kept{i}") for i in range(2)]
        a_kept = [sem(f"a_kept{i}") for i in range(2)]
        (score_ps, score_ready, max_ready, sub_ready, exp_ready, rec_ready, prob_ready, probT_ps,
         probT_ready) = (sem(n) for n in (
             "score_ps", "score_ready", "max_ready", "sub_ready", "exp_ready", "rec_ready", "prob_ready",
             "probT_ps", "probT_ready"))
        dve_self = sem("dve_self")
        rt_sub, rt_exp, rt_hot, rt_pos, rt_taken, rt_done = (sem(n) for n in (
            "rt_sub", "rt_exp", "rt_hot", "rt_pos", "rt_taken", "rt_done"))
        rows_out, rows_out2 = [sem(f"rows_out{i}") for i in range(2)], sem("rows_out2")
        x_rows = [sem(f"x_rows{i}") for i in range(2)]
        meta_in = [sem(f"meta_in{i}") for i in range(2)]
        b1_in = [sem(f"b1_in{i}") for i in range(2)]
        b2_in = [sem(f"b2_in{i}") for i in range(2)]
        w1_in, w2_in, x_low, h_low, gelu_done = (sem(n) for n in ("w1_in", "w2_in", "x_low", "h_low", "gelu_done"))
        w_high = [sem(f"w{m}_high") for m in (1, 2)]
        w_low = [sem(f"w{m}_low") for m in (1, 2)]
        shared_out = [sem(f"shared_out{i}") for i in range(2)]
        xT_ps, xT_ready, h_ps, h_ready, y_ps, y_ready, added1, added2 = (sem(n) for n in (
            "xT_ps", "xT_ready", "h_ps", "h_ready", "y_ps", "y_ready", "added1", "added2"))
        acc_in = [sem(f"acc_in{b}") for b in range(B)]
        x2_in = [sem(f"x2_in{b}") for b in range(B)]
        x2_kept = [sem(f"x2_kept{b}") for b in range(B)]
        y_in = [sem(f"y_in{i}") for i in range(2)]
        xn_out = [sem(f"xn_out{i}") for i in range(4)]
        c_tanh, c_norm, c_bias, cT_ps, cT_ready, cg_ps, cg_ready = (sem(n) for n in (
            "c_tanh", "c_norm", "c_bias", "cT_ps", "cT_ready", "cg_ps", "cg_ready"))

        SHARED = 2 * E
        NPAR = 14
        FILL = 5
        NCONST = 12
        M2 = G1 + GS
        block = ctx.enter_context(nc.Block())

        def rows(dram, g, width=D):
            return dram[ds(g * R, R), 0:width].rearrange("(h p) d -> p h d", p=P)

        def run_steps(eng, step, lo, first, last, hi, chain=None, per=0):
            for s in range(lo, first):
                step(s, s % 2)
            if last > first:
                with eng.Fori(first // 2, last // 2) as i:
                    if chain:
                        chain.enter((i - first // 2) * per)
                    step(2 * i, 0)
                    step(2 * i + 1, 1)
                    if chain:
                        chain.leave((last - first) // 2, per)
            for s in range(last, hi):
                step(s, s % 2)

        def wait_apart(eng, cell, own, n):
            eng.wait_ge(own, n)
            eng.tensor_tensor(cell[:, 1:2], cell[:, 0:1], cell[:, 0:1], ALU.add)

        class Chain:

            def __init__(self, eng, own):
                self.eng, self.own, self.n, self.base = eng, own, 0, 0

            def link(self, ins, scratch=None):
                ins.then_inc(self.own, 1)
                self.n += 1
                if scratch:
                    wait_apart(self.eng, scratch, self.own, self.base + self.n)
                else:
                    self.eng.wait_ge(self.own, self.base + self.n)

            def enter(self, base):
                self.base, self.at = base, self.n

            def leave(self, turns, per):
                assert self.n - self.at == per, (self.n - self.at, per)
                self.n, self.base = self.at + turns * per, 0

        def slots_of(g, par, half):
            return 2 * g - par - (G1 - 2) * half

        def known(s, least):
            return not isinstance(s, int) or s >= least

        def below(s, end):
            return not isinstance(s, int) or s < end

        @block.sync
        def _(sp):
            def par(dst, src):
                sp.dma_start(dst, src).then_inc(par_in, 16)

            par(ctxT, io["ctxT"].rearrange("(k p) n -> p k n", p=P))
            par(wkv, io["Wkv"].rearrange("(k p) n -> p k n", p=P))
            par(nullc[0:DH, :], io["null"])
            par(nullc[DH:P, :], io["null"])
            par(wqT, io["WqT"].rearrange("(q p) n -> p q n", p=P))
            par(wo, io["Wo"].rearrange("(q p) n -> p q n", p=P))
            par(gcol[:], io["ln_g"])
            par(mask8[:], io["mask"].partition_broadcast(P))
            par(ogam[:], io["out_g"].partition_broadcast(P))
            par(sb2[:], io["sb2"].partition_broadcast(P))
            par(prob[:], io["probs"])
            par(wg1[:], io["wg1"].rearrange("(k p) n -> p k n", p=P))
            par(wg2[:], io["wg2"].rearrange("(k p) n -> p k n", p=P))
            par(sb1[:], io["sb1"])
            for b in range(B):
                sp.dma_start(X[:, b * TPB:(b + 1) * TPB, :],
                             io["x"][b * N:(b + 1) * N, :].rearrange("(t p) d -> p t d", p=P)).then_inc(x_in, 16)

            def copy_step(s, par):
                if below(s, NP_):
                    sp.wait_ge(text_ready, s + 1)
                    sp.dma_start(AR[:, ds(2 * s, 2), 0:D], text[par][:]).then_inc(text_kept[par], 16)
                if known(s, 3):
                    sp.wait_ge(a_ready, s - 2)
                    sp.dma_start(AR[:, ds(2 * s - 6, 2), 0:D], act_a[1 - par][:]).then_inc(a_kept[1 - par], 16)
                    sp.dma_start(rows(acc1, s - 3), act_a[1 - par][:]).then_inc(a_kept[1 - par], 16)
            run_steps(sp, copy_step, 0, 4, NP_, NP_ + 3)

            def w1_load(n, e, name):
                if known(n, 1):
                    sp.wait_ge(w_low[0], 2 * n)
                sp.dma_start(raw[:, 0:2, :], io[name][ds(e, 1), :, :].rearrange("o p (k f) -> p (o k) f", k=KC)).then_inc(w1_in, 16)

            def w2_load(n, e, name):
                if known(n, 1):
                    sp.wait_ge(w_low[1], 2 * n)
                sp.dma_start(raw[:, 2:4, :], io[name][ds(e, 1), :, :].rearrange("o p (h f) -> p (o h) f", h=2)).then_inc(w2_in, 16)

            sp.wait_ge(att_ps, NP_)
            w1_load(0, 0, "W1a")
            w2_load(0, 0, "W2a")
            sp.wait_ge(rows_out[0], 16 * 2 * HT)

            def x_load(g, par, src):
                if known(g, 2):
                    sp.wait_ge(xT_ps, g - 1)
                sp.dma_start(xr[par][:], src).then_inc(x_rows[par], 16)

            def moe1_loads(n, half, following, names):
                for k in range(2):
                    x_load(2 * n + k, k, rows(xs1, slots_of(2 * n + k, k, half)))
                    (w1_load, w2_load)[k](n + 1, following, names[k])
            moe1_loads(0, 0, 1, ("W1a", "W2a"))
            with sp.Fori(1, E - 1) as n:
                moe1_loads(n, 0, n + 1, ("W1a", "W2a"))
            moe1_loads(E - 1, 0, 0, ("W1a", "W2a"))
            sp.wait_ge(rows_out[1], 16 * 2 * HT)
            with sp.Fori(E, 2 * E - 1) as n:
                moe1_loads(n, 1, n + 1 - E, ("W1a", "W2a"))
            moe1_loads(2 * E - 1, 1, 0, ("sW1", "sW2"))

            sp.wait_ge(added1, 32 * G1)

            sp.wait_ge(w_low[1], 2 * SHARED + 2)
            for b in range(B):
                sp.dma_start(AR[:, b * TPB:(b + 1) * TPB, 0:D],
                             acc1[b * N:(b + 1) * N, :].rearrange("(t p) d -> p t d", p=P)).then_inc(acc_in[b], 16)
                if b < 2:
                    sp.dma_start(x2[b], io["x"][b * N:(b + 1) * N, :].rearrange("(t p) d -> p t d", p=P)).then_inc(x2_in[b], 16)

            with sp.Fori(0, B) as b:
                for k in range(4):
                    sp.wait_ge(c_norm, 4 * b + k + 1)
                    sp.dma_start(rows(xn2, 4 * b + k), xn[k][:]).then_inc(xn_out[k], 16)
                    sp.dma_start(AR[:, ds(8 * b + 2 * k, 2), 0:D], xn[k][:]).then_inc(xn_out[k], 16)
            for k in range(4):
                sp.wait_ge(xn_out[k], 32 * B)
            sp.wait_ge(cT_ps, NP_)

            for b in range(B):
                sp.wait_ge(x2_kept[b], 16)
            for t in range(2):
                x_load(G1 + t, t, rows(xn2, t))
                sp.dma_start(y[t][:], rows(x2b, t)).then_inc(y_in[t], 16)

            def shared_store(t, par):
                sp.wait_ge(y_ready, G1 + t + 1)
                sp.dma_start(rows(out, t), y[par][:]).then_inc(shared_out[par], 16)

            x_load(G1 + 2, 0, rows(xn2, 2))

            def shared_step(t, par):
                if below(t, GS - 3):
                    x_load(G1 + t + 3, 1 - par, rows(xn2, t + 3))
                shared_store(t, par)
                sp.wait_ge(shared_out[par], 16 * (t // 2 + 1))
                sp.dma_start(y[par][:], rows(x2b, t + 2)).then_inc(y_in[par], 16)
            run_steps(sp, shared_step, 0, 0, GS - 4, GS - 4)

            sp.wait_ge(rt_done, 3)

            def expert_of(t):
                return sp.value_load(eid[0:1, ds(t, 1)], min_val=0, max_val=E - 1)

            def routed_w1(t, par):
                e, g = expert_of(t), M2 + t
                if known(t, 2):
                    sp.wait_ge(h_ready, 4 * g - 4)
                sp.dma_start(b1b[par][:], io["b1"][ds(e, 1), :, :].rearrange("o p c -> p (o c)")).then_inc(b1_in[par], 16)
                w1_load(SHARED + 1 + t, e, "W1b")

            def routed_w2(t, par):
                e, g = expert_of(t), M2 + t
                w2_load(SHARED + 1 + t, e, "W2b")
                if known(t, 2):
                    sp.wait_ge(y_ready, g - 1)
                sp.dma_start(b2b[par][:], io["b2"][ds(e, 1), :].broadcast_to([P, D])).then_inc(b2_in[par], 16)

            routed_w1(0, 0)
            routed_w2(0, 0)
            shared_step(GS - 4, 0)
            sp.wait_ge(rows_out2, 16 * 2 * NT)
            x_load(M2, 0, rows(xs2, 0))
            shared_step(GS - 3, 1)
            shared_store(GS - 2, 0)
            x_load(M2 + 1, 1, rows(xs2, 1))
            routed_w1(1, 1)

            def routed_step(t, par):
                if below(t, G2 - 2):
                    x_load(M2 + t + 2, par, rows(xs2, t + 2))
                    routed_w1(t + 2, par)
                routed_w2(t + 1, 1 - par)
            routed_step(0, 0)
            shared_store(GS - 1, 1)
            run_steps(sp, routed_step, 1, 2, G2 - 3 - (G2 - 3) % 2, G2 - 1)
            sp.wait_ge(added2, 32 * G2)
            for i in range(2):
                sp.wait_ge(shared_out[i], 16 * GS // 2)

        @block.tensor
        def _(pe):
            mm = nc.tensor.matmul
            pe.wait_ge(par_in, 16 * NPAR)
            for kv in range(2):
                for q in range(NQ):
                    for k in range(KC):
                        last = mm(bank[4 * kv + q][:, 0:B * NCTX],
                                  wkv[:, k, kv * H * DH + q * P:kv * H * DH + (q + 1) * P], ctxT[:, k, :],
                                  start=(k == 0), stop=(k == KC - 1))
            last.then_inc(kv_ps, 1)
            pe.wait_ge(k_ev, 1)
            for b in range(B):
                for k in range(KC):
                    n = b * KC + k
                    if n >= 2:
                        pe.wait_ge(m_ev, n - 1)
                    for q in range(NQ):
                        last = mm(bank[2 * (n % 2) + q // 2][:, (q % 2) * 2 * NK:(q % 2 + 1) * 2 * NK],
                                  wqT[:, q, k * P:(k + 1) * P], KB[:, b, q, :], start=True, stop=True)
                    last.then_inc(m_ps, 1)
            pe.wait_ge(v_ev, 1)
            for b in range(B):
                for c2 in range(3):
                    n = b * 3 + c2
                    if n >= 4:
                        pe.wait_ge(vw_ev, n - 3)
                    for c in range(2 * c2, min(2 * c2 + 2, PC)):
                        parts = [(q, v) for q, v in ((c - 1, 1), (c, 0)) if 0 <= q < NQ]
                        for m, (q, v) in enumerate(parts):
                            last = mm(bank[4 + n % 4][:, (c % 2) * D:(c % 2 + 1) * D], VB[:, b, q, v * P:(v + 1) * P],
                                      wo[:, q, :], start=(m == 0), stop=(m == len(parts) - 1))
                    last.then_inc(vw_ps, 1)
            pe.wait_ge(m_ev, B * KC)
            pe.wait_ge(vw_ev, B * 3)
            pe.wait_ge(consts, NCONST)

            def count_slots(n, hot, banks):
                pe.wait_ge(rt_hot, n)
                mm(banks[0], upper[:], hot, start=True, stop=True)
                mm(banks[1], ones[:], hot, start=True, stop=True).then_inc(rt_pos, 1)

            def choices(half):
                return OH1[:, half].rearrange("p k j e -> p (k j e)")

            def transposes(dst, src, done):
                for u in range(2):
                    for k in range(KC):
                        last = nc.tensor.transpose(dst[:, (u * KC + k) * P:(u * KC + k + 1) * P],
                                                   src[:, u, k * P:(k + 1) * P], ident[:])
                last.then_inc(done, 1)

            def att_step(s, par):
                A, Bs = known(s, 0) and below(s, NP_), known(s, 2) and below(s, NP_ + 2)
                G = known(s, 4)

                def scores(u):
                    if u == 0:
                        pe.wait_ge(textT_ready, s + 1)
                    if known(s, 1) or u:
                        pe.wait_ge(score_ready, 2 * s + u)
                    for half in range(2):
                        for k in range(KC):
                            last = mm(bank[1 + half][:, 0:SK // 2], tT[:, u, k, :],
                                      MQ[:, ds(s // 4, 1), k, half * SK // 2:(half + 1) * SK // 2].rearrange("p b c -> p (b c)"),
                                      start=(k == 0), stop=(k == KC - 1))
                    last.then_inc(score_ps, 1)

                def prob_t(u):
                    pe.wait_ge(prob_ready, 2 * (s - 2) + u + 1)
                    for c in range(PC):
                        last = nc.tensor.transpose(bank[3 + c // 4][:, (c % 4) * P:(c % 4 + 1) * P],
                                                   score[par][u][:, c * P:(c + 1) * P], ident[:])
                    last.then_inc(probT_ps, 1)

                def attend(u):
                    pe.wait_ge(probT_ready, 2 * (s - 2) + u + 1)
                    if u == 0 and known(s, 3):
                        pe.wait_ge(z_ready, s - 2)
                    for c in range(PC):
                        last = mm(bank[5][:, u * D:(u + 1) * D], pT[u][:, c, :],
                                  VW[:, ds((s - 2) // 4, 1), c, :].rearrange("p b d -> p (b d)"),
                                  start=(c == 0), stop=(c == PC - 1))
                    if u:
                        last.then_inc(att_ps, 1)

                if Bs:
                    prob_t(0)
                if A:
                    scores(0)
                if G:
                    pe.wait_ge(a_ready, s - 3)
                    transposes(bank[6], act_a[par], aT_ps)
                if Bs:
                    attend(0)
                    prob_t(1)
                if A:
                    scores(1)
                if below(s, NP_ - 1):
                    pe.wait_ge(text_ready, s + 2)
                    transposes(bank[0], text[1 - par], textT_ps)
                if G:
                    pe.wait_ge(aT_ready, s - 3)
                    if known(s, 5):
                        pe.wait_ge(gate_ready, s - 4)
                    if isinstance(s, int) and s == 14:
                        pe.wait_ge(rt_taken, 1)
                    for u in range(2):
                        for k in range(KC):
                            last = mm(bank[7][:, u * E:(u + 1) * E], aT[:, u, k, :], wg1[:, k, :],
                                      start=(k == 0), stop=(k == KC - 1))
                    last.then_inc(gate_ps, 1)
                if Bs:
                    attend(1)
            run_steps(pe, att_step, -1, 6, 14, 14)
            pe.wait_ge(gate_ready, 14 - 4)
            count_slots(1, choices(0), (bank[7][:, 0:2 * HT * E], bank[7][:, 2 * HT * E:4 * HT * E]))
            run_steps(pe, att_step, 14, 14, 14, NP_ + 4)
            pe.wait_ge(gate_ready, NP_)
            count_slots(2, choices(1), (bank[7][:, 0:2 * HT * E], bank[7][:, 2 * HT * E:4 * HT * E]))

            def x_turn(g, par):
                pe.wait_ge(x_rows[par], 16 * (g // 2 + 1))
                if known(g, 1):
                    pe.wait_ge(x_low, g)
                for k in range(KC):
                    for u in range(2):
                        last = nc.tensor.transpose(bank[0][:, k * R + u * P:k * R + (u + 1) * P],
                                                   xr[par][:, u, k * P:(k + 1) * P], ident[:])
                last.then_inc(xT_ps, 1)

            def product(dst, lhs, rhs, chunks):
                for c in range(chunks):
                    for n, (p, q) in enumerate(((0, 0), (0, 1), (1, 0))):
                        last = mm(dst, lhs(c, p), rhs(c, q), start=(c == 0 and n == 0), stop=(c == chunks - 1 and n == 2))
                return last

            def first_product(g, par, n, wb):
                pe.wait_ge(x_low, g + 1)
                if n is not None:
                    pe.wait_ge(w_low[0], 2 * n + 2)
                for j in range(FC // 2):
                    if known(g, 1):
                        pe.wait_ge(h_low, 4 * (g - 1) + j + 1)
                    for c in (2 * j, 2 * j + 1):
                        last = product(bank[1 + j][:, (c % 2) * R:(c % 2 + 1) * R],
                                       lambda k, part: (w_h, w_l)[part][wb][:, k, c * P:(c + 1) * P],
                                       lambda k, part: (x_h, x_l)[part][par][:, k, :], KC)
                    last.then_inc(h_ps, 1)

            def second_product(g, par, n, wb):
                pe.wait_ge(h_low, 4 * g + 4)
                if n is not None:
                    pe.wait_ge(w_low[1], 2 * n + 2)
                if known(g, 2):
                    pe.wait_ge(y_ready, g - 1)
                for u in range(2):
                    last = product(bank[5 + par][:, u * D:(u + 1) * D],
                                   lambda c, part: (h_h, h_l)[part][par][:, c, u * P:(u + 1) * P],
                                   lambda c, part: (w_h, w_l)[part][wb][:, 2 + c // 4, (c % 4) * D:(c % 4 + 1) * D], FC)
                last.then_inc(y_ps, 1)

            x_turn(0, 0)

            def moe1_sets(i):
                for k in range(4):
                    g, n = 4 * i + k, 2 * i + k // 2
                    if below(g, G1 - 1):
                        x_turn(g + 1, (k + 1) % 2)
                    first_product(g, k % 2, n if k % 2 == 0 else None, k // 2)
                    if known(g, 1):
                        second_product(g - 1, (k - 1) % 2, n if k % 2 else None, (k - 1) % 4 // 2)
            moe1_sets(0)
            with pe.Fori(1, E - 1) as i:
                moe1_sets(i)
            moe1_sets(E - 1)
            second_product(G1 - 1, 1, None, 1)

            def x2_gate(s, par):
                pe.wait_ge(cT_ready, s + 1)
                if known(s, 1):
                    pe.wait_ge(cg_ready, s)
                for u in range(2):
                    for k in range(KC):
                        last = mm(bank[7][:, u * E:(u + 1) * E], xnT[par][:, u, k, :], wg2[:, k, :],
                                  start=(k == 0), stop=(k == KC - 1))
                last.then_inc(cg_ps, 1)

            def x2_batch(b):
                for k in range(4):
                    s = 4 * b + k
                    pe.wait_ge(c_norm, s + 1)
                    if known(s, 1):
                        pe.wait_ge(cT_ready, s)
                    transposes(bank[0] if k % 2 == 0 else bank[6], xn[k], cT_ps)
                    if known(s, 1):
                        x2_gate(s - 1, 1 - k % 2)
            x2_batch(0)
            with pe.Fori(1, B) as b:
                x2_batch(b)
            x2_gate(NP_ - 1, 1)

            def shared_step(t, par):
                g = G1 + t
                x_turn(g + 1, 1 - par)
                first_product(g, par, None if known(t, 1) else SHARED, 0)
                if known(t, 1):
                    second_product(g - 1, 1 - par, SHARED if isinstance(t, int) and t == 1 else None, 0)
            x_turn(G1, 0)
            shared_step(0, 0)
            shared_step(1, 1)
            count_slots(3, OH[:, 0].rearrange("p j e -> p (j e)"), (bank[7][:, 0:NT * E], bank[7][:, NT * E:2 * NT * E]))
            run_steps(pe, shared_step, 2, 2, GS, GS)

            def routed_step(t, par):
                g, n = M2 + t, SHARED + 1 + t
                if below(t, G2 - 1):
                    x_turn(g + 1, 1 - par)
                first_product(g, par, n, 1 - par)
                second_product(g - 1, 1 - par, n - 1 if known(t, 1) else None, par)
            run_steps(pe, routed_step, 0, 2, G2 - 1 - (G2 - 1) % 2, G2)
            second_product(M2 + G2 - 1, (G2 - 1) % 2, SHARED + G2, G2 % 2)

        @block.scalar
        def _(act):
            A_ = nc.scalar.activation
            act.wait_ge(kv_ps, 1)
            act.wait_ge(kb_zero, 2)
            for q in range(NQ):
                v = bank[4 + q][:, 0:B * NCTX].rearrange("p (b n) -> p b n", b=B)
                o = 28 * q
                A_(VB[0:DH, :, q, o + 1:o + NK], v[0:DH], ACT.Copy)
                A_(VB[DH:P, :, q, o + NK + 1:o + 2 * NK], v[DH:P], ACT.Copy)
                A_(VB[0:DH, :, q, o], nullc[0:DH, 1:2].broadcast_to([DH, B]), ACT.Copy)
                last = A_(VB[DH:P, :, q, o + NK], nullc[DH:P, 1:2].broadcast_to([DH, B]), ACT.Copy)
            last.then_inc(v_ev, 1)
            for n in range(B * 3):
                b, c = n // 3, 2 * (n % 3)
                w = min(2, PC - c)
                act.wait_ge(vw_ps, n + 1)
                A_(VW[:, b, c:c + w, :].rearrange("p c d -> p (c d)"), bank[4 + n % 4][:, 0:w * D], ACT.Copy).then_inc(vw_ev, 1)

            act.wait_ge(consts, NCONST)
            act.dma_start(acc1[T:T + SPARE, :].rearrange("(h p) d -> p h d", p=P), fill[:, :, 0:D]).then_inc(filled[0], 16)
            act.dma_start(out[T:T + SPARE, :].rearrange("(h p) d -> p h d", p=P), fill[:, :, 0:D]).then_inc(filled[0], 16)

            def empty_slots(m, dram, tiles, c):
                n = min(FILL, tiles - c * FILL)
                for h in range(2 if n > 0 else 0):
                    act.dma_start(dram[c * FILL * R:(c * FILL + n) * R, :].rearrange("(n h p) c -> h p n c", h=2, p=P)[h],
                                  fill[:, h, :].unsqueeze(1).broadcast_to([P, n, RW])).then_inc(filled[m], 16)

            def att_step(s, par):
                A, Bs, C = known(s, 0) and below(s, NP_), known(s, 2) and below(s, NP_ + 2), known(s, 3) and below(s, NP_ + 3)
                G = known(s, 4)

                if isinstance(s, int) and s < 6:
                    empty_slots(0, xs1, G1, s + 1)
                elif isinstance(s, int):
                    empty_slots(1, xs2, G2, s - 12)

                def prob_t(u):
                    act.wait_ge(probT_ps, 2 * (s - 2) + u + 1)
                    A_(pT[u][:, 0:4, :].rearrange("p c n -> p (c n)"), bank[3][:], ACT.Copy)
                    A_(pT[u][:, 4, :], bank[4][:, 0:P], ACT.Copy).then_inc(probT_ready, 1)

                def exps(u):
                    act.wait_ge(sub_ready, 2 * s + u + 1)
                    A_(score[par][u][:, 0:SK], score[par][u][:, 0:SK], ACT.Exp).then_inc(exp_ready, 1)

                if Bs:
                    prob_t(0)
                if G:
                    act.wait_ge(aT_ps, s - 3)
                    if known(s, 5):
                        act.wait_ge(gate_ps, s - 4)
                    A_(aT[:].rearrange("p u k n -> p (u k n)"), bank[6][:], ACT.Copy).then_inc(aT_ready, 1)
                if Bs:
                    prob_t(1)
                if A:
                    exps(0)
                if C:
                    act.wait_ge(rstd_ready, s - 2)
                    for u in range(2):
                        last = A_(z[1 - par][:, u, :], z[1 - par][:, u, :], ACT.Tanh, scale=rstd[:, u:u + 1])
                    last.then_inc(tanh_ready, 1)
                if below(s, NP_ - 1):
                    act.wait_ge(textT_ps, s + 2)
                    A_(tT[:].rearrange("p u k n -> p (u k n)"), bank[0][:], ACT.Copy).then_inc(textT_ready, 1)
                if A:
                    exps(1)
            def route_exp(n, logits):
                act.wait_ge(rt_sub, n)
                A_(logits, logits, ACT.Exp).then_inc(rt_exp, 1)

            run_steps(act, att_step, -1, 6, 12, 12)
            route_exp(1, RA[:, 0:HT, :])
            run_steps(act, att_step, 12, 12, 14, NP_ + 4)

            route_exp(2, RA[:, HT:NT, :])

            def x_high(g, par):
                act.wait_ge(xT_ps, g + 1)
                if known(g, 2):
                    act.wait_ge(h_ps, 4 * (g - 1))
                A_(x_h[par][:].rearrange("p k r -> p (k r)"), bank[0][:], ACT.Copy).then_inc(xT_ready, 1)

            def w_part(n, q, wb):
                act.wait_ge((w1_in, w2_in)[q // 2], 16 * (n + 1))
                A_(w_h[wb][:, q, :], raw[:, q, :], ACT.Copy).then_inc(w_high[q // 2], 1)

            def pair_of(buf, par, j):
                return buf[par][:, 2 * j:2 * j + 2, :].rearrange("p c r -> p (c r)")

            for i in range(2):
                act.wait_ge(a_kept[i], 32 * NP_ // 2)
            for q in range(4):
                w_part(0, q, 0)
            x_high(0, 0)

            def moe1_sets(i):
                for k in range(4):
                    g, n = 4 * i + k, 2 * i + k // 2
                    if below(g, G1 - 1):
                        x_high(g + 1, (k + 1) % 2)
                    if known(g, 2):
                        act.wait_ge(y_ps, g - 1)
                    for j in range(FC // 2):
                        act.wait_ge(h_ps, 4 * g + j + 1)
                        A_(pair_of(h_h, k % 2, j), bank[1 + j][:], ACT.Relu).then_inc(h_ready, 1)
                    for q in (2 * (k % 2), 2 * (k % 2) + 1):
                        w_part(n + 1, q, 1 - k // 2)
            moe1_sets(0)
            with act.Fori(1, E - 1) as i:
                moe1_sets(i)
            moe1_sets(E - 1)

            def x2_tanh(b):
                act.wait_ge(acc_in[b], 16)
                A_(AR[:, b * TPB:(b + 1) * TPB, 0:D], AR[:, b * TPB:(b + 1) * TPB, 0:D], ACT.Tanh).then_inc(c_tanh, 1)

            def x2_logits(s):
                act.wait_ge(cg_ps, s + 1)
                A_(LG[:, ds(2 * s, 2), :], bank[7][:, 0:2 * E].rearrange("p (u e) -> p u e", u=2), ACT.Copy).then_inc(cg_ready, 1)

            def x2_step(s, par):
                act.wait_ge(cT_ps, s + 1)
                A_(xnT[par][:].rearrange("p u k n -> p (u k n)"), bank[0 if par == 0 else 6][:], ACT.Copy).then_inc(cT_ready, 1)
                if known(s, 1):
                    x2_logits(s - 1)
            x2_tanh(0)
            for b in range(B):
                if b < B - 1:
                    x2_tanh(b + 1)
                first = b * TPB // 2
                run_steps(act, x2_step, first, max(first, 2), first + TPB // 2, first + TPB // 2)
            x2_logits(NP_ - 1)
            route_exp(3, RA[:])

            def hidden(g, par, bias):
                act.wait_ge(y_ps, g - 1)
                for j in range(FC // 2 + 1):
                    if j < FC // 2:
                        act.wait_ge(h_ps, 4 * g + j + 1)
                        act.wait_ge(h_low, 4 * g - 3 + j)
                        for c in (2 * j, 2 * j + 1):
                            last = A_(gel[:, j, (c % 2) * R:(c % 2 + 1) * R], bank[1 + j][:, (c % 2) * R:(c % 2 + 1) * R],
                                      ACT.Gelu, bias=bias[:, c:c + 1])
                        last.then_inc(gelu_done, 1)
                    if j:
                        act.wait_ge(gelu_done, 4 * (g - G1) + j)
                        A_(pair_of(h_h, par, j - 1), gel[:, j - 1, :], ACT.Copy).then_inc(h_ready, 1)

            def shared_step(t, par):
                x_high(G1 + t + 1, 1 - par)
                hidden(G1 + t, par, sb1)
            x_high(G1, 0)
            run_steps(act, shared_step, 0, 2, GS, GS)
            for q in range(2):
                w_part(SHARED + 1, q, 1)

            def routed_step(t, par):
                g, n = M2 + t, SHARED + 1 + t
                if below(t, G2 - 1):
                    x_high(g + 1, 1 - par)
                act.wait_ge(b1_in[par], 16 * (t // 2 + 1))
                hidden(g, par, b1b[par])
                if below(t, G2 - 1):
                    for q in (0, 1):
                        w_part(n + 1, q, par)
                for q in (2, 3):
                    w_part(n, q, 1 - par)
            run_steps(act, routed_step, 0, 2, G2 - 1 - (G2 - 1) % 2, G2)

        @block.vector
        def _(v):
            ve = nc.vector
            chain = Chain(v, dve_self)
            link = chain.link
            scratch = cell_v
            link(ve.memset(cell_v[:], 0.0))

            def rsqrt(r, x, t):
                link(ve.tensor_scalar(t.bitcast(I32), x.bitcast(I32), 1, None, ALU.logical_shift_right))
                link(ve.tensor_scalar(r.bitcast(I32), t.bitcast(I32), -1.0, RSQRT_SEED, ALU.mult, ALU.add))
                for k in range(3):
                    link(ve.scalar_tensor_tensor(t, r, -0.5, r, ALU.mult, ALU.mult))
                    link(ve.tensor_tensor(t, t, x, ALU.mult))
                    link(ve.scalar_tensor_tensor(r, t, 1.5, r, ALU.add, ALU.mult))

            mean, r1, rsc, t_a, t_b, t_c, t_d = (ln[:, i, :] for i in range(7))

            def row_stats(t, n):
                mean, _, _, t_a, t_b, t_c, _ = (ln[:, i, t:t + n] for i in range(7))
                m_e, v_e, m_o, v_o = (rows6[:, t:t + n, i] for i in (1, 2, 4, 5))
                link(ve.tensor_tensor(t_a, m_e, m_o, ALU.subtract))
                link(ve.tensor_tensor(t_b, m_e, m_o, ALU.add))
                link(ve.tensor_scalar(mean, t_b, 0.5, None, ALU.mult))
                link(ve.scalar_tensor_tensor(t_b, t_a, 0.25, t_a, ALU.mult, ALU.mult))
                link(ve.tensor_tensor(t_c, v_e, v_o, ALU.add))
                link(ve.scalar_tensor_tensor(t_a, t_c, 1.0 / D, t_b, ALU.mult, ALU.add))

            def row(rows, t):
                return rows[:, ds(t, 1), :].rearrange("p o d -> p (o d)")

            def normed(t, dst, src):
                return ve.tensor_scalar(dst, src, ln[:, 0, ds(t, 1)], ln[:, 1, ds(t, 1)], ALU.subtract, ALU.mult)

            v.wait_ge(par_in, 16 * NPAR)
            v.wait_ge(kb_zero, 2)
            link(ve.memset(maskb[:], 0.0))
            ve.tensor_scalar(maskb[:, :, 1:NK], mask8[:].rearrange("p (b n) -> p b n", b=B), FMAX, -FMAX, ALU.mult,
                             ALU.add).then_inc(maskb_ready, 1)
            v.wait_ge(kv_ps, 1)
            for q in range(NQ):
                k = bank[q][:, 0:B * NCTX].rearrange("p (b n) -> p b n", b=B)
                ve.tensor_copy(KB[0:DH, :, q, 1:NK], k[0:DH])
                ve.tensor_copy(KB[DH:P, :, q, NK + 1:2 * NK], k[DH:P])
                ve.tensor_copy(KB[0:DH, :, q, 0], nullc[0:DH, 0:1].broadcast_to([DH, B]))
                last = ve.tensor_copy(KB[DH:P, :, q, NK], nullc[DH:P, 0:1].broadcast_to([DH, B]))
            last.then_inc(k_ev, 1)
            v.wait_ge(x_in, 16 * B)
            for n in range(B * KC):
                for t in range(NT // 8 * n, NT // 8 * (n + 1)):
                    last = ve.bn_stats(rows6[:, t, :], X[:, t, :])
                b, k = n // KC, n % KC
                v.wait_ge(m_ps, n + 1)
                for half in range(2):
                    last = ve.tensor_scalar(MQ[:, b, k, half * SK // 2:(half + 1) * SK // 2],
                                            bank[2 * (n % 2) + half][:, 0:SK // 2], gcol[:, k:k + 1], float(DH) ** -0.5,
                                            ALU.mult, ALU.mult)
                last.then_inc(m_ev, 1)
            v.wait_ge(m_ev, B * KC)
            row_stats(0, NT)
            link(ve.tensor_scalar(t_b, t_a, EPS, None, ALU.add))
            rsqrt(r1, t_b, t_c)
            link(ve.tensor_scalar(t_a, t_a, 1.0 + EPS, EPS * EPS, ALU.mult, ALU.add))
            rsqrt(t_d, t_a, t_c)
            link(ve.tensor_tensor(t_a, r1, t_d, ALU.mult))
            link(ve.tensor_tensor(rsc, t_a, t_b, ALU.mult))
            v.wait_ge(vw_ps, B * 3)
            for i in range(2):
                for u in range(2):
                    link(ve.memset(score[i][u][:, SK:PK], 0.0))

            def bc(a):
                return a.unsqueeze(2).broadcast_to([P, a.shape[1], E])

            def te(a, n):
                return a.unsqueeze(1).broadcast_to([P, n, E])

            mx, sm, g1, g2, ix, den, w1, w2, p1, p2, k1, k2, t0, t1 = range(14)

            def col(i, at):
                return v32[:, i, at]

            def top(at, n, g, hot):
                link(ve.tensor_reduce(col(g, at), RA[:, at, :], AX.X, ALU.max))
                link(ve.tensor_tensor(RT[:, at, :], RA[:, at, :], bc(col(g, at)), ALU.is_equal))
                link(ve.tensor_tensor(RT[:, at, :], RT[:, at, :], te(iota_e8[:], n), ALU.mult))
                link(ve.tensor_reduce(col(ix, at), RT[:, at, :], AX.X, ALU.min))
                link(ve.tensor_tensor(hot, te(iota_e8[:], n), bc(col(ix, at)), ALU.is_equal))

            def softmax_start(at):
                link(ve.tensor_reduce(col(mx, at), LG[:, at, :], AX.X, ALU.max))
                ve.tensor_tensor(RA[:, at, :], LG[:, at, :], bc(col(mx, at)), ALU.subtract).then_inc(rt_sub, 1)

            def softmax_end(at, n):
                v.wait_ge(rt_exp, n)
                link(ve.tensor_reduce(col(sm, at), RA[:, at, :], AX.X, ALU.add))
                link(ve.reciprocal(col(t0, at), col(sm, at)))
                link(ve.tensor_tensor(RA[:, at, :], RA[:, at, :], bc(col(t0, at)), ALU.mult))

            def gate_weights(at, eps):
                link(ve.scalar_tensor_tensor(col(den, at), col(g1, at), eps, col(g2, at), ALU.add, ALU.add))
                link(ve.reciprocal(col(t0, at), col(den, at)))
                link(ve.tensor_tensor(col(w1, at), col(g1, at), col(t0, at), ALU.mult))
                link(ve.tensor_tensor(col(w2, at), col(g2, at), col(t0, at), ALU.mult))

            def combine_weights(at, hot1, hot2):
                link(ve.tensor_tensor(RT[:, at, :], hot1, bc(col(w1, at)), ALU.mult))
                link(ve.tensor_tensor(RB[:, at, :], hot2, bc(col(w2, at)), ALU.mult))
                link(ve.tensor_tensor(AR[:, at, D:D + E], RT[:, at, :], RB[:, at, :], ALU.add))

            def pick(at, dst, hot, src):
                link(ve.tensor_tensor(RT[:, at, :], hot, src, ALU.mult))
                link(ve.tensor_reduce(col(dst, at), RT[:, at, :], AX.X, ALU.add))

            HB = B // 2
            every = slice(0, NT)

            def half_of(half):
                return slice(half * HT, (half + 1) * HT), OH1[:, half, 0], OH1[:, half, 1]

            def by_batch(a):
                return a.rearrange("p (b j) e -> p b j e", b=HB)

            def route_choices(half):
                at, hot1, hot2 = half_of(half)
                softmax_end(at, half + 1)
                top(at, HT, g1, hot1)
                link(ve.tensor_scalar(RT[:, at, :], hot1, -1.0, 1.0, ALU.mult, ALU.add))
                link(ve.tensor_tensor(RA[:, at, :], RA[:, at, :], RT[:, at, :], ALU.mult))
                top(at, HT, g2, hot2)
                gate_weights(at, 1e-9)
                link(ve.tensor_scalar(col(t0, at), col(w2, at), 1.0 / THRESH, None, ALU.mult))
                link(ve.tensor_tensor(col(t0, at), prob[:, at], col(t0, at), ALU.is_lt))
                ve.tensor_tensor(hot2, hot2, bc(col(t0, at)), ALU.mult).then_inc(rt_hot, 1)

            def route_positions(half, before, totals):
                at, hot1, hot2 = half_of(half)
                tot, scan, pos = (a[:].rearrange("p a b c -> p (a b c)")[:, 0:2 * HT * E] for a in (TO, SCN, POS))
                kej = dict(k=2, e=E)
                v.wait_ge(rt_pos, half + 1)
                link(ve.tensor_copy(tot.rearrange("p (k e j) -> p k e j", **kej), totals.rearrange("p (k j e) -> p k e j", **kej)))
                link(ve.tensor_tensor_scan(scan, seg1[:], tot, 0.0, ALU.mult, ALU.add))
                link(ve.tensor_scalar(m1c[:], scan.rearrange("p (k e j) -> p k e j", **kej)[:, 0]
                                      .rearrange("p e (b j) -> p b e j", b=HB)[:, :, :, TPB - 1], float(CAP), None, ALU.min))
                link(ve.tensor_tensor(scan, scan, tot, ALU.subtract))
                pos = pos.rearrange("p (k j e) -> p k j e", **kej)
                link(ve.tensor_tensor(pos, before.rearrange("p (k j e) -> p k j e", **kej),
                                      scan.rearrange("p (k e j) -> p k j e", **kej), ALU.add))
                ve.tensor_copy(cell_v[:, 0:1], ones[:, 0:1]).then_inc(rt_taken, 1)
                link(ve.tensor_tensor(by_batch(pos[:, 1]), by_batch(pos[:, 1]),
                                      m1c[:].unsqueeze(2).broadcast_to([P, HB, TPB, E]), ALU.add))
                pick(at, p1, hot1, pos[:, 0])
                pick(at, p2, hot2, pos[:, 1])

            def route_slots(half):
                at, hot1, hot2 = half_of(half)
                P1, P2, K1, K2, W1, W2, T0, T1 = (col(i, at) for i in (p1, p2, k1, k2, w1, w2, t0, t1))
                link(ve.tensor_scalar(K1, P1, float(CAP), None, ALU.is_lt))
                link(ve.tensor_reduce(T1, hot2, AX.X, ALU.add))
                link(ve.scalar_tensor_tensor(K2, P2, float(CAP), T1, ALU.is_lt, ALU.mult))
                link(ve.scalar_tensor_tensor(K2, W2, 0.0, K2, ALU.is_gt, ALU.mult))
                link(ve.tensor_tensor(W1, W1, K1, ALU.mult))
                link(ve.tensor_tensor(W2, W2, K2, ALU.mult))
                combine_weights(at, hot1, hot2)
                for k, (hot, p, kept) in enumerate(((hot1, P1, K1), (hot2, P2, K2))):
                    spare = spare_row[:, k, at]
                    link(ve.tensor_tensor(by_batch(RT[:, at, :]), by_batch(hot),
                                          first_slot[:, half * HB:(half + 1) * HB, :].unsqueeze(2).broadcast_to([P, HB, TPB, E]),
                                          ALU.mult))
                    link(ve.tensor_reduce(T0, RT[:, at, :], AX.X, ALU.add))
                    link(ve.tensor_tensor(T0, T0, p, ALU.add))
                    link(ve.tensor_tensor(T0, T0, spare, ALU.subtract))
                    link(ve.tensor_tensor(T0, T0, kept, ALU.mult))
                    link(ve.tensor_tensor(slot[k][:, at], T0, spare, ALU.add))
                ve.tensor_copy(T1, T0).then_inc(rt_done, 1)

            def att_step(s, par):
                A, L = known(s, 0) and below(s, NP_), below(s, NP_ - 1)
                M = known(s, 1) and below(s, NP_ + 1)
                C, G = known(s, 3) and below(s, NP_ + 3), known(s, 4)

                def mask_and_max(u):
                    v.wait_ge(score_ps, 2 * s + u + 1)
                    if known(s, 2):
                        v.wait_ge(probT_ps, 2 * (s - 2) + u + 1)
                    sc = score[par][u]
                    for half in range(2):
                        c = slice(half * SK // 2, (half + 1) * SK // 2)
                        last = ve.scalar_tensor_tensor(
                            sc[:, c].rearrange("p (h n) -> p h n", n=NK),
                            bank[1 + half][:, 0:SK // 2].rearrange("p (h n) -> p h n", n=NK), ln[:, 2, ds(2 * s + u, 1)],
                            maskb[:, ds(s // 4, 1), :].broadcast_to([P, H // 2, NK]), ALU.mult, ALU.add)
                    last.then_inc(score_ready, 1)
                    v.wait_ge(score_ready, 2 * s + u + 1)
                    ve.tensor_reduce(smax[par][u][:], sc[:, 0:SK].rearrange("p (h n) -> p h n", n=NK), AX.X,
                                     ALU.max).then_inc(max_ready, 1)

                def sums(u):
                    v.wait_ge(exp_ready, 2 * s - 1 + u)
                    link(ve.tensor_reduce(ssum[u][:], score[1 - par][u][:, 0:SK].rearrange("p (h n) -> p h n", n=NK), AX.X,
                                          ALU.add))
                    if known(s, 2):
                        v.wait_ge(prob_ready, 2 * s - 3 + u)
                    ve.reciprocal(srec[u][:], ssum[u][:]).then_inc(rec_ready, 1)

                if C:
                    wait_apart(v, scratch, att_ps, s - 2)
                    for u in range(2):
                        last = ve.bn_stats(st6[:, u, :], bank[5][:, u * D:(u + 1) * D])
                    link(last, scratch)
                    for u in range(2):
                        last = ve.bn_aggr(mv_out[:, u, :], st6[:, u, :])
                    link(last)
                    if known(s, 5):
                        v.wait_ge(a_ready, s - 4)
                    for u in range(2):
                        last = ve.scalar_tensor_tensor(z[1 - par][:, u, :], bank[5][:, u * D:(u + 1) * D], mv_out[:, u, 0:1],
                                                       ogam[:], ALU.subtract, ALU.mult)
                    last.then_inc(z_ready, 1)
                if M:
                    sums(0)
                if A:
                    mask_and_max(0)
                if M:
                    sums(1)
                if L:
                    if known(s, 1):
                        v.wait_ge(textT_ps, s)
                        v.wait_ge(text_kept[1 - par], 16 * ((s - 1) // 2 + 1))
                    for u in range(2):
                        last = normed(2 * s + 2 + u, text[1 - par][:, u, :], row(X, 2 * s + 2 + u))
                    last.then_inc(text_ready, 1)
                if C:
                    link(ve.tensor_scalar(var[:], mv_out[:, :, 1], EPS, None, ALU.add))
                    if known(s, 4):
                        v.wait_ge(tanh_ready, s - 3)
                    rsqrt(rstd[:], var[:], nwt[:])
                    ve.tensor_copy(nwt[:], rstd[:]).then_inc(rstd_ready, 1)
                if A:
                    mask_and_max(1)
                if G:
                    v.wait_ge(gate_ps, s - 3)
                    ve.tensor_copy(LG[:, ds(2 * s - 8, 2), :], bank[7][:, 0:2 * E].rearrange("p (u e) -> p u e", u=2))\
                      .then_inc(gate_ready, 1)
            run_steps(v, att_step, -1, 6, 12, 12, chain, 2 * 16)
            v.wait_ge(gate_ready, NP_ // 2)
            softmax_start(slice(0, HT))
            att_step(12, 0)
            route_choices(0)
            att_step(13, 1)
            route_positions(0, bank[7][:, 0:2 * HT * E], bank[7][:, 2 * HT * E:4 * HT * E])
            att_step(14, 0)
            route_slots(0)
            run_steps(v, att_step, 15, 16, 16, NP_ + 4)
            v.wait_ge(gate_ready, NP_)
            softmax_start(slice(HT, NT))
            route_choices(1)


            def scale_out(g, par, free, metas, w):
                v.wait_ge(y_ps, g + 1)
                free()
                v.wait_ge(meta_in[par], metas)
                for u in range(2):
                    last = ve.tensor_scalar(y[par][:, u, :], bank[5 + par][:, u * D:(u + 1) * D], w(u), None, ALU.mult)
                last.then_inc(y_ready, 1)

            def moe1_out(g, k, e):
                par = k % 2

                def free():
                    if known(g, 2):
                        v.wait_ge(added1, 32 * (g - 1))
                scale_out(g, par, free, 16 * (g // 2 + 1), lambda u: meta[par][:, u, ds(e, 1)])

            def w_rest(n, q, wb):
                v.wait_ge(w_high[q // 2], 2 * n + q % 2 + 1)
                ve.tensor_tensor(w_l[wb][:, q, :], raw[:, q, :], w_h[wb][:, q, :].bitcast(F32), ALU.subtract)\
                  .then_inc(w_low[q // 2], 1)

            def x_rest(g, par):
                v.wait_ge(xT_ready, g + 1)
                ve.tensor_tensor(x_l[par][:].rearrange("p k r -> p (k r)"), bank[0][:],
                                 x_h[par][:].rearrange("p k r -> p (k r)").bitcast(F32), ALU.subtract).then_inc(x_low, 1)

            def pair_of(buf, par, j):
                return buf[par][:, 2 * j:2 * j + 2, :].rearrange("p c r -> p (c r)")

            for i in range(2):
                v.wait_ge(a_kept[i], 32 * NP_ // 2)
            for q in range(4):
                w_rest(0, q, 0)
            x_rest(0, 0)

            def moe1_rest(i, k, half):
                g, n = 4 * i + k, 2 * i + k // 2
                if below(g, G1 - 1):
                    x_rest(g + 1, (k + 1) % 2)
                for j in range(FC // 2):
                    v.wait_ge(h_ready, 4 * g + j + 1)
                    ve.scalar_tensor_tensor(pair_of(h_l, k % 2, j), bank[1 + j][:], 0.0,
                                            pair_of(h_h, k % 2, j).bitcast(F32), ALU.max, ALU.subtract).then_inc(h_low, 1)
                for q in (2 * (k % 2), 2 * (k % 2) + 1):
                    w_rest(n + 1, q, 1 - k // 2)
                if known(g, 1):
                    e = n - (1 - k % 2) - E * half
                    moe1_out(g - 1, (k - 1) % 2, e)
            moe1_rest(0, 0, 0)
            route_positions(1, bank[7][:, 0:2 * HT * E], bank[7][:, 2 * HT * E:4 * HT * E])
            moe1_rest(0, 1, 0)
            route_slots(1)
            moe1_rest(0, 2, 0)
            moe1_rest(0, 3, 0)

            def moe1_sets(i, half):
                for k in range(4):
                    moe1_rest(i, k, half)
            with v.Fori(1, E // 2) as i:
                moe1_sets(i, 0)
            moe1_rest(E // 2, 0, 0)
            for k in range(1, 4):
                moe1_rest(E // 2, k, 1)
            with v.Fori(E // 2 + 1, E - 1) as i:
                moe1_sets(i, 1)
            moe1_sets(E - 1, 1)
            moe1_out(G1 - 1, 1, E - 1)

            def x2_batch(b):
                at = slice(b * TPB, (b + 1) * TPB)
                v.wait_ge(c_tanh, b + 1)
                v.wait_ge(x2_in[b], 16)
                link(ve.tensor_tensor(x2[b % 2], x2[b % 2], AR[:, at, 0:D], ALU.add))
                for t in range(TPB):
                    last = ve.bn_stats(rows6[:, b * TPB + t, :], x2[b % 2][:, t, :])
                link(last)
                row_stats(b * TPB, TPB)
                link(ve.tensor_scalar(t_b[:, at], t_a[:, at], EPS, None, ALU.add))
                rsqrt(r1[:, at], t_b[:, at], t_c[:, at])

            for b in range(B):
                x2_batch(b)
                for k in range(4):
                    if b:
                        v.wait_ge(cT_ps, 4 * (b - 1) + k + 1)
                        v.wait_ge(xn_out[k], 32 * b)
                    for u in range(2):
                        last = normed(8 * b + 2 * k + u, xn[k][:, u, :], x2[b % 2][:, 2 * k + u, :])
                    last.then_inc(c_norm, 1)
            v.wait_ge(cg_ready, NP_)

            def gelu_rest(g, par):
                for j in range(FC // 2):
                    v.wait_ge(h_ready, 4 * g + j + 1)
                    ve.tensor_tensor(pair_of(h_l, par, j), gel[:, j, :], pair_of(h_h, par, j).bitcast(F32),
                                     ALU.subtract).then_inc(h_low, 1)

            def shared_rest(t, par):
                x_rest(G1 + t + 1, 1 - par)
                gelu_rest(G1 + t, par)

            hot1, hot2 = OH[:, 0], OH[:, 1]
            softmax_start(every)
            softmax_end(every, 3)
            x_rest(G1, 0)
            top(every, NT, g1, hot1)
            shared_rest(0, 0)
            link(ve.scalar_tensor_tensor(RA[:], hot1, -2.0, RA[:], ALU.mult, ALU.add))
            top(every, NT, g2, hot2)
            gate_weights(every, 0.0)
            combine_weights(every, hot1, hot2)
            link(ve.tensor_copy(POS[:, 1], hot1))
            ve.tensor_tensor(OH[:, 0], OH[:, 0], OH[:, 1], ALU.add).then_inc(rt_hot, 1)
            both, hot1 = OH[:, 0], POS[:, 1]

            def shared_out_step(t, par):
                v.wait_ge(y_ps, G1 + t + 1)
                v.wait_ge(y_in[par], 16 * (t // 2 + 1))
                ve.tensor_tensor(y[par][:], bank[5 + par][:].rearrange("p (u d) -> p u d", u=2), y[par][:],
                                 ALU.add).then_inc(y_ready, 1)

            shared_rest(1, 1)
            shared_out_step(0, 0)
            v.wait_ge(rt_pos, 3)
            tot, pos = TO[:, 0], bank[7][:, 0:NT * E].rearrange("p (j e) -> p j e", e=E)
            link(ve.tensor_copy(tot, bank[7][:, NT * E:2 * NT * E].rearrange("p (j e) -> p e j", e=E)))
            link(ve.memset(TO[:, 1], 1.0))
            link(ve.memset(TO[:, 1, :, 0:1], 0.0))
            link(ve.tensor_tensor_scan(SCN[:, 0].rearrange("p e j -> p (e j)"), TO[:, 1].rearrange("p e j -> p (e j)"),
                                       tot.rearrange("p e j -> p (e j)"), 0.0, ALU.mult, ALU.add))
            count, tiles, end, start, off = (e8[:, i, :] for i in range(5))
            link(ve.tensor_copy(count, SCN[:, 0, :, NT - 1]))
            link(ve.tensor_tensor(SCN[:, 0], SCN[:, 0], tot, ALU.subtract))
            link(ve.tensor_tensor(POS[:, 0], pos, SCN[:, 0].rearrange("p e j -> p j e"), ALU.add))
            shared_rest(2, 0)
            shared_out_step(1, 1)
            link(ve.tensor_tensor(cmp, iota_256k[:].unsqueeze(1).broadcast_to([P, E, NT // 2]),
                                  count.unsqueeze(2).broadcast_to([P, E, NT // 2]), ALU.is_lt))
            link(ve.tensor_reduce(tiles, cmp, AX.X, ALU.add))
            link(ve.tensor_tensor_scan(end, ones[:, 0:E], tiles, 0.0, ALU.mult, ALU.add))
            link(ve.tensor_tensor(start, end, tiles, ALU.subtract))
            link(ve.tensor_scalar(off, start, float(R), None, ALU.mult))
            link(ve.tensor_tensor(POS[:, 0], POS[:, 0], te(off, NT), ALU.add))
            pick(every, p1, hot1, POS[:, 0])
            pick(every, p2, hot2, POS[:, 0])
            link(ve.tensor_copy(slot[0][:], col(p1, every)))
            link(ve.tensor_copy(slot[1][:], col(p2, every)))
            shared_rest(3, 1)
            shared_out_step(2, 0)
            it = iota_t[:].unsqueeze(2).broadcast_to([P, G2, E])
            link(ve.tensor_tensor(OHT[:], it, start.unsqueeze(1).broadcast_to([P, G2, E]), ALU.is_ge))
            link(ve.tensor_tensor(oht2, it, end.unsqueeze(1).broadcast_to([P, G2, E]), ALU.is_lt))
            link(ve.tensor_tensor(OHT[:], OHT[:], oht2, ALU.mult))
            link(ve.tensor_tensor(oht2, OHT[:], iota_e[:].unsqueeze(1).broadcast_to([P, G2, E]), ALU.mult))
            link(ve.tensor_reduce(eidf[:], oht2, AX.X, ALU.add))
            ve.tensor_copy(eid[:], eidf[:]).then_inc(rt_done, 1)

            def shared_step(t, par):
                shared_rest(t, par)
                shared_out_step(t - 1, 1 - par)
            run_steps(v, shared_step, 4, 4, GS, GS)
            for q in range(2):
                w_rest(SHARED + 1, q, 1)

            def routed_out(t, par):
                g = M2 + t
                v.wait_ge(meta_in[par], 16 * (G1 // 2 + t // 2 + 1))
                link(ve.tensor_tensor(wsel[:], meta[par][:, :, 0:E], OHT[:, ds(t, 1), :].broadcast_to([P, 2, E]), ALU.mult))
                link(ve.tensor_reduce(wv[:], wsel[:], AX.X, ALU.add))
                v.wait_ge(y_ps, g + 1)
                v.wait_ge(b2_in[par], 16 * (t // 2 + 1))
                link(ve.tensor_tensor(yb[:], bank[5 + par][:].rearrange("p (u d) -> p u d", u=2),
                                      b2b[par][:].unsqueeze(1).broadcast_to([P, 2, D]), ALU.add))
                if known(t, 2):
                    v.wait_ge(added2, 32 * (t - 1))
                else:
                    v.wait_ge(shared_out[par], 16 * GS // 2)
                for u in range(2):
                    last = ve.tensor_scalar(y[par][:, u, :], yb[:, u, :], wv[:, u:u + 1], None, ALU.mult)
                last.then_inc(y_ready, 1)

            def routed_step(t, par):
                g, n = M2 + t, SHARED + 1 + t
                if below(t, G2 - 1):
                    x_rest(g + 1, 1 - par)
                gelu_rest(g, par)
                if below(t, G2 - 1):
                    for q in (0, 1):
                        w_rest(n + 1, q, par)
                for q in (2, 3):
                    w_rest(n, q, 1 - par)
                if known(t, 1):
                    routed_out(t - 1, 1 - par)
                else:
                    shared_out_step(GS - 1, 1)
            run_steps(v, routed_step, 0, 4, G2 - 1 - (G2 - 1) % 2, G2, chain, 2 * 3)
            routed_out(G2 - 1, (G2 - 1) % 2)

        @block.gpsimd
        def _(pool):
            po = nc.gpsimd
            tiles_done = pool.alloc_register("tiles_done")
            po.memset(area[:, 0:2496], 0.0).then_inc(kb_zero, 1)
            po.memset(area[:, 2496:6592], 0.0).then_inc(kb_zero, 1)
            n = [0]

            def const(ins, wait=False):
                ins.then_inc(consts, 1)
                n[0] += 1
                if wait:
                    pool.wait_ge(consts, n[0])

            def iota(dst, pattern, base=0, mult=0, wait=False):
                const(po.iota(dst, pattern, base=base, channel_multiplier=mult, allow_small_or_imprecise_dtypes=True), wait)

            const(po.memset(ident[:], 0.0))
            const(po.memset(upper[:], 1.0))
            const(po.memset(fill[:], 0.0), True)
            const(po.affine_select(out=ident[:], in_=ident[:], compare_op=ALU.not_equal, fill=1.0, base=0,
                                   pattern=[[-1, P]], channel_multiplier=1))
            const(po.affine_select(out=upper[:], in_=upper[:], compare_op=ALU.is_gt, fill=0.0, base=0,
                                   pattern=[[1, P]], channel_multiplier=-1))
            iota(fill[:, :, CID:CID + 1].rearrange("p h o -> p (h o)").bitcast(I32), [[P, 2]], base=T, mult=1)
            const(po.memset(ones[:], 1.0))
            iota(iota_e8[:], [[1, E]], base=-E)
            iota(iota_e[:], [[1, E]])
            iota(first_slot[:], [[CAP, B], [B * CAP, E]])
            iota(iota_256k[:], [[R, NT // 2]])
            iota(iota_t[:], [[1, G2]])
            assert n[0] == NCONST
            po.iota(spare_row[:], [[T, 2], [P, NT]], base=S1, channel_multiplier=1, allow_small_or_imprecise_dtypes=True)
            po.memset(AR[:, :, CID:RW], 0.0).then_inc(kb_zero, 1)
            po.memset(seg1[:], 1.0).then_inc(kb_zero, 1)
            pool.wait_ge(kb_zero, 4)
            po.memset(seg1[:].rearrange("p (s j) -> p s j", j=TPB)[:, :, 0:1], 0.0)
            po.iota(AR[:, :, CID:CID + 1].rearrange("p j o -> p (j o)").bitcast(I32), [[P, NT]], base=0, channel_multiplier=1)

            def att_step(s, par):
                A, M, C = below(s, NP_), known(s, 1) and below(s, NP_ + 1), known(s, 3)

                def heads(op, sc, col):
                    sc = sc[:, 0:SK].rearrange("p (h n) -> p h n", n=NK)
                    return po.tensor_tensor(sc, sc, col[:].unsqueeze(2).broadcast_to([P, H, NK]), op)
                for u in range(2):
                    if M:
                        pool.wait_ge(rec_ready, 2 * s - 1 + u)
                        heads(ALU.mult, score[1 - par][u], srec[u]).then_inc(prob_ready, 1)
                    if A:
                        pool.wait_ge(max_ready, 2 * s + u + 1)
                        heads(ALU.subtract, score[par][u], smax[par][u]).then_inc(sub_ready, 1)
                if C:
                    if known(s, 5):
                        pool.wait_ge(aT_ps, s - 4)
                        pool.wait_ge(a_kept[1 - par], 32 * ((s - 5) // 2 + 1))
                    pool.wait_ge(text_kept[1 - par], 16 * ((s - 3) // 2 + 1))
                    pool.wait_ge(tanh_ready, s - 2)
                    po.tensor_tensor(act_a[1 - par][:], z[1 - par][:], AR[:, ds(2 * s - 6, 2), 0:D], ALU.add).then_inc(a_ready, 1)
            def scatter_rows(dram, first, n, done):
                for j in range(first, first + n):
                    for k in range(2):
                        po.indirect_dma_start(dram, bass.IndirectOffsetOnAxis(ap=slot[k][:, j:j + 1], axis=0),
                                              AR[:, j, :], None).then_inc(done, 16)

            run_steps(pool, att_step, 0, 6, NP_, NP_ + 1)
            for i in range(2):
                pool.wait_ge(a_kept[i], 32 * HT // 4)
            pool.wait_ge(rt_done, 1)
            pool.wait_ge(filled[0], 16 * (2 + 2 * -(-G1 // FILL)))
            scatter_rows(xs1, 0, HT // 4, rows_out[0])
            att_step(NP_ + 1, 1)
            scatter_rows(xs1, HT // 4, HT // 4, rows_out[0])
            att_step(NP_ + 2, 0)
            scatter_rows(xs1, HT // 2, HT // 2, rows_out[0])

            def scatter_add(dram, par, done):
                for u in range(2):
                    po.indirect_dma_start(dram, bass.IndirectOffsetOnAxis(ap=meta[par][:, u, E:E + 1].bitcast(I32), axis=0),
                                          y[par][:, u, :], None, compute_op=ALU.add).then_inc(done, 16)

            def meta_load(dram, t, par):
                po.dma_start(meta[par][:], dram[ds(t * R, R), D:D + E + 1].rearrange("(h p) d -> p h d", p=P))\
                  .then_inc(meta_in[par], 16)

            def tile_step(n, dram, slots, sums, first, done):
                def step(t, par):
                    if known(t, 2):
                        pool.wait_ge(done, 32 * (t - 1))
                    if below(t, n):
                        meta_load(dram, slots(t, par), par)
                    if known(t, 1):
                        pool.reg_mov(tiles_done, first + t)
                        pool.wait_ge(rt_done, 1)
                        pool.wait_ge(y_ready, tiles_done)
                        scatter_add(sums, 1 - par, done)
                return step

            pool.wait_ge(rows_out[0], 16 * 2 * HT)
            for i in range(2):
                pool.wait_ge(a_kept[i], 32 * NP_ // 2)
            step = tile_step(G1, xs1, lambda t, par: slots_of(t, par, 0), acc1, 0, added1)
            step(0, 0)
            step(1, 1)
            pool.wait_ge(rt_done, 2)
            for t in range(2, 10):
                scatter_rows(xs1, HT + 2 * (t - 2), 2, rows_out[1])
                step(t, t % 2)
            run_steps(pool, step, 10, 10, G1 // 2, G1 // 2)
            pool.wait_ge(rows_out[1], 16 * 2 * HT)
            step = tile_step(G1, xs1, lambda t, par: slots_of(t, par, 1), acc1, 0, added1)
            run_steps(pool, step, G1 // 2, G1 // 2, G1, G1 + 1)
            pool.wait_ge(added1, 32 * G1)

            def x2_bias(s, b):
                pool.wait_ge(c_norm, s + 1)
                xp = x2[b % 2][:, ds(2 * s - b * TPB, 2), :]
                po.tensor_tensor(xp, xp, sb2[:].unsqueeze(1).broadcast_to([P, 2, D]), ALU.add).then_inc(c_bias, 1)
            for b in range(B):
                first = b * TPB // 2
                run_steps(pool, lambda s, par: x2_bias(s, b), first, first, first + TPB // 2, first + TPB // 2)
                pool.wait_ge(c_bias, first + TPB // 2)
                po.dma_start(x2b[b * N:(b + 1) * N, :].rearrange("(t p) d -> p t d", p=P), x2[b % 2]).then_inc(x2_kept[b], 16)
                if b < 2:
                    pool.wait_ge(x2_kept[b], 16)
                    po.dma_start(x2[b % 2], io["x"][(b + 2) * N:(b + 3) * N, :].rearrange("(t p) d -> p t d", p=P))\
                      .then_inc(x2_in[b + 2], 16)
            pool.wait_ge(rt_done, 3)
            pool.wait_ge(filled[1], 16 * 2 * -(-G2 // FILL))
            scatter_rows(xs2, 0, NT, rows_out2)
            pool.wait_ge(rows_out2, 16 * 2 * NT)
            for i in range(2):
                pool.wait_ge(shared_out[i], 16 * GS // 2)
            run_steps(pool, tile_step(G2, xs2, lambda t, par: t, out, M2, added2), 0, 2, G2 - G2 % 2, G2 + 1)


def kernel(x, ctx_1024, fside_BxS_0, mask_BxS2_bk0, L0_xattn_ln_gamma, L0_xattn_null_kv, L0_xattn_Wq, L0_xattn_Wkv,
           L0_xattn_Wo, L0_xattn_out_gamma, L0_xattn_w_gate, L0_xattn_w1, L0_xattn_w2, L0_ffn_gate_w, L0_ffn_W1,
           L0_ffn_b1, L0_ffn_W2, L0_ffn_b2, L0_ffn_sW1, L0_ffn_sb1, L0_ffn_sW2, L0_ffn_sb2):
    import numpy as np
    import concourse.bacc as bacc
    from concourse.bass_utils import run_bass_kernel_spmd

    def a(v):
        return np.asarray(v)

    def w1_rows(w):
        return a(w).reshape(-1, KC, P, F).transpose(0, 2, 1, 3).reshape(-1, P, KC * F)

    def w2_rows(w):
        return a(w).reshape(-1, FC, P, D).transpose(0, 2, 1, 3).reshape(-1, P, FC * D)

    data = {
        "x": a(x).reshape(T, D),
        "ctxT": a(ctx_1024).reshape(B * NCTX, D).T,
        "probs": a(fside_BxS_0).reshape(NT, P).T,
        "mask": a(mask_BxS2_bk0).reshape(B * NCTX),
        "ln_g": a(L0_xattn_ln_gamma).reshape(KC, P).T,
        "null": a(L0_xattn_null_kv).T,
        "WqT": a(L0_xattn_Wq).T,
        "Wkv": a(L0_xattn_Wkv),
        "Wo": a(L0_xattn_Wo),
        "out_g": a(L0_xattn_out_gamma),
        "wg1": a(L0_xattn_w_gate),
        "wg2": a(L0_ffn_gate_w).T,
        "W1a": w1_rows(L0_xattn_w1), "W2a": w2_rows(L0_xattn_w2),
        "W1b": w1_rows(L0_ffn_W1), "W2b": w2_rows(L0_ffn_W2),
        "sW1": w1_rows(L0_ffn_sW1), "sW2": w2_rows(L0_ffn_sW2),
        "b1": a(L0_ffn_b1).reshape(E, FC, P).transpose(0, 2, 1),
        "b2": a(L0_ffn_b2),
        "sb1": a(L0_ffn_sb1).reshape(FC, P).T,
        "sb2": a(L0_ffn_sb2),
    }
    nc = bacc.Bacc("TRN2", target_bir_lowering=False, num_devices=1)
    arrays, io = {}, {}
    for name, v in data.items():
        v = np.ascontiguousarray(v)
        arrays[f"in_{name}"] = v
        io[name] = nc.dram_tensor(f"in_{name}", v.shape, mybir.dt.from_np(v.dtype), kind="ExternalInput").ap()
    io["out"] = nc.dram_tensor("out_rows", (T + SPARE, D), F32, kind="ExternalOutput").ap()
    build(nc, io)
    r = run_bass_kernel_spmd(nc, [arrays], core_ids=[0])
    return r.results[0]["out_rows"][:T].reshape(B, N, D)
```

```python
from contextlib import ExitStack

import concourse.bass as bass
from concourse import mybir

F32 = mybir.dt.float32
F32R = mybir.dt.float32r
I32 = mybir.dt.int32
U8 = mybir.dt.uint8
ALU = mybir.AluOpType
ACT = mybir.ActivationFunctionType
AX = mybir.AxisListType
ds = bass.ds

P = 128
B, N, D = 4, 1024, 256
KC = D // P
NCTX = 77
NK = NCTX + 1
H, DH = 8, 64
NQ = H * DH // P
SK = H * NK
PK = 640
PC = PK // P
E = 8
F = 1024
FC = F // P
CAP = 2 * N // E
THRESH = 0.2
T = B * N
NT = T // P
NP_ = NT // 2
HT = NT // 2
HP = HT // 2
HB = B // 2
TPB = N // P
R = 2 * P
RW = 272
CID = D + E
S1 = E * B * CAP
G1 = S1 // R
HG = G1 // 2
GS = T // R
G2 = (2 * T + E * (R - 1)) // R
S2 = G2 * R
SPARE = 2 * P
S1ROWS = S1 + 2 * T
EPS = 1e-5
FMAX = 3.4028234663852886e38
RSQRT_SEED = 1597463007.0


def build(nc, io):
    with ExitStack() as ctx:
        def sb(name, shape, dt=F32):
            return ctx.enter_context(nc.sbuf_tensor(name, shape, dt))

        def sem(name):
            return ctx.enter_context(nc.semaphore(name))

        bank = [ctx.enter_context(nc.psum_tensor(f"bank{i}", [P, 512], F32)) for i in range(8)]

        xs1 = nc.dram_tensor("xs1", [S1ROWS, RW], F32).ap()
        xs2 = nc.dram_tensor("xs2", [S2, RW], F32).ap()
        xn2 = nc.dram_tensor("xn2", [T, D], F32).ap()
        x2b = nc.dram_tensor("x2b", [T, D], F32).ap()
        acc1 = nc.dram_tensor("acc1", [T + SPARE, D], F32).ap()
        out = io["out"]

        AR = sb("AR", [P, NT, RW])
        ident = sb("ident", [P, P])
        upper = sb("upper", [P, P])
        ones = sb("ones", [P, P])
        iota_e8 = sb("iota_e8", [P, E])
        iota_256k = sb("iota_256k", [P, NT // 2])
        iota_t = sb("iota_t", [P, G2])
        iota_e = sb("iota_e", [P, E])
        sb2 = sb("sb2", [P, D])
        sb1 = sb("sb1", [P, FC])
        wg2 = sb("wg2", [P, KC, E])
        b1b = [sb(f"b1b{i}", [P, FC]) for i in range(2)]
        b2b = [sb(f"b2b{i}", [P, D]) for i in range(2)]
        text = [sb(f"text{i}", [P, 2, D]) for i in range(2)]
        xr = text
        y = [sb(f"y{i}", [P, 2, D]) for i in range(2)]
        meta = [sb(f"meta{i}", [P, 2, E + 1]) for i in range(2)]
        wsel = sb("wsel", [P, 2, E])
        wv = sb("wv", [P, 2])
        ln = sb("ln", [P, 7, NT])
        LG = sb("LG", [P, NT, E])
        RA = sb("RA", [P, NT, E])
        RB = sb("RB", [P, NT, E])
        rows6 = RB[:, :, 0:6]
        RT = sb("RT", [P, NT, E])
        OH = sb("OH", [P, 2, NT, E])
        OH1 = OH[:].rearrange("p k j e -> p (k j e)").rearrange("p (h k j e) -> p h k j e", h=2, k=2, e=E)
        TO = sb("TO", [P, 2, E, NT])
        SCN = sb("SCN", [P, 2, E, NT])
        POS = sb("POS", [P, 2, NT, E])
        v32 = sb("v32", [P, 16, NT])
        slot = [sb(f"slot{k}", [P, NT], I32) for k in range(2)]
        cmp = TO[:].rearrange("p k e j -> p (k e j)")[:, 0:E * NT // 2].rearrange("p (e n) -> p e n", e=E)
        e8 = sb("e8", [P, 5, E])
        OHT = sb("OHT", [P, G2, E])
        oht2 = SCN[:].rearrange("p k e j -> p (k e j)")[:, 0:G2 * E].rearrange("p (t e) -> p t e", e=E)
        eidf = sb("eidf", [P, G2])
        eid = sb("eid", [P, G2], I32)
        cell_v = sb("cell_v", [P, 2])
        cell_a = sb("cell_a", [P, 1])

        with ExitStack() as first:
            def sa(name, shape, dt=F32):
                return first.enter_context(nc.sbuf_tensor(name, shape, dt))

            X = sa("X", [P, NT, D])
            area = sa("area", [P, 12288])
            KB = area[:, 0:2496].rearrange("p (b q c) -> p b q c", b=B, q=NQ)
            VB = area[:, 2496:6592].rearrange("p (b q c) -> p b q c", b=B, q=NQ)
            MQ = area[:, 6592:11584].rearrange("p (b k c) -> p b k c", b=B, k=KC)
            VW = sa("VW", [P, B, PC, D])
            area3 = sa("area3", [P, 4712])
            wkv = area3[:, 0:2048].rearrange("p (k n) -> p k n", k=KC)
            wqT = area3[:, 2048:3072].rearrange("p (q n) -> p q n", q=NQ)
            wo = area3[:, 3072:4096].rearrange("p (q n) -> p q n", q=NQ)
            ctxT = area3[:, 4096:4712].rearrange("p (k n) -> p k n", k=KC)
            score = [[area3[:, PK * (2 * i + u):PK * (2 * i + u + 1)] for u in range(2)] for i in range(2)]
            pT = [area3[:, PK * (4 + u):PK * (5 + u)].rearrange("p (c n) -> p c n", c=PC) for u in range(2)]
            z = [sa(f"z{i}", [P, 2, D]) for i in range(2)]
            act_a = [sa(f"act_a{i}", [P, 2, D]) for i in range(2)]
            tT = sa("tT", [P, 2, KC, P])
            aT = sa("aT", [P, 2, KC, P])
            smax = [[sa(f"smax{i}{u}", [P, H]) for u in range(2)] for i in range(2)]
            ssum = [sa(f"ssum{u}", [P, H]) for u in range(2)]
            srec = [sa(f"srec{u}", [P, H]) for u in range(2)]
            st6 = sa("st6", [P, 2, 6])
            mv_out = sa("mv_out", [P, 2, 2])
            var = sa("var", [P, 2])
            rstd = sa("rstd", [P, 2])
            nwt = sa("nwt", [P, 2])
            first_slot = sa("first_slot", [P, B, E])
            spare_row = sa("spare_row", [P, 2, NT])
            seg1 = sa("seg1", [P, 2 * E * HT])
            m1c = sa("m1c", [P, B // 2, E])
            fill = sa("fill", [P, 2, RW])
            nullc = sa("nullc", [P, 2])
            gcol = sa("gcol", [P, KC])
            ogam = sa("ogam", [P, D])
            mask8 = sa("mask8", [P, B * NCTX], U8)
            maskb = sa("maskb", [P, B, NK])
            prob = sa("prob", [P, NT])
            wg1 = sa("wg1", [P, KC, E])

        raw = sb("raw", [P, 4, F])
        w_h = [sb(f"w_h{i}", [P, 4, F], F32R) for i in range(2)]
        w_l = [sb(f"w_l{i}", [P, 4, F], F32R) for i in range(2)]
        h_h = [sb(f"h_h{i}", [P, FC, R], F32R) for i in range(2)]
        h_l = [sb(f"h_l{i}", [P, FC, R], F32R) for i in range(2)]
        x_h = [sb(f"x_h{i}", [P, KC, R], F32R) for i in range(2)]
        x_l = [sb(f"x_l{i}", [P, KC, R], F32R) for i in range(2)]
        gel = sb("gel", [P, FC // 2, 2 * R])
        x2 = [raw[:, 2 * i:2 * i + 2, :].rearrange("p q f -> p (q f)").rearrange("p (t d) -> p t d", t=TPB)
              for i in range(2)]
        yb = sb("yb", [P, 2, D])
        xnT = [sb("xnT0", [P, 2, KC, P]), yb[:].rearrange("p u (k n) -> p u k n", k=KC)]
        xh = [sb(f"xh{i}", [P, 2, D]) for i in range(2)]
        xhn = [sb(f"xhn{i}", [P, 2, D]) for i in range(2)]
        xn = xh + xhn

        x_in, par_in, consts, kb_zero = sem("x_in"), sem("par_in"), sem("consts"), sem("kb_zero")
        filled = [sem(f"filled{m}") for m in range(2)]
        kv_ps, k_ev, v_ev, m_ps, m_ev, vw_ps, vw_ev, maskb_ready = (sem(n) for n in (
            "kv_ps", "k_ev", "v_ev", "m_ps", "m_ev", "vw_ps", "vw_ev", "maskb_ready"))
        (text_ready, textT_ps, textT_ready, att_ps, z_ready, rstd_ready, tanh_ready, a_ready,
         aT_ps, aT_ready, gate_ps, gate_ready) = (sem(n) for n in (
             "text_ready", "textT_ps", "textT_ready", "att_ps", "z_ready", "rstd_ready", "tanh_ready", "a_ready",
             "aT_ps", "aT_ready", "gate_ps", "gate_ready"))
        text_kept = [sem(f"text_kept{i}") for i in range(2)]
        a_kept = [sem(f"a_kept{i}") for i in range(2)]
        (score_ps, score_ready, max_ready, sub_ready, exp_ready, rec_ready, prob_ready, probT_ps,
         probT_ready) = (sem(n) for n in (
             "score_ps", "score_ready", "max_ready", "sub_ready", "exp_ready", "rec_ready", "prob_ready",
             "probT_ps", "probT_ready"))
        dve_self = sem("dve_self")
        rt_sub, rt_exp, rt_hot, rt_pos, rt_taken, rt_done = (sem(n) for n in (
            "rt_sub", "rt_exp", "rt_hot", "rt_pos", "rt_taken", "rt_done"))
        rows_out, rows_out2 = [sem(f"rows_out{i}") for i in range(2)], sem("rows_out2")
        x_rows = [sem(f"x_rows{i}") for i in range(2)]
        meta_in = [sem(f"meta_in{i}") for i in range(2)]
        b1_in = [sem(f"b1_in{i}") for i in range(2)]
        b2_in = [sem(f"b2_in{i}") for i in range(2)]
        w1_in, w2_in, x_low, h_low, gelu_done = (sem(n) for n in ("w1_in", "w2_in", "x_low", "h_low", "gelu_done"))
        w_high = [sem(f"w{m}_high") for m in (1, 2)]
        w_low = [sem(f"w{m}_low") for m in (1, 2)]
        shared_out = [sem(f"shared_out{i}") for i in range(2)]
        xT_ps, xT_ready, h_ps, h_ready, y_ps, y_ready, added1, added2 = (sem(n) for n in (
            "xT_ps", "xT_ready", "h_ps", "h_ready", "y_ps", "y_ready", "added1", "added2"))
        o_in = [sem(f"o_in{i}") for i in range(2)]
        o_out = [sem(f"o_out{i}") for i in range(2)]
        o_tanh, o_norm, o_bias, oT_ps, oT_ready, og_ps, og_ready = (sem(n) for n in (
            "o_tanh", "o_norm", "o_bias", "oT_ps", "oT_ready", "og_ps", "og_ready"))
        acc_in = [sem(f"acc_in{b}") for b in range(B)]
        x2_in = [sem(f"x2_in{b}") for b in range(B)]
        x2_kept = [sem(f"x2_kept{b}") for b in range(B)]
        y_in = [sem(f"y_in{i}") for i in range(2)]
        xn_out = [sem(f"xn_out{i}") for i in range(4)]
        c_tanh = sem("c_tanh")

        SHARED = 2 * E
        NPAR = 14
        X2_LINKS = 20
        FILL = 5
        NCONST = 12
        M2 = G1 + GS
        block = ctx.enter_context(nc.Block())

        def rows(dram, g, width=D):
            return dram[ds(g * R, R), 0:width].rearrange("(h p) d -> p h d", p=P)

        def run_steps(eng, step, lo, first, last, hi, chain=None, per=0):
            for s in range(lo, first):
                step(s, s % 2)
            if last > first:
                with eng.Fori(first // 2, last // 2) as i:
                    if chain:
                        chain.enter((i - first // 2) * per)
                    step(2 * i, 0)
                    step(2 * i + 1, 1)
                    if chain:
                        chain.leave((last - first) // 2, per)
            for s in range(last, hi):
                step(s, s % 2)

        def wait_apart(eng, cell, own, n):
            eng.wait_ge(own, n)
            eng.tensor_tensor(cell[:, 1:2], cell[:, 0:1], cell[:, 0:1], ALU.add)

        class Chain:

            def __init__(self, eng, own):
                self.eng, self.own, self.n, self.base = eng, own, 0, 0

            def link(self, ins, scratch=None):
                ins.then_inc(self.own, 1)
                self.n += 1
                if scratch:
                    wait_apart(self.eng, scratch, self.own, self.base + self.n)
                else:
                    self.eng.wait_ge(self.own, self.base + self.n)

            def enter(self, base):
                self.base, self.at = base, self.n

            def leave(self, turns, per):
                assert self.n - self.at == per, (self.n - self.at, per)
                self.n, self.base = self.at + turns * per, 0

        def slots_of(g, par, half):
            return 2 * g - par - (G1 - 2) * half

        def known(s, least):
            return not isinstance(s, int) or s >= least

        def below(s, end):
            return not isinstance(s, int) or s < end

        @block.sync
        def _(sp):
            def par(dst, src):
                sp.dma_start(dst, src).then_inc(par_in, 16)

            par(ctxT, io["ctxT"].rearrange("(k p) n -> p k n", p=P))
            par(wkv, io["Wkv"].rearrange("(k p) n -> p k n", p=P))
            par(nullc[0:DH, :], io["null"])
            par(nullc[DH:P, :], io["null"])
            par(wqT, io["WqT"].rearrange("(q p) n -> p q n", p=P))
            par(wo, io["Wo"].rearrange("(q p) n -> p q n", p=P))
            par(gcol[:], io["ln_g"])
            par(mask8[:], io["mask"].partition_broadcast(P))
            par(ogam[:], io["out_g"].partition_broadcast(P))
            par(sb2[:], io["sb2"].partition_broadcast(P))
            par(prob[:], io["probs"])
            par(wg1[:], io["wg1"].rearrange("(k p) n -> p k n", p=P))
            par(wg2[:], io["wg2"].rearrange("(k p) n -> p k n", p=P))
            par(sb1[:], io["sb1"])
            for b in range(B):
                sp.dma_start(X[:, b * TPB:(b + 1) * TPB, :],
                             io["x"][b * N:(b + 1) * N, :].rearrange("(t p) d -> p t d", p=P)).then_inc(x_in, 16)

            def copy_step(s, par):
                if below(s, NP_):
                    sp.wait_ge(text_ready, s + 1)
                    sp.dma_start(AR[:, ds(2 * s, 2), 0:D], text[par][:]).then_inc(text_kept[par], 16)
                if known(s, 3):
                    sp.wait_ge(a_ready, s - 2)
                    sp.dma_start(AR[:, ds(2 * s - 6, 2), 0:D], act_a[1 - par][:]).then_inc(a_kept[1 - par], 16)
                    sp.dma_start(rows(acc1, s - 3), act_a[1 - par][:]).then_inc(a_kept[1 - par], 16)
            run_steps(sp, copy_step, 0, 4, NP_, NP_ + 3)

            def w1_load(n, e, name):
                if known(n, 1):
                    sp.wait_ge(w_low[0], 2 * n)
                sp.dma_start(raw[:, 0:2, :], io[name][ds(e, 1), :, :].rearrange("o p (k f) -> p (o k) f", k=KC)).then_inc(w1_in, 16)

            def w2_load(n, e, name):
                if known(n, 1):
                    sp.wait_ge(w_low[1], 2 * n)
                sp.dma_start(raw[:, 2:4, :], io[name][ds(e, 1), :, :].rearrange("o p (h f) -> p (o h) f", h=2)).then_inc(w2_in, 16)

            sp.wait_ge(att_ps, NP_)
            w1_load(0, 0, "W1a")
            w2_load(0, 0, "W2a")
            sp.wait_ge(rows_out[0], 16 * 2 * HT)

            def x_load(g, par, src):
                if known(g, 2):
                    sp.wait_ge(xT_ps, g - 1)
                sp.dma_start(xr[par][:], src).then_inc(x_rows[par], 16)

            def moe1_loads(n, half, following, names):
                for k in range(2):
                    x_load(2 * n + k, k, rows(xs1, slots_of(2 * n + k, k, half)))
                    (w1_load, w2_load)[k](n + 1, following, names[k])
            moe1_loads(0, 0, 1, ("W1a", "W2a"))
            with sp.Fori(1, E - 1) as n:
                moe1_loads(n, 0, n + 1, ("W1a", "W2a"))
            moe1_loads(E - 1, 0, 0, ("W1a", "W2a"))
            sp.wait_ge(rows_out[1], 16 * 2 * HT)

            def half_load(p):
                if p >= 2:
                    sp.wait_ge(oT_ps, p - 1)
                    sp.wait_ge(o_out[p % 2], 48 * (p // 2))
                sp.dma_start(xh[p % 2][:], rows(io["x"], p)).then_inc(o_in[p % 2], 16)

            sp.wait_ge(filled[1], 16 * 2 * -(-G2 // FILL))
            for n in range(E, 2 * E):
                last = n == 2 * E - 1
                moe1_loads(n, 1, 0 if last else n + 1 - E, ("sW1", "sW2") if last else ("W1a", "W2a"))
                if n == E + 1:
                    sp.wait_ge(added1, 32 * HG)
                    for b in range(HB):
                        sp.dma_start(AR[:, b * TPB:(b + 1) * TPB, 0:D],
                                     acc1[b * N:(b + 1) * N, :].rearrange("(t p) d -> p t d", p=P)).then_inc(acc_in[b], 16)
                if n >= E + 1:
                    half_load(n - E - 1)
            half_load(HP - 1)

            def shared_x(t, par):
                x_load(G1 + t, par, rows(xn2, t))

            def shared_y(t, par):
                sp.dma_start(y[par][:], rows(x2b, t)).then_inc(y_in[par], 16)

            shared_x(0, 0)
            shared_x(1, 1)
            sp.wait_ge(added1, 32 * G1)
            sp.wait_ge(w_low[1], 2 * SHARED + 2)
            for b in range(HB, B):
                sp.dma_start(AR[:, b * TPB:(b + 1) * TPB, 0:D],
                             acc1[b * N:(b + 1) * N, :].rearrange("(t p) d -> p t d", p=P)).then_inc(acc_in[b], 16)
                sp.dma_start(x2[b % 2], io["x"][b * N:(b + 1) * N, :].rearrange("(t p) d -> p t d", p=P)).then_inc(x2_in[b], 16)
            shared_y(0, 0)
            shared_y(1, 1)

            def shared_store(t, par):
                sp.wait_ge(y_ready, G1 + t + 1)
                sp.dma_start(rows(out, t), y[par][:]).then_inc(shared_out[par], 16)

            shared_x(2, 0)

            def shared_step(t, par):
                if below(t, GS - 3):
                    shared_x(t + 3, 1 - par)
                shared_store(t, par)
                sp.wait_ge(shared_out[par], 16 * (t // 2 + 1))
                shared_y(t + 2, par)
            for t in range(3):
                shared_step(t, t % 2)
            for i in range(2):
                sp.wait_ge(o_out[i], 48 * HP // 2)
            shared_step(3, 1)
            shared_step(4, 0)
            for k in range(4):
                sp.wait_ge(xn_out[k], 32 * HB)
            for b in range(HB, B):
                sp.wait_ge(x2_kept[b], 16)
            run_steps(sp, shared_step, 5, 6, GS - 4, GS - 4)

            sp.wait_ge(rt_done, 3)

            def expert_of(t):
                return sp.value_load(eid[0:1, ds(t, 1)], min_val=0, max_val=E - 1)

            def routed_w1(t, par):
                e, g = expert_of(t), M2 + t
                if known(t, 2):
                    sp.wait_ge(h_ready, 4 * g - 4)
                sp.dma_start(b1b[par][:], io["b1"][ds(e, 1), :, :].rearrange("o p c -> p (o c)")).then_inc(b1_in[par], 16)
                w1_load(SHARED + 1 + t, e, "W1b")

            def routed_w2(t, par):
                e, g = expert_of(t), M2 + t
                w2_load(SHARED + 1 + t, e, "W2b")
                if known(t, 2):
                    sp.wait_ge(y_ready, g - 1)
                sp.dma_start(b2b[par][:], io["b2"][ds(e, 1), :].broadcast_to([P, D])).then_inc(b2_in[par], 16)

            routed_w1(0, 0)
            routed_w2(0, 0)
            shared_step(GS - 4, 0)
            sp.wait_ge(rows_out2, 16 * 2 * NT)
            x_load(M2, 0, rows(xs2, 0))
            shared_step(GS - 3, 1)
            shared_store(GS - 2, 0)
            x_load(M2 + 1, 1, rows(xs2, 1))
            routed_w1(1, 1)

            def routed_step(t, par):
                if below(t, G2 - 2):
                    x_load(M2 + t + 2, par, rows(xs2, t + 2))
                    routed_w1(t + 2, par)
                routed_w2(t + 1, 1 - par)
            routed_step(0, 0)
            shared_store(GS - 1, 1)
            run_steps(sp, routed_step, 1, 2, G2 - 3 - (G2 - 3) % 2, G2 - 1)
            sp.wait_ge(added2, 32 * G2)
            for i in range(2):
                sp.wait_ge(shared_out[i], 16 * GS // 2)

        @block.tensor
        def _(pe):
            mm = nc.tensor.matmul
            pe.wait_ge(par_in, 16 * NPAR)
            for kv in range(2):
                for q in range(NQ):
                    for k in range(KC):
                        last = mm(bank[4 * kv + q][:, 0:B * NCTX],
                                  wkv[:, k, kv * H * DH + q * P:kv * H * DH + (q + 1) * P], ctxT[:, k, :],
                                  start=(k == 0), stop=(k == KC - 1))
            last.then_inc(kv_ps, 1)
            pe.wait_ge(k_ev, 1)
            for b in range(B):
                for k in range(KC):
                    n = b * KC + k
                    if n >= 2:
                        pe.wait_ge(m_ev, n - 1)
                    for q in range(NQ):
                        last = mm(bank[2 * (n % 2) + q // 2][:, (q % 2) * 2 * NK:(q % 2 + 1) * 2 * NK],
                                  wqT[:, q, k * P:(k + 1) * P], KB[:, b, q, :], start=True, stop=True)
                    last.then_inc(m_ps, 1)
            pe.wait_ge(v_ev, 1)
            for b in range(B):
                for c2 in range(3):
                    n = b * 3 + c2
                    if n >= 4:
                        pe.wait_ge(vw_ev, n - 3)
                    for c in range(2 * c2, min(2 * c2 + 2, PC)):
                        parts = [(q, v) for q, v in ((c - 1, 1), (c, 0)) if 0 <= q < NQ]
                        for m, (q, v) in enumerate(parts):
                            last = mm(bank[4 + n % 4][:, (c % 2) * D:(c % 2 + 1) * D], VB[:, b, q, v * P:(v + 1) * P],
                                      wo[:, q, :], start=(m == 0), stop=(m == len(parts) - 1))
                    last.then_inc(vw_ps, 1)
            pe.wait_ge(m_ev, B * KC)
            pe.wait_ge(vw_ev, B * 3)
            pe.wait_ge(consts, NCONST)

            def count_slots(n, hot, banks):
                pe.wait_ge(rt_hot, n)
                mm(banks[0], upper[:], hot, start=True, stop=True)
                mm(banks[1], ones[:], hot, start=True, stop=True).then_inc(rt_pos, 1)

            def choices(half):
                return OH1[:, half].rearrange("p k j e -> p (k j e)")

            def transposes(dst, src, done):
                for u in range(2):
                    for k in range(KC):
                        last = nc.tensor.transpose(dst[:, (u * KC + k) * P:(u * KC + k + 1) * P],
                                                   src[:, u, k * P:(k + 1) * P], ident[:])
                last.then_inc(done, 1)

            def att_step(s, par):
                A, Bs = known(s, 0) and below(s, NP_), known(s, 2) and below(s, NP_ + 2)
                G = known(s, 4)

                def scores(u):
                    if u == 0:
                        pe.wait_ge(textT_ready, s + 1)
                    if known(s, 1) or u:
                        pe.wait_ge(score_ready, 2 * s + u)
                    for half in range(2):
                        for k in range(KC):
                            last = mm(bank[1 + half][:, 0:SK // 2], tT[:, u, k, :],
                                      MQ[:, ds(s // 4, 1), k, half * SK // 2:(half + 1) * SK // 2].rearrange("p b c -> p (b c)"),
                                      start=(k == 0), stop=(k == KC - 1))
                    last.then_inc(score_ps, 1)

                def prob_t(u):
                    pe.wait_ge(prob_ready, 2 * (s - 2) + u + 1)
                    for c in range(PC):
                        last = nc.tensor.transpose(bank[3 + c // 4][:, (c % 4) * P:(c % 4 + 1) * P],
                                                   score[par][u][:, c * P:(c + 1) * P], ident[:])
                    last.then_inc(probT_ps, 1)

                def attend(u):
                    pe.wait_ge(probT_ready, 2 * (s - 2) + u + 1)
                    if u == 0 and known(s, 3):
                        pe.wait_ge(z_ready, s - 2)
                    for c in range(PC):
                        last = mm(bank[5][:, u * D:(u + 1) * D], pT[u][:, c, :],
                                  VW[:, ds((s - 2) // 4, 1), c, :].rearrange("p b d -> p (b d)"),
                                  start=(c == 0), stop=(c == PC - 1))
                    if u:
                        last.then_inc(att_ps, 1)

                if Bs:
                    prob_t(0)
                if A:
                    scores(0)
                if G:
                    pe.wait_ge(a_ready, s - 3)
                    transposes(bank[6], act_a[par], aT_ps)
                if Bs:
                    attend(0)
                    prob_t(1)
                if A:
                    scores(1)
                if below(s, NP_ - 1):
                    pe.wait_ge(text_ready, s + 2)
                    transposes(bank[0], text[1 - par], textT_ps)
                if G:
                    pe.wait_ge(aT_ready, s - 3)
                    if known(s, 5):
                        pe.wait_ge(gate_ready, s - 4)
                    if isinstance(s, int) and s == 14:
                        pe.wait_ge(rt_taken, 1)
                    for u in range(2):
                        for k in range(KC):
                            last = mm(bank[7][:, u * E:(u + 1) * E], aT[:, u, k, :], wg1[:, k, :],
                                      start=(k == 0), stop=(k == KC - 1))
                    last.then_inc(gate_ps, 1)
                if Bs:
                    attend(1)
            run_steps(pe, att_step, -1, 6, 14, 14)
            pe.wait_ge(gate_ready, 14 - 4)
            count_slots(1, choices(0), (bank[7][:, 0:2 * HT * E], bank[7][:, 2 * HT * E:4 * HT * E]))
            run_steps(pe, att_step, 14, 14, 14, NP_ + 4)
            pe.wait_ge(gate_ready, NP_)
            count_slots(2, choices(1), (bank[7][:, 0:2 * HT * E], bank[7][:, 2 * HT * E:4 * HT * E]))

            def x_turn(g, par):
                pe.wait_ge(x_rows[par], 16 * (g // 2 + 1))
                if known(g, 1):
                    pe.wait_ge(x_low, g)
                for k in range(KC):
                    for u in range(2):
                        last = nc.tensor.transpose(bank[0][:, k * R + u * P:k * R + (u + 1) * P],
                                                   xr[par][:, u, k * P:(k + 1) * P], ident[:])
                last.then_inc(xT_ps, 1)

            def product(dst, lhs, rhs, chunks):
                for c in range(chunks):
                    for n, (p, q) in enumerate(((0, 0), (0, 1), (1, 0))):
                        last = mm(dst, lhs(c, p), rhs(c, q), start=(c == 0 and n == 0), stop=(c == chunks - 1 and n == 2))
                return last

            def first_product(g, par, n, wb):
                pe.wait_ge(x_low, g + 1)
                if n is not None:
                    pe.wait_ge(w_low[0], 2 * n + 2)
                for j in range(FC // 2):
                    if known(g, 1):
                        pe.wait_ge(h_low, 4 * (g - 1) + j + 1)
                    for c in (2 * j, 2 * j + 1):
                        last = product(bank[1 + j][:, (c % 2) * R:(c % 2 + 1) * R],
                                       lambda k, part: (w_h, w_l)[part][wb][:, k, c * P:(c + 1) * P],
                                       lambda k, part: (x_h, x_l)[part][par][:, k, :], KC)
                    last.then_inc(h_ps, 1)

            def second_product(g, par, n, wb):
                pe.wait_ge(h_low, 4 * g + 4)
                if n is not None:
                    pe.wait_ge(w_low[1], 2 * n + 2)
                if known(g, 2):
                    pe.wait_ge(y_ready, g - 1)
                for u in range(2):
                    last = product(bank[5 + par][:, u * D:(u + 1) * D],
                                   lambda c, part: (h_h, h_l)[part][par][:, c, u * P:(u + 1) * P],
                                   lambda c, part: (w_h, w_l)[part][wb][:, 2 + c // 4, (c % 4) * D:(c % 4 + 1) * D], FC)
                last.then_inc(y_ps, 1)

            x_turn(0, 0)

            def half_turn(p, src, dst):
                pe.wait_ge(o_norm, p + 1)
                transposes(dst, src, oT_ps)

            def half_gate(p, par):
                pe.wait_ge(oT_ready, p + 1)
                pe.wait_ge(og_ready, p + 1)
                for u in range(2):
                    for k in range(KC):
                        last = mm(bank[7][:, u * E:(u + 1) * E], xnT[par][:, u, k, :], wg2[:, k, :],
                                  start=(k == 0), stop=(k == KC - 1))
                last.then_inc(og_ps, 1)

            def moe1_sets(i, x2_too=False):
                for k in range(4):
                    g, n = 4 * i + k, 2 * i + k // 2
                    if below(g, G1 - 1):
                        x_turn(g + 1, (k + 1) % 2)
                    first_product(g, k % 2, n if k % 2 == 0 else None, k // 2)
                    p = 2 * i - E - 2 + k // 2
                    if x2_too and k % 2 == 0:
                        pe.wait_ge(og_ready, p + 1)
                        half_turn(p, xhn[k // 2], bank[7])
                    if known(g, 1):
                        second_product(g - 1, (k - 1) % 2, n if k % 2 else None, (k - 1) % 4 // 2)
                    if x2_too and k % 2 == 0:
                        half_gate(p, 0)
            moe1_sets(0)
            with pe.Fori(1, E // 2 + 1) as i:
                moe1_sets(i)
            with pe.Fori(E // 2 + 1, E - 1) as i:
                moe1_sets(i, True)
            moe1_sets(E - 1, True)
            second_product(G1 - 1, 1, None, 1)
            for p in (HP - 2, HP - 1):
                pe.wait_ge(og_ready, p + 1)
                half_turn(p, xhn[p % 2], bank[7])
                half_gate(p, 0)

            def shared_step(t, par):
                g = G1 + t
                x_turn(g + 1, 1 - par)
                first_product(g, par, None if known(t, 1) else SHARED, 0)
                if known(t, 1):
                    second_product(g - 1, 1 - par, SHARED if isinstance(t, int) and t == 1 else None, 0)

            def batch_gates(b, t):
                pe.wait_ge(x_low, G1 + t + 2)
                for k in range(4):
                    p = HP + 4 * (b - HB) + k
                    if k:
                        pe.wait_ge(oT_ready, p)
                    half_turn(p, xn[k], bank[0])
                    if k:
                        half_gate(p - 1, 1 - k % 2)
                half_gate(p, 1)
            x_turn(G1, 0)
            shared_step(0, 0)
            shared_step(1, 1)
            batch_gates(HB, 1)
            shared_step(2, 0)
            batch_gates(HB + 1, 2)
            shared_step(3, 1)
            shared_step(4, 0)
            count_slots(3, OH[:, 0].rearrange("p j e -> p (j e)"), (bank[7][:, 0:NT * E], bank[7][:, NT * E:2 * NT * E]))
            run_steps(pe, shared_step, 5, 6, GS, GS)

            def routed_step(t, par):
                g, n = M2 + t, SHARED + 1 + t
                if below(t, G2 - 1):
                    x_turn(g + 1, 1 - par)
                first_product(g, par, n, 1 - par)
                second_product(g - 1, 1 - par, n - 1 if known(t, 1) else None, par)
            run_steps(pe, routed_step, 0, 2, G2 - 1 - (G2 - 1) % 2, G2)
            second_product(M2 + G2 - 1, (G2 - 1) % 2, SHARED + G2, G2 % 2)

        @block.scalar
        def _(act):
            A_ = nc.scalar.activation
            act.wait_ge(kv_ps, 1)
            act.wait_ge(kb_zero, 2)
            for q in range(NQ):
                v = bank[4 + q][:, 0:B * NCTX].rearrange("p (b n) -> p b n", b=B)
                o = 28 * q
                A_(VB[0:DH, :, q, o + 1:o + NK], v[0:DH], ACT.Copy)
                A_(VB[DH:P, :, q, o + NK + 1:o + 2 * NK], v[DH:P], ACT.Copy)
                A_(VB[0:DH, :, q, o], nullc[0:DH, 1:2].broadcast_to([DH, B]), ACT.Copy)
                last = A_(VB[DH:P, :, q, o + NK], nullc[DH:P, 1:2].broadcast_to([DH, B]), ACT.Copy)
            last.then_inc(v_ev, 1)
            for n in range(B * 3):
                b, c = n // 3, 2 * (n % 3)
                w = min(2, PC - c)
                act.wait_ge(vw_ps, n + 1)
                A_(VW[:, b, c:c + w, :].rearrange("p c d -> p (c d)"), bank[4 + n % 4][:, 0:w * D], ACT.Copy).then_inc(vw_ev, 1)

            act.wait_ge(consts, NCONST)
            act.dma_start(acc1[T:T + SPARE, :].rearrange("(h p) d -> p h d", p=P), fill[:, :, 0:D]).then_inc(filled[0], 16)
            act.dma_start(out[T:T + SPARE, :].rearrange("(h p) d -> p h d", p=P), fill[:, :, 0:D]).then_inc(filled[0], 16)

            def empty_slots(m, dram, tiles, c):
                n = min(FILL, tiles - c * FILL)
                for h in range(2 if n > 0 else 0):
                    act.dma_start(dram[c * FILL * R:(c * FILL + n) * R, :].rearrange("(n h p) c -> h p n c", h=2, p=P)[h],
                                  fill[:, h, :].unsqueeze(1).broadcast_to([P, n, RW])).then_inc(filled[m], 16)

            def att_step(s, par):
                A, Bs, C = known(s, 0) and below(s, NP_), known(s, 2) and below(s, NP_ + 2), known(s, 3) and below(s, NP_ + 3)
                G = known(s, 4)

                if isinstance(s, int) and s < 6:
                    empty_slots(0, xs1, G1, s + 1)
                elif isinstance(s, int):
                    empty_slots(1, xs2, G2, s - 12)

                def prob_t(u):
                    act.wait_ge(probT_ps, 2 * (s - 2) + u + 1)
                    A_(pT[u][:, 0:4, :].rearrange("p c n -> p (c n)"), bank[3][:], ACT.Copy)
                    A_(pT[u][:, 4, :], bank[4][:, 0:P], ACT.Copy).then_inc(probT_ready, 1)

                def exps(u):
                    act.wait_ge(sub_ready, 2 * s + u + 1)
                    A_(score[par][u][:, 0:SK], score[par][u][:, 0:SK], ACT.Exp).then_inc(exp_ready, 1)

                if Bs:
                    prob_t(0)
                if G:
                    act.wait_ge(aT_ps, s - 3)
                    if known(s, 5):
                        act.wait_ge(gate_ps, s - 4)
                    A_(aT[:].rearrange("p u k n -> p (u k n)"), bank[6][:], ACT.Copy).then_inc(aT_ready, 1)
                if Bs:
                    prob_t(1)
                if A:
                    exps(0)
                if C:
                    act.wait_ge(rstd_ready, s - 2)
                    for u in range(2):
                        last = A_(z[1 - par][:, u, :], z[1 - par][:, u, :], ACT.Tanh, scale=rstd[:, u:u + 1])
                    last.then_inc(tanh_ready, 1)
                if below(s, NP_ - 1):
                    act.wait_ge(textT_ps, s + 2)
                    A_(tT[:].rearrange("p u k n -> p (u k n)"), bank[0][:], ACT.Copy).then_inc(textT_ready, 1)
                if A:
                    exps(1)
            def route_exp(n, logits):
                act.wait_ge(rt_sub, n)
                A_(logits, logits, ACT.Exp).then_inc(rt_exp, 1)

            run_steps(act, att_step, -1, 6, 12, 12)
            route_exp(1, RA[:, 0:HT, :])
            run_steps(act, att_step, 12, 12, 14, NP_ + 4)

            route_exp(2, RA[:, HT:NT, :])

            def x_high(g, par):
                act.wait_ge(xT_ps, g + 1)
                if known(g, 2):
                    act.wait_ge(h_ps, 4 * (g - 1))
                A_(x_h[par][:].rearrange("p k r -> p (k r)"), bank[0][:], ACT.Copy).then_inc(xT_ready, 1)

            def w_part(n, q, wb):
                act.wait_ge((w1_in, w2_in)[q // 2], 16 * (n + 1))
                A_(w_h[wb][:, q, :], raw[:, q, :], ACT.Copy).then_inc(w_high[q // 2], 1)

            def pair_of(buf, par, j):
                return buf[par][:, 2 * j:2 * j + 2, :].rearrange("p c r -> p (c r)")

            for i in range(2):
                act.wait_ge(a_kept[i], 32 * NP_ // 2)
            for q in range(4):
                w_part(0, q, 0)
            x_high(0, 0)

            def half_tanh(p):
                for b in range(HB):
                    act.wait_ge(acc_in[b], 16)
                A_(AR[:, ds(2 * p, 2), 0:D], AR[:, ds(2 * p, 2), 0:D], ACT.Tanh).then_inc(o_tanh, 1)

            def half_logits(p):
                act.wait_ge(og_ps, p + 1)
                A_(LG[:, ds(2 * p, 2), :], bank[7][:, 0:2 * E].rearrange("p (u e) -> p u e", u=2), ACT.Copy).then_inc(og_ready, 1)

            def half_turned(p, src, par):
                act.wait_ge(oT_ps, p + 1)
                A_(xnT[par][:].rearrange("p u k n -> p (u k n)"), src[:], ACT.Copy).then_inc(oT_ready, 1)

            def moe1_sets(i, x2_from=4):
                for k in range(4):
                    g, n = 4 * i + k, 2 * i + k // 2
                    p = 2 * i - E - 2 + (k + 1) // 2
                    if k % 2 and k >= x2_from:
                        if known(p, 1):
                            half_logits(p - 1)
                        half_tanh(p)
                    if below(g, G1 - 1):
                        x_high(g + 1, (k + 1) % 2)
                    if known(g, 2):
                        act.wait_ge(y_ps, g - 1)
                    for j in range(FC // 2):
                        act.wait_ge(h_ps, 4 * g + j + 1)
                        A_(pair_of(h_h, k % 2, j), bank[1 + j][:], ACT.Relu).then_inc(h_ready, 1)
                    if k % 2 == 0 and k >= x2_from:
                        half_turned(p, bank[7], 0)
                    for q in (2 * (k % 2), 2 * (k % 2) + 1):
                        w_part(n + 1, q, 1 - k // 2)
            moe1_sets(0)
            with act.Fori(1, E // 2) as i:
                moe1_sets(i)
            act.wait_ge(rt_done, 2)
            A_(cell_a[:], ident[:, 0:1], ACT.Copy).then_inc(og_ready, 1)
            moe1_sets(E // 2, 3)
            with act.Fori(E // 2 + 1, E - 1) as i:
                moe1_sets(i, 0)
            moe1_sets(E - 1, 0)
            half_turned(HP - 2, bank[7], 0)
            half_logits(HP - 2)
            half_tanh(HP - 1)
            half_turned(HP - 1, bank[7], 0)
            half_logits(HP - 1)

            def x2_tanh(b):
                act.wait_ge(acc_in[b], 16)
                A_(AR[:, b * TPB:(b + 1) * TPB, 0:D], AR[:, b * TPB:(b + 1) * TPB, 0:D], ACT.Tanh).then_inc(c_tanh, 1)

            def hidden(g, par, bias):
                act.wait_ge(y_ps, g - 1)
                for j in range(FC // 2 + 1):
                    if j < FC // 2:
                        act.wait_ge(h_ps, 4 * g + j + 1)
                        act.wait_ge(h_low, 4 * g - 3 + j)
                        for c in (2 * j, 2 * j + 1):
                            last = A_(gel[:, j, (c % 2) * R:(c % 2 + 1) * R], bank[1 + j][:, (c % 2) * R:(c % 2 + 1) * R],
                                      ACT.Gelu, bias=bias[:, c:c + 1])
                        last.then_inc(gelu_done, 1)
                    if j:
                        act.wait_ge(gelu_done, 4 * (g - G1) + j)
                        A_(pair_of(h_h, par, j - 1), gel[:, j - 1, :], ACT.Copy).then_inc(h_ready, 1)

            def shared_step(t, par):
                x_high(G1 + t + 1, 1 - par)
                hidden(G1 + t, par, sb1)

            def batch_gates(b):
                for k in range(4):
                    p = HP + 4 * (b - HB) + k
                    half_turned(p, bank[0], k % 2)
                    if k:
                        half_logits(p - 1)
                half_logits(p)
            x_high(G1, 0)
            shared_step(0, 0)
            x2_tanh(HB)
            shared_step(1, 1)
            x2_tanh(HB + 1)
            batch_gates(HB)
            shared_step(2, 0)
            batch_gates(HB + 1)
            route_exp(3, RA[:])
            run_steps(act, shared_step, 3, 4, GS, GS)
            for q in range(2):
                w_part(SHARED + 1, q, 1)

            def routed_step(t, par):
                g, n = M2 + t, SHARED + 1 + t
                if below(t, G2 - 1):
                    x_high(g + 1, 1 - par)
                act.wait_ge(b1_in[par], 16 * (t // 2 + 1))
                hidden(g, par, b1b[par])
                if below(t, G2 - 1):
                    for q in (0, 1):
                        w_part(n + 1, q, par)
                for q in (2, 3):
                    w_part(n, q, 1 - par)
            run_steps(act, routed_step, 0, 2, G2 - 1 - (G2 - 1) % 2, G2)

        @block.vector
        def _(v):
            ve = nc.vector
            chain = Chain(v, dve_self)
            link = chain.link
            scratch = cell_v
            link(ve.memset(cell_v[:], 0.0))

            def rsqrt(r, x, t):
                link(ve.tensor_scalar(t.bitcast(I32), x.bitcast(I32), 1, None, ALU.logical_shift_right))
                link(ve.tensor_scalar(r.bitcast(I32), t.bitcast(I32), -1.0, RSQRT_SEED, ALU.mult, ALU.add))
                for k in range(3):
                    link(ve.scalar_tensor_tensor(t, r, -0.5, r, ALU.mult, ALU.mult))
                    link(ve.tensor_tensor(t, t, x, ALU.mult))
                    link(ve.scalar_tensor_tensor(r, t, 1.5, r, ALU.add, ALU.mult))

            mean, r1, rsc, t_a, t_b, t_c, t_d = (ln[:, i, :] for i in range(7))

            def row_stats(t, n):
                mean, _, _, t_a, t_b, t_c, _ = (ln[:, i, ds(t, n)] for i in range(7))
                m_e, v_e, m_o, v_o = (rows6[:, ds(t, n), i] for i in (1, 2, 4, 5))
                link(ve.tensor_tensor(t_a, m_e, m_o, ALU.subtract))
                link(ve.tensor_tensor(t_b, m_e, m_o, ALU.add))
                link(ve.tensor_scalar(mean, t_b, 0.5, None, ALU.mult))
                link(ve.scalar_tensor_tensor(t_b, t_a, 0.25, t_a, ALU.mult, ALU.mult))
                link(ve.tensor_tensor(t_c, v_e, v_o, ALU.add))
                link(ve.scalar_tensor_tensor(t_a, t_c, 1.0 / D, t_b, ALU.mult, ALU.add))

            def row(rows, t):
                return rows[:, ds(t, 1), :].rearrange("p o d -> p (o d)")

            def normed(t, dst, src):
                return ve.tensor_scalar(dst, src, ln[:, 0, ds(t, 1)], ln[:, 1, ds(t, 1)], ALU.subtract, ALU.mult)

            v.wait_ge(par_in, 16 * NPAR)
            v.wait_ge(kb_zero, 2)
            link(ve.memset(maskb[:], 0.0))
            ve.tensor_scalar(maskb[:, :, 1:NK], mask8[:].rearrange("p (b n) -> p b n", b=B), FMAX, -FMAX, ALU.mult,
                             ALU.add).then_inc(maskb_ready, 1)
            v.wait_ge(kv_ps, 1)
            for q in range(NQ):
                k = bank[q][:, 0:B * NCTX].rearrange("p (b n) -> p b n", b=B)
                ve.tensor_copy(KB[0:DH, :, q, 1:NK], k[0:DH])
                ve.tensor_copy(KB[DH:P, :, q, NK + 1:2 * NK], k[DH:P])
                ve.tensor_copy(KB[0:DH, :, q, 0], nullc[0:DH, 0:1].broadcast_to([DH, B]))
                last = ve.tensor_copy(KB[DH:P, :, q, NK], nullc[DH:P, 0:1].broadcast_to([DH, B]))
            last.then_inc(k_ev, 1)
            v.wait_ge(x_in, 16 * B)
            for n in range(B * KC):
                for t in range(NT // 8 * n, NT // 8 * (n + 1)):
                    last = ve.bn_stats(rows6[:, t, :], X[:, t, :])
                b, k = n // KC, n % KC
                v.wait_ge(m_ps, n + 1)
                for half in range(2):
                    last = ve.tensor_scalar(MQ[:, b, k, half * SK // 2:(half + 1) * SK // 2],
                                            bank[2 * (n % 2) + half][:, 0:SK // 2], gcol[:, k:k + 1], float(DH) ** -0.5,
                                            ALU.mult, ALU.mult)
                last.then_inc(m_ev, 1)
            v.wait_ge(m_ev, B * KC)
            row_stats(0, NT)
            link(ve.tensor_scalar(t_b, t_a, EPS, None, ALU.add))
            rsqrt(r1, t_b, t_c)
            link(ve.tensor_scalar(t_a, t_a, 1.0 + EPS, EPS * EPS, ALU.mult, ALU.add))
            rsqrt(t_d, t_a, t_c)
            link(ve.tensor_tensor(t_a, r1, t_d, ALU.mult))
            link(ve.tensor_tensor(rsc, t_a, t_b, ALU.mult))
            v.wait_ge(vw_ps, B * 3)
            for i in range(2):
                for u in range(2):
                    link(ve.memset(score[i][u][:, SK:PK], 0.0))

            def bc(a):
                return a.unsqueeze(2).broadcast_to([P, a.shape[1], E])

            def te(a, n):
                return a.unsqueeze(1).broadcast_to([P, n, E])

            mx, sm, g1, g2, ix, den, w1, w2, p1, p2, k1, k2, t0, t1 = range(14)

            def col(i, at):
                return v32[:, i, at]

            def top(at, n, g, hot):
                link(ve.tensor_reduce(col(g, at), RA[:, at, :], AX.X, ALU.max))
                link(ve.tensor_tensor(RT[:, at, :], RA[:, at, :], bc(col(g, at)), ALU.is_equal))
                link(ve.tensor_tensor(RT[:, at, :], RT[:, at, :], te(iota_e8[:], n), ALU.mult))
                link(ve.tensor_reduce(col(ix, at), RT[:, at, :], AX.X, ALU.min))
                link(ve.tensor_tensor(hot, te(iota_e8[:], n), bc(col(ix, at)), ALU.is_equal))

            def softmax_start(at):
                link(ve.tensor_reduce(col(mx, at), LG[:, at, :], AX.X, ALU.max))
                ve.tensor_tensor(RA[:, at, :], LG[:, at, :], bc(col(mx, at)), ALU.subtract).then_inc(rt_sub, 1)

            def softmax_end(at, n):
                v.wait_ge(rt_exp, n)
                link(ve.tensor_reduce(col(sm, at), RA[:, at, :], AX.X, ALU.add))
                link(ve.reciprocal(col(t0, at), col(sm, at)))
                link(ve.tensor_tensor(RA[:, at, :], RA[:, at, :], bc(col(t0, at)), ALU.mult))

            def gate_weights(at, eps):
                link(ve.scalar_tensor_tensor(col(den, at), col(g1, at), eps, col(g2, at), ALU.add, ALU.add))
                link(ve.reciprocal(col(t0, at), col(den, at)))
                link(ve.tensor_tensor(col(w1, at), col(g1, at), col(t0, at), ALU.mult))
                link(ve.tensor_tensor(col(w2, at), col(g2, at), col(t0, at), ALU.mult))

            def combine_weights(at, hot1, hot2):
                link(ve.tensor_tensor(RT[:, at, :], hot1, bc(col(w1, at)), ALU.mult))
                link(ve.tensor_tensor(RB[:, at, :], hot2, bc(col(w2, at)), ALU.mult))
                link(ve.tensor_tensor(AR[:, at, D:D + E], RT[:, at, :], RB[:, at, :], ALU.add))

            def pick(at, dst, hot, src):
                link(ve.tensor_tensor(RT[:, at, :], hot, src, ALU.mult))
                link(ve.tensor_reduce(col(dst, at), RT[:, at, :], AX.X, ALU.add))

            every = slice(0, NT)

            def half_of(half):
                return slice(half * HT, (half + 1) * HT), OH1[:, half, 0], OH1[:, half, 1]

            def by_batch(a):
                return a.rearrange("p (b j) e -> p b j e", b=HB)

            def route_choices(half):
                at, hot1, hot2 = half_of(half)
                softmax_end(at, half + 1)
                top(at, HT, g1, hot1)
                link(ve.tensor_scalar(RT[:, at, :], hot1, -1.0, 1.0, ALU.mult, ALU.add))
                link(ve.tensor_tensor(RA[:, at, :], RA[:, at, :], RT[:, at, :], ALU.mult))
                top(at, HT, g2, hot2)
                gate_weights(at, 1e-9)
                link(ve.tensor_scalar(col(t0, at), col(w2, at), 1.0 / THRESH, None, ALU.mult))
                link(ve.tensor_tensor(col(t0, at), prob[:, at], col(t0, at), ALU.is_lt))
                ve.tensor_tensor(hot2, hot2, bc(col(t0, at)), ALU.mult).then_inc(rt_hot, 1)

            def route_positions(half, before, totals):
                at, hot1, hot2 = half_of(half)
                tot, scan, pos = (a[:].rearrange("p a b c -> p (a b c)")[:, 0:2 * HT * E] for a in (TO, SCN, POS))
                kej = dict(k=2, e=E)
                v.wait_ge(rt_pos, half + 1)
                link(ve.tensor_copy(tot.rearrange("p (k e j) -> p k e j", **kej), totals.rearrange("p (k j e) -> p k e j", **kej)))
                link(ve.tensor_tensor_scan(scan, seg1[:], tot, 0.0, ALU.mult, ALU.add))
                link(ve.tensor_scalar(m1c[:], scan.rearrange("p (k e j) -> p k e j", **kej)[:, 0]
                                      .rearrange("p e (b j) -> p b e j", b=HB)[:, :, :, TPB - 1], float(CAP), None, ALU.min))
                link(ve.tensor_tensor(scan, scan, tot, ALU.subtract))
                pos = pos.rearrange("p (k j e) -> p k j e", **kej)
                link(ve.tensor_tensor(pos, before.rearrange("p (k j e) -> p k j e", **kej),
                                      scan.rearrange("p (k e j) -> p k j e", **kej), ALU.add))
                ve.tensor_copy(cell_v[:, 0:1], ones[:, 0:1]).then_inc(rt_taken, 1)
                link(ve.tensor_tensor(by_batch(pos[:, 1]), by_batch(pos[:, 1]),
                                      m1c[:].unsqueeze(2).broadcast_to([P, HB, TPB, E]), ALU.add))
                pick(at, p1, hot1, pos[:, 0])
                pick(at, p2, hot2, pos[:, 1])

            def route_slots(half):
                at, hot1, hot2 = half_of(half)
                P1, P2, K1, K2, W1, W2, T0, T1 = (col(i, at) for i in (p1, p2, k1, k2, w1, w2, t0, t1))
                link(ve.tensor_scalar(K1, P1, float(CAP), None, ALU.is_lt))
                link(ve.tensor_reduce(T1, hot2, AX.X, ALU.add))
                link(ve.scalar_tensor_tensor(K2, P2, float(CAP), T1, ALU.is_lt, ALU.mult))
                link(ve.scalar_tensor_tensor(K2, W2, 0.0, K2, ALU.is_gt, ALU.mult))
                link(ve.tensor_tensor(W1, W1, K1, ALU.mult))
                link(ve.tensor_tensor(W2, W2, K2, ALU.mult))
                combine_weights(at, hot1, hot2)
                for k, (hot, p, kept) in enumerate(((hot1, P1, K1), (hot2, P2, K2))):
                    spare = spare_row[:, k, at]
                    link(ve.tensor_tensor(by_batch(RT[:, at, :]), by_batch(hot),
                                          first_slot[:, half * HB:(half + 1) * HB, :].unsqueeze(2).broadcast_to([P, HB, TPB, E]),
                                          ALU.mult))
                    link(ve.tensor_reduce(T0, RT[:, at, :], AX.X, ALU.add))
                    link(ve.tensor_tensor(T0, T0, p, ALU.add))
                    link(ve.tensor_tensor(T0, T0, spare, ALU.subtract))
                    link(ve.tensor_tensor(T0, T0, kept, ALU.mult))
                    link(ve.tensor_tensor(slot[k][:, at], T0, spare, ALU.add))
                ve.tensor_copy(T1, T0).then_inc(rt_done, 1)

            def att_step(s, par):
                A, L = known(s, 0) and below(s, NP_), below(s, NP_ - 1)
                M = known(s, 1) and below(s, NP_ + 1)
                C, G = known(s, 3) and below(s, NP_ + 3), known(s, 4)

                def mask_and_max(u):
                    v.wait_ge(score_ps, 2 * s + u + 1)
                    if known(s, 2):
                        v.wait_ge(probT_ps, 2 * (s - 2) + u + 1)
                    sc = score[par][u]
                    for half in range(2):
                        c = slice(half * SK // 2, (half + 1) * SK // 2)
                        last = ve.scalar_tensor_tensor(
                            sc[:, c].rearrange("p (h n) -> p h n", n=NK),
                            bank[1 + half][:, 0:SK // 2].rearrange("p (h n) -> p h n", n=NK), ln[:, 2, ds(2 * s + u, 1)],
                            maskb[:, ds(s // 4, 1), :].broadcast_to([P, H // 2, NK]), ALU.mult, ALU.add)
                    last.then_inc(score_ready, 1)
                    v.wait_ge(score_ready, 2 * s + u + 1)
                    ve.tensor_reduce(smax[par][u][:], sc[:, 0:SK].rearrange("p (h n) -> p h n", n=NK), AX.X,
                                     ALU.max).then_inc(max_ready, 1)

                def sums(u):
                    v.wait_ge(exp_ready, 2 * s - 1 + u)
                    link(ve.tensor_reduce(ssum[u][:], score[1 - par][u][:, 0:SK].rearrange("p (h n) -> p h n", n=NK), AX.X,
                                          ALU.add))
                    if known(s, 2):
                        v.wait_ge(prob_ready, 2 * s - 3 + u)
                    ve.reciprocal(srec[u][:], ssum[u][:]).then_inc(rec_ready, 1)

                if C:
                    wait_apart(v, scratch, att_ps, s - 2)
                    for u in range(2):
                        last = ve.bn_stats(st6[:, u, :], bank[5][:, u * D:(u + 1) * D])
                    link(last, scratch)
                    for u in range(2):
                        last = ve.bn_aggr(mv_out[:, u, :], st6[:, u, :])
                    link(last)
                    if known(s, 5):
                        v.wait_ge(a_ready, s - 4)
                    for u in range(2):
                        last = ve.scalar_tensor_tensor(z[1 - par][:, u, :], bank[5][:, u * D:(u + 1) * D], mv_out[:, u, 0:1],
                                                       ogam[:], ALU.subtract, ALU.mult)
                    last.then_inc(z_ready, 1)
                if M:
                    sums(0)
                if A:
                    mask_and_max(0)
                if M:
                    sums(1)
                if L:
                    if known(s, 1):
                        v.wait_ge(textT_ps, s)
                        v.wait_ge(text_kept[1 - par], 16 * ((s - 1) // 2 + 1))
                    for u in range(2):
                        last = normed(2 * s + 2 + u, text[1 - par][:, u, :], row(X, 2 * s + 2 + u))
                    last.then_inc(text_ready, 1)
                if C:
                    link(ve.tensor_scalar(var[:], mv_out[:, :, 1], EPS, None, ALU.add))
                    if known(s, 4):
                        v.wait_ge(tanh_ready, s - 3)
                    rsqrt(rstd[:], var[:], nwt[:])
                    ve.tensor_copy(nwt[:], rstd[:]).then_inc(rstd_ready, 1)
                if A:
                    mask_and_max(1)
                if G:
                    v.wait_ge(gate_ps, s - 3)
                    ve.tensor_copy(LG[:, ds(2 * s - 8, 2), :], bank[7][:, 0:2 * E].rearrange("p (u e) -> p u e", u=2))\
                      .then_inc(gate_ready, 1)
            run_steps(v, att_step, -1, 6, 12, 12, chain, 2 * 16)
            v.wait_ge(gate_ready, NP_ // 2)
            softmax_start(slice(0, HT))
            att_step(12, 0)
            route_choices(0)
            att_step(13, 1)
            route_positions(0, bank[7][:, 0:2 * HT * E], bank[7][:, 2 * HT * E:4 * HT * E])
            att_step(14, 0)
            route_slots(0)
            run_steps(v, att_step, 15, 16, 16, NP_ + 4)
            v.wait_ge(gate_ready, NP_)
            softmax_start(slice(HT, NT))
            route_choices(1)


            def scale_out(g, par, free, metas, w):
                v.wait_ge(y_ps, g + 1)
                free()
                v.wait_ge(meta_in[par], metas)
                for u in range(2):
                    last = ve.tensor_scalar(y[par][:, u, :], bank[5 + par][:, u * D:(u + 1) * D], w(u), None, ALU.mult)
                last.then_inc(y_ready, 1)

            def moe1_out(g, k, e):
                par = k % 2

                def free():
                    if known(g, 2):
                        v.wait_ge(added1, 32 * (g - 1))
                scale_out(g, par, free, 16 * (g // 2 + 1), lambda u: meta[par][:, u, ds(e, 1)])

            def w_rest(n, q, wb):
                v.wait_ge(w_high[q // 2], 2 * n + q % 2 + 1)
                ve.tensor_tensor(w_l[wb][:, q, :], raw[:, q, :], w_h[wb][:, q, :].bitcast(F32), ALU.subtract)\
                  .then_inc(w_low[q // 2], 1)

            def x_rest(g, par):
                v.wait_ge(xT_ready, g + 1)
                ve.tensor_tensor(x_l[par][:].rearrange("p k r -> p (k r)"), bank[0][:],
                                 x_h[par][:].rearrange("p k r -> p (k r)").bitcast(F32), ALU.subtract).then_inc(x_low, 1)

            def pair_of(buf, par, j):
                return buf[par][:, 2 * j:2 * j + 2, :].rearrange("p c r -> p (c r)")

            for i in range(2):
                v.wait_ge(a_kept[i], 32 * NP_ // 2)
            for q in range(4):
                w_rest(0, q, 0)
            x_rest(0, 0)

            def half_rows(p, par):
                v.wait_ge(o_tanh, p + 1)
                v.wait_ge(o_in[par], 16 * (p // 2 + 1))
                link(ve.tensor_tensor(xh[par][:], xh[par][:], AR[:, ds(2 * p, 2), 0:D], ALU.add), scratch)
                for u in range(2):
                    last = ve.bn_stats(rows6[:, ds(2 * p + u, 1), :].rearrange("p o d -> p (o d)"), xh[par][:, u, :])
                link(last)
                row_stats(2 * p, 2)
                at = ds(2 * p, 2)
                link(ve.tensor_scalar(ln[:, 4, at], ln[:, 3, at], EPS, None, ALU.add))
                rsqrt(ln[:, 1, at], ln[:, 4, at], ln[:, 5, at])
                for u in range(2):
                    last = normed(2 * p + u, xhn[par][:, u, :], xh[par][:, u, :])
                last.then_inc(o_norm, 1)

            def moe1_rest(i, k, half, x2_too=False):
                g, n = 4 * i + k, 2 * i + k // 2
                if below(g, G1 - 1):
                    x_rest(g + 1, (k + 1) % 2)
                for j in range(FC // 2):
                    v.wait_ge(h_ready, 4 * g + j + 1)
                    ve.scalar_tensor_tensor(pair_of(h_l, k % 2, j), bank[1 + j][:], 0.0,
                                            pair_of(h_h, k % 2, j).bitcast(F32), ALU.max, ALU.subtract).then_inc(h_low, 1)
                for q in (2 * (k % 2), 2 * (k % 2) + 1):
                    w_rest(n + 1, q, 1 - k // 2)
                if x2_too:
                    half_rows(2 * i - E - 1 + k // 2, 1 - k // 2)
                if known(g, 1):
                    e = n - (1 - k % 2) - E * half
                    moe1_out(g - 1, (k - 1) % 2, e)
            moe1_rest(0, 0, 0)
            route_positions(1, bank[7][:, 0:2 * HT * E], bank[7][:, 2 * HT * E:4 * HT * E])
            moe1_rest(0, 1, 0)
            route_slots(1)
            moe1_rest(0, 2, 0)
            moe1_rest(0, 3, 0)

            def moe1_sets(i, half):
                for k in range(4):
                    moe1_rest(i, k, half)
            with v.Fori(1, E // 2) as i:
                moe1_sets(i, 0)
            moe1_rest(E // 2, 0, 0)
            for k in range(1, 4):
                moe1_rest(E // 2, k, 1, k == 3)

            def x2_sets(i):
                for k in range(4):
                    moe1_rest(i, k, 1, k % 2 == 1)
            with v.Fori(E // 2 + 1, E - 1) as i:
                chain.enter((i - (E // 2 + 1)) * 2 * X2_LINKS)
                x2_sets(i)
                chain.leave(E // 2 - 2, 2 * X2_LINKS)
            x2_sets(E - 1)
            moe1_out(G1 - 1, 1, E - 1)
            half_rows(HP - 1, 1)

            def x2_batch(b):
                at = slice(b * TPB, (b + 1) * TPB)
                v.wait_ge(c_tanh, b - HB + 1)
                v.wait_ge(x2_in[b], 16)
                link(ve.tensor_tensor(x2[b % 2], x2[b % 2], AR[:, at, 0:D], ALU.add))
                for t in range(TPB):
                    last = ve.bn_stats(rows6[:, b * TPB + t, :], x2[b % 2][:, t, :])
                link(last)
                row_stats(b * TPB, TPB)
                link(ve.tensor_scalar(t_b[:, at], t_a[:, at], EPS, None, ALU.add))
                rsqrt(r1[:, at], t_b[:, at], t_c[:, at])

            def gelu_rest(g, par):
                for j in range(FC // 2):
                    v.wait_ge(h_ready, 4 * g + j + 1)
                    ve.tensor_tensor(pair_of(h_l, par, j), gel[:, j, :], pair_of(h_h, par, j).bitcast(F32),
                                     ALU.subtract).then_inc(h_low, 1)

            def shared_rest(t, par):
                x_rest(G1 + t + 1, 1 - par)
                gelu_rest(G1 + t, par)

            def x2_normed(b, pairs):
                for k in pairs:
                    if b == HB:
                        v.wait_ge(o_out[k % 2], 48 * HP // 2)
                        v.wait_ge(oT_ps, HP)
                    else:
                        v.wait_ge(xn_out[k], 32)
                        v.wait_ge(oT_ps, HP + k + 1)
                    for u in range(2):
                        last = normed(8 * b + 2 * k + u, xn[k][:, u, :], x2[b % 2][:, 2 * k + u, :])
                    last.then_inc(o_norm, 1)

            def shared_out_step(t, par):
                v.wait_ge(y_ps, G1 + t + 1)
                v.wait_ge(y_in[par], 16 * (t // 2 + 1))
                ve.tensor_tensor(y[par][:], bank[5 + par][:].rearrange("p (u d) -> p u d", u=2), y[par][:],
                                 ALU.add).then_inc(y_ready, 1)

            x_rest(G1, 0)
            shared_rest(0, 0)
            x2_batch(HB)
            x2_normed(HB, range(4))
            shared_rest(1, 1)
            shared_out_step(0, 0)
            x2_batch(HB + 1)
            shared_rest(2, 0)
            shared_out_step(1, 1)
            x2_normed(HB + 1, range(4))
            v.wait_ge(og_ready, NP_ + 1)

            hot1, hot2 = OH[:, 0], OH[:, 1]
            softmax_start(every)
            softmax_end(every, 3)
            top(every, NT, g1, hot1)
            shared_rest(3, 1)
            shared_out_step(2, 0)
            link(ve.scalar_tensor_tensor(RA[:], hot1, -2.0, RA[:], ALU.mult, ALU.add))
            top(every, NT, g2, hot2)
            gate_weights(every, 0.0)
            combine_weights(every, hot1, hot2)
            link(ve.tensor_copy(POS[:, 1], hot1))
            ve.tensor_tensor(OH[:, 0], OH[:, 0], OH[:, 1], ALU.add).then_inc(rt_hot, 1)
            both, hot1 = OH[:, 0], POS[:, 1]

            shared_rest(4, 0)
            shared_out_step(3, 1)
            v.wait_ge(rt_pos, 3)
            tot, pos = TO[:, 0], bank[7][:, 0:NT * E].rearrange("p (j e) -> p j e", e=E)
            link(ve.tensor_copy(tot, bank[7][:, NT * E:2 * NT * E].rearrange("p (j e) -> p e j", e=E)))
            link(ve.memset(TO[:, 1], 1.0))
            link(ve.memset(TO[:, 1, :, 0:1], 0.0))
            link(ve.tensor_tensor_scan(SCN[:, 0].rearrange("p e j -> p (e j)"), TO[:, 1].rearrange("p e j -> p (e j)"),
                                       tot.rearrange("p e j -> p (e j)"), 0.0, ALU.mult, ALU.add))
            count, tiles, end, start, off = (e8[:, i, :] for i in range(5))
            link(ve.tensor_copy(count, SCN[:, 0, :, NT - 1]))
            link(ve.tensor_tensor(SCN[:, 0], SCN[:, 0], tot, ALU.subtract))
            link(ve.tensor_tensor(POS[:, 0], pos, SCN[:, 0].rearrange("p e j -> p j e"), ALU.add))
            shared_rest(5, 1)
            shared_out_step(4, 0)
            link(ve.tensor_tensor(cmp, iota_256k[:].unsqueeze(1).broadcast_to([P, E, NT // 2]),
                                  count.unsqueeze(2).broadcast_to([P, E, NT // 2]), ALU.is_lt))
            link(ve.tensor_reduce(tiles, cmp, AX.X, ALU.add))
            link(ve.tensor_tensor_scan(end, ones[:, 0:E], tiles, 0.0, ALU.mult, ALU.add))
            link(ve.tensor_tensor(start, end, tiles, ALU.subtract))
            link(ve.tensor_scalar(off, start, float(R), None, ALU.mult))
            link(ve.tensor_tensor(POS[:, 0], POS[:, 0], te(off, NT), ALU.add))
            pick(every, p1, hot1, POS[:, 0])
            pick(every, p2, hot2, POS[:, 0])
            link(ve.tensor_copy(slot[0][:], col(p1, every)))
            link(ve.tensor_copy(slot[1][:], col(p2, every)))
            shared_rest(6, 0)
            shared_out_step(5, 1)
            it = iota_t[:].unsqueeze(2).broadcast_to([P, G2, E])
            link(ve.tensor_tensor(OHT[:], it, start.unsqueeze(1).broadcast_to([P, G2, E]), ALU.is_ge))
            link(ve.tensor_tensor(oht2, it, end.unsqueeze(1).broadcast_to([P, G2, E]), ALU.is_lt))
            link(ve.tensor_tensor(OHT[:], OHT[:], oht2, ALU.mult))
            link(ve.tensor_tensor(oht2, OHT[:], iota_e[:].unsqueeze(1).broadcast_to([P, G2, E]), ALU.mult))
            link(ve.tensor_reduce(eidf[:], oht2, AX.X, ALU.add))
            ve.tensor_copy(eid[:], eidf[:]).then_inc(rt_done, 1)

            def shared_step(t, par):
                shared_rest(t, par)
                shared_out_step(t - 1, 1 - par)
            run_steps(v, shared_step, 7, 8, GS, GS)
            for q in range(2):
                w_rest(SHARED + 1, q, 1)

            def routed_out(t, par):
                g = M2 + t
                v.wait_ge(meta_in[par], 16 * (G1 // 2 + t // 2 + 1))
                link(ve.tensor_tensor(wsel[:], meta[par][:, :, 0:E], OHT[:, ds(t, 1), :].broadcast_to([P, 2, E]), ALU.mult))
                link(ve.tensor_reduce(wv[:], wsel[:], AX.X, ALU.add))
                v.wait_ge(y_ps, g + 1)
                v.wait_ge(b2_in[par], 16 * (t // 2 + 1))
                link(ve.tensor_tensor(yb[:], bank[5 + par][:].rearrange("p (u d) -> p u d", u=2),
                                      b2b[par][:].unsqueeze(1).broadcast_to([P, 2, D]), ALU.add))
                if known(t, 2):
                    v.wait_ge(added2, 32 * (t - 1))
                else:
                    v.wait_ge(shared_out[par], 16 * GS // 2)
                for u in range(2):
                    last = ve.tensor_scalar(y[par][:, u, :], yb[:, u, :], wv[:, u:u + 1], None, ALU.mult)
                last.then_inc(y_ready, 1)

            def routed_step(t, par):
                g, n = M2 + t, SHARED + 1 + t
                if below(t, G2 - 1):
                    x_rest(g + 1, 1 - par)
                gelu_rest(g, par)
                if below(t, G2 - 1):
                    for q in (0, 1):
                        w_rest(n + 1, q, par)
                for q in (2, 3):
                    w_rest(n, q, 1 - par)
                if known(t, 1):
                    routed_out(t - 1, 1 - par)
                else:
                    shared_out_step(GS - 1, 1)
            run_steps(v, routed_step, 0, 4, G2 - 1 - (G2 - 1) % 2, G2, chain, 2 * 3)
            routed_out(G2 - 1, (G2 - 1) % 2)

        @block.gpsimd
        def _(pool):
            po = nc.gpsimd
            tiles_done = pool.alloc_register("tiles_done")
            po.memset(area[:, 0:2496], 0.0).then_inc(kb_zero, 1)
            po.memset(area[:, 2496:6592], 0.0).then_inc(kb_zero, 1)
            n = [0]

            def const(ins, wait=False):
                ins.then_inc(consts, 1)
                n[0] += 1
                if wait:
                    pool.wait_ge(consts, n[0])

            def iota(dst, pattern, base=0, mult=0, wait=False):
                const(po.iota(dst, pattern, base=base, channel_multiplier=mult, allow_small_or_imprecise_dtypes=True), wait)

            const(po.memset(ident[:], 0.0))
            const(po.memset(upper[:], 1.0))
            const(po.memset(fill[:], 0.0), True)
            const(po.affine_select(out=ident[:], in_=ident[:], compare_op=ALU.not_equal, fill=1.0, base=0,
                                   pattern=[[-1, P]], channel_multiplier=1))
            const(po.affine_select(out=upper[:], in_=upper[:], compare_op=ALU.is_gt, fill=0.0, base=0,
                                   pattern=[[1, P]], channel_multiplier=-1))
            iota(fill[:, :, CID:CID + 1].rearrange("p h o -> p (h o)").bitcast(I32), [[P, 2]], base=T, mult=1)
            const(po.memset(ones[:], 1.0))
            iota(iota_e8[:], [[1, E]], base=-E)
            iota(iota_e[:], [[1, E]])
            iota(first_slot[:], [[CAP, B], [B * CAP, E]])
            iota(iota_256k[:], [[R, NT // 2]])
            iota(iota_t[:], [[1, G2]])
            assert n[0] == NCONST
            po.iota(spare_row[:], [[T, 2], [P, NT]], base=S1, channel_multiplier=1, allow_small_or_imprecise_dtypes=True)
            po.memset(AR[:, :, CID:RW], 0.0).then_inc(kb_zero, 1)
            po.memset(seg1[:], 1.0).then_inc(kb_zero, 1)
            pool.wait_ge(kb_zero, 4)
            po.memset(seg1[:].rearrange("p (s j) -> p s j", j=TPB)[:, :, 0:1], 0.0)
            po.iota(AR[:, :, CID:CID + 1].rearrange("p j o -> p (j o)").bitcast(I32), [[P, NT]], base=0, channel_multiplier=1)

            def att_step(s, par):
                A, M, C = below(s, NP_), known(s, 1) and below(s, NP_ + 1), known(s, 3)

                def heads(op, sc, col):
                    sc = sc[:, 0:SK].rearrange("p (h n) -> p h n", n=NK)
                    return po.tensor_tensor(sc, sc, col[:].unsqueeze(2).broadcast_to([P, H, NK]), op)
                for u in range(2):
                    if M:
                        pool.wait_ge(rec_ready, 2 * s - 1 + u)
                        heads(ALU.mult, score[1 - par][u], srec[u]).then_inc(prob_ready, 1)
                    if A:
                        pool.wait_ge(max_ready, 2 * s + u + 1)
                        heads(ALU.subtract, score[par][u], smax[par][u]).then_inc(sub_ready, 1)
                if C:
                    if known(s, 5):
                        pool.wait_ge(aT_ps, s - 4)
                        pool.wait_ge(a_kept[1 - par], 32 * ((s - 5) // 2 + 1))
                    pool.wait_ge(text_kept[1 - par], 16 * ((s - 3) // 2 + 1))
                    pool.wait_ge(tanh_ready, s - 2)
                    po.tensor_tensor(act_a[1 - par][:], z[1 - par][:], AR[:, ds(2 * s - 6, 2), 0:D], ALU.add).then_inc(a_ready, 1)
            def scatter_rows(dram, first, n, done):
                for j in range(first, first + n):
                    for k in range(2):
                        po.indirect_dma_start(dram, bass.IndirectOffsetOnAxis(ap=slot[k][:, j:j + 1], axis=0),
                                              AR[:, j, :], None).then_inc(done, 16)

            run_steps(pool, att_step, 0, 6, NP_, NP_ + 1)
            for i in range(2):
                pool.wait_ge(a_kept[i], 32 * HT // 4)
            pool.wait_ge(rt_done, 1)
            pool.wait_ge(filled[0], 16 * (2 + 2 * -(-G1 // FILL)))
            scatter_rows(xs1, 0, HT // 4, rows_out[0])
            att_step(NP_ + 1, 1)
            scatter_rows(xs1, HT // 4, HT // 4, rows_out[0])
            att_step(NP_ + 2, 0)
            scatter_rows(xs1, HT // 2, HT // 2, rows_out[0])

            def scatter_add(dram, par, done):
                for u in range(2):
                    po.indirect_dma_start(dram, bass.IndirectOffsetOnAxis(ap=meta[par][:, u, E:E + 1].bitcast(I32), axis=0),
                                          y[par][:, u, :], None, compute_op=ALU.add).then_inc(done, 16)

            def meta_load(dram, t, par):
                po.dma_start(meta[par][:], dram[ds(t * R, R), D:D + E + 1].rearrange("(h p) d -> p h d", p=P))\
                  .then_inc(meta_in[par], 16)

            def tile_step(n, dram, slots, sums, first, done):
                def step(t, par):
                    if known(t, 2):
                        pool.wait_ge(done, 32 * (t - 1))
                    if below(t, n):
                        meta_load(dram, slots(t, par), par)
                    if known(t, 1):
                        pool.reg_mov(tiles_done, first + t)
                        pool.wait_ge(rt_done, 1)
                        pool.wait_ge(y_ready, tiles_done)
                        scatter_add(sums, 1 - par, done)
                return step

            pool.wait_ge(rows_out[0], 16 * 2 * HT)
            for i in range(2):
                pool.wait_ge(a_kept[i], 32 * NP_ // 2)
            step = tile_step(G1, xs1, lambda t, par: slots_of(t, par, 0), acc1, 0, added1)
            step(0, 0)
            step(1, 1)
            pool.wait_ge(rt_done, 2)
            for t in range(2, 10):
                scatter_rows(xs1, HT + 2 * (t - 2), 2, rows_out[1])
                step(t, t % 2)
            run_steps(pool, step, 10, 10, G1 // 2, G1 // 2)
            pool.wait_ge(rows_out[1], 16 * 2 * HT)
            step = tile_step(G1, xs1, lambda t, par: slots_of(t, par, 1), acc1, 0, added1)

            def half_keep(p, par):
                pool.wait_ge(o_norm, p + 1)
                po.tensor_tensor(xh[par][:], xh[par][:], sb2[:].unsqueeze(1).broadcast_to([P, 2, D]), ALU.add).then_inc(o_bias, 1)
                po.dma_start(rows(xn2, p), xhn[par][:]).then_inc(o_out[par], 16)
                po.dma_start(AR[:, ds(2 * p, 2), 0:D], xhn[par][:]).then_inc(o_out[par], 16)
                pool.reg_mov(tiles_done, p + 1)
                pool.wait_ge(rt_done, 1)
                pool.wait_ge(o_bias, tiles_done)
                po.dma_start(rows(x2b, p), xh[par][:]).then_inc(o_out[par], 16)

            run_steps(pool, step, HG, HG, HG + 4, HG + 4)
            half_keep(0, 0)
            with pool.Fori(HG // 4 + 1, G1 // 4) as i:
                for k in range(4):
                    step(4 * i + k, k % 2)
                    if k % 2:
                        half_keep(2 * i - HP - 1 + k // 2, 1 - k // 2)
            step(G1, 0)
            pool.wait_ge(added1, 32 * G1)
            half_keep(HP - 1, 1)

            for b in range(HB, B):
                for k in range(4):
                    p = HP + 4 * (b - HB) + k
                    pool.wait_ge(o_norm, p + 1)
                    xp = x2[b % 2][:, 2 * k:2 * k + 2, :]
                    po.tensor_tensor(xp, xp, sb2[:].unsqueeze(1).broadcast_to([P, 2, D]), ALU.add).then_inc(o_bias, 1)
                    po.dma_start(rows(xn2, p), xn[k][:]).then_inc(xn_out[k], 16)
                    po.dma_start(AR[:, 2 * p:2 * p + 2, 0:D], xn[k][:]).then_inc(xn_out[k], 16)
                pool.wait_ge(o_bias, HP + 4 * (b - HB) + 4)
                po.dma_start(x2b[b * N:(b + 1) * N, :].rearrange("(t p) d -> p t d", p=P), x2[b % 2]).then_inc(x2_kept[b], 16)
            for i in range(2):
                pool.wait_ge(o_out[i], 48 * HP // 2)
            for k in range(4):
                pool.wait_ge(xn_out[k], 32 * HB)
            pool.wait_ge(rt_done, 3)
            pool.wait_ge(filled[1], 16 * 2 * -(-G2 // FILL))
            scatter_rows(xs2, 0, NT, rows_out2)
            pool.wait_ge(rows_out2, 16 * 2 * NT)
            for i in range(2):
                pool.wait_ge(shared_out[i], 16 * GS // 2)
            run_steps(pool, tile_step(G2, xs2, lambda t, par: t, out, M2, added2), 0, 2, G2 - G2 % 2, G2 + 1)


def kernel(x, ctx_1024, fside_BxS_0, mask_BxS2_bk0, L0_xattn_ln_gamma, L0_xattn_null_kv, L0_xattn_Wq, L0_xattn_Wkv,
           L0_xattn_Wo, L0_xattn_out_gamma, L0_xattn_w_gate, L0_xattn_w1, L0_xattn_w2, L0_ffn_gate_w, L0_ffn_W1,
           L0_ffn_b1, L0_ffn_W2, L0_ffn_b2, L0_ffn_sW1, L0_ffn_sb1, L0_ffn_sW2, L0_ffn_sb2):
    import numpy as np
    import concourse.bacc as bacc
    from concourse.bass_utils import run_bass_kernel_spmd

    def a(v):
        return np.asarray(v)

    def w1_rows(w):
        return a(w).reshape(-1, KC, P, F).transpose(0, 2, 1, 3).reshape(-1, P, KC * F)

    def w2_rows(w):
        return a(w).reshape(-1, FC, P, D).transpose(0, 2, 1, 3).reshape(-1, P, FC * D)

    data = {
        "x": a(x).reshape(T, D),
        "ctxT": a(ctx_1024).reshape(B * NCTX, D).T,
        "probs": a(fside_BxS_0).reshape(NT, P).T,
        "mask": a(mask_BxS2_bk0).reshape(B * NCTX),
        "ln_g": a(L0_xattn_ln_gamma).reshape(KC, P).T,
        "null": a(L0_xattn_null_kv).T,
        "WqT": a(L0_xattn_Wq).T,
        "Wkv": a(L0_xattn_Wkv),
        "Wo": a(L0_xattn_Wo),
        "out_g": a(L0_xattn_out_gamma),
        "wg1": a(L0_xattn_w_gate),
        "wg2": a(L0_ffn_gate_w).T,
        "W1a": w1_rows(L0_xattn_w1), "W2a": w2_rows(L0_xattn_w2),
        "W1b": w1_rows(L0_ffn_W1), "W2b": w2_rows(L0_ffn_W2),
        "sW1": w1_rows(L0_ffn_sW1), "sW2": w2_rows(L0_ffn_sW2),
        "b1": a(L0_ffn_b1).reshape(E, FC, P).transpose(0, 2, 1),
        "b2": a(L0_ffn_b2),
        "sb1": a(L0_ffn_sb1).reshape(FC, P).T,
        "sb2": a(L0_ffn_sb2),
    }
    nc = bacc.Bacc("TRN2", target_bir_lowering=False, num_devices=1)
    arrays, io = {}, {}
    for name, v in data.items():
        v = np.ascontiguousarray(v)
        arrays[f"in_{name}"] = v
        io[name] = nc.dram_tensor(f"in_{name}", v.shape, mybir.dt.from_np(v.dtype), kind="ExternalInput").ap()
    io["out"] = nc.dram_tensor("out_rows", (T + SPARE, D), F32, kind="ExternalOutput").ap()
    build(nc, io)
    r = run_bass_kernel_spmd(nc, [arrays], core_ids=[0])
    return r.results[0]["out_rows"][:T].reshape(B, N, D)
```
